# Optimizing a Trainium2 kernel written in Bass

```python
import numpy as np
import jax
import jax.numpy as jnp

def _softmax(x, axis=-1):
    return jax.nn.softmax(x, axis=axis)

def _gelu(x):
    return jax.nn.gelu(x, approximate=True)

def _silu(x):
    return jax.nn.silu(x)

def _sigmoid(x):
    return jax.nn.sigmoid(x)

def _layernorm(x, axis=-1, eps=1e-05):
    m = jnp.mean(x, axis=axis, keepdims=True)
    v = jnp.var(x, axis=axis, keepdims=True)
    return (x - m) / jnp.sqrt(v + eps)

def _scatter_add(tgt, idx, src, axis=0):
    return tgt.at[idx].add(src)

def _segment_sum(src, seg, n):
    return jax.ops.segment_sum(src, seg, n)
kernel_name = 'mk_flamingo_gated_d4_seqx_r8_60f9cd'

def setup_inputs(seed: int=0):
    np.random.seed(seed)
    _w = jnp.asarray

    def _rec_inputs():
        import jax
        import jax.numpy as jnp
        _rk = jax.random.key(seed)
        x = 7.22e-05 + 1 * jax.random.normal(jax.random.fold_in(_rk, 1), (16, 128, 256), jnp.float32)
        _lenS = 128 - jax.random.randint(jax.random.fold_in(_rk, 7), (16,), 0, max(1, 128 // 4) + 1, jnp.int32)
        _lenS2 = 128 - jax.random.randint(jax.random.fold_in(_rk, 8), (16,), 0, max(1, 128 // 4) + 1, jnp.int32)
        _ctx_1024P = jax.random.normal(jax.random.fold_in(_rk, 11), (16, 16, 128), jnp.float32)
        _ctx_1024c = jax.random.dirichlet(jax.random.fold_in(_rk, 511), 0.3 * jnp.ones((16,), jnp.float32), (16, 128))
        _ctx_1024t = jnp.einsum('bsk,bkd->bsd', _ctx_1024c, _ctx_1024P)
        _ctx_1024t = _ctx_1024t * jax.lax.rsqrt(jnp.mean(jnp.square(_ctx_1024t)) + 1e-12) * 0.953939
        ctx_1024 = -1.39393e-06 + 0.999914 * (_ctx_1024t + 0.3 * jax.random.normal(jax.random.fold_in(_rk, 611), (16, 128, 128), jnp.float32))
        fside_BxSx2_0 = jax.random.uniform(jax.random.fold_in(_rk, 12), (16, 128, 2), jnp.float32, 0.0, 0.999707)
        _validS = jnp.arange(128)[None, :] < _lenS[:, None]
        _validS2 = jnp.arange(128)[None, :] < _lenS2[:, None]
        _causal = jnp.tril(jnp.ones((128, 128), dtype=bool))
        mask_BxS2_bf1 = jnp.ones((16, 128), dtype=bool)
        _g = jax.random.normal(jax.random.fold_in(_rk, 9001), (2, 4), jnp.float32)
        _g = jnp.sign(_g) * jnp.maximum(jnp.abs(_g), 1.0) + (_g == 0) * 1.0
        g_xattn = _g[0]
        g_ffn = _g[1]
        return (x, ctx_1024, fside_BxSx2_0, mask_BxS2_bf1, g_xattn, g_ffn)
    x, ctx_1024, fside_BxSx2_0, mask_BxS2_bf1, g_xattn, g_ffn = _rec_inputs()

    def _L0_xattn_setup():
        import jax, jax.numpy as jnp
        import numpy as np
        DIM = 256
        CTX_DIM = 128
        N_HEADS = 32
        HEAD_DIM = DIM // N_HEADS
        POS_DIM = 2
        B, N, CTXN = (2, 256, 256)
        ROPE_BASE = 10000.0

        def apply_axial_rope(x, pos):
            b, n, h, d = x.shape
            p = pos.shape[-1]
            dpa = d // p
            half = dpa // 2
            freqs = ROPE_BASE ** (-jnp.arange(half, dtype=x.dtype) / half)
            ang = pos[..., :, None] * freqs
            cos = jnp.cos(ang)[:, :, None, :, :]
            sin = jnp.sin(ang)[:, :, None, :, :]
            xr = x.reshape(b, n, h, p, half, 2)
            x1, x2 = (xr[..., 0], xr[..., 1])
            out = jnp.stack([x1 * cos - x2 * sin, x1 * sin + x2 * cos], axis=-1)
            return out.reshape(b, n, h, d)
        key = jax.random.key(seed)
        ks = jax.random.split(key, 8)
        x = jax.random.normal(ks[0], (B, N, DIM), jnp.float32)
        ctx = jax.random.normal(ks[1], (B, CTXN, CTX_DIM), jnp.float32)
        pos_map = jax.random.uniform(ks[2], (B, N, POS_DIM), jnp.float32)
        ctx_pos_map = jax.random.uniform(ks[3], (B, CTXN, POS_DIM), jnp.float32)
        Wq = jax.random.normal(ks[4], (DIM, DIM), jnp.float32) / np.sqrt(DIM)
        Wkv = jax.random.normal(ks[5], (CTX_DIM, 2 * DIM), jnp.float32) / np.sqrt(CTX_DIM)
        Wout = jax.random.normal(ks[6], (DIM, DIM), jnp.float32) / np.sqrt(DIM)
        bout = jnp.zeros((DIM,), jnp.float32)
        return {'x': x, 'ctx': ctx, 'pos_map': pos_map, 'ctx_pos_map': ctx_pos_map, 'Wq': Wq, 'Wkv': Wkv, 'Wout': Wout, 'bout': bout}
    _L0_xattn_all = _L0_xattn_setup()
    _L0_xattn_in = {k: v for k, v in _L0_xattn_all.items() if k in ('Wq', 'Wkv', 'Wout', 'bout')}
    del _L0_xattn_all

    def _L0_ffn_setup():
        import jax, jax.numpy as jnp
        import numpy as np
        EPS = 1e-05

        def act_quant(x):
            scale = 127.0 / jnp.clip(jnp.max(jnp.abs(x), axis=-1, keepdims=True), EPS)
            return jnp.clip(jnp.round(x * scale), -128.0, 127.0) / scale

        def weight_quant(w):
            scale = 1.0 / jnp.clip(jnp.mean(jnp.abs(w)), EPS)
            return jnp.clip(jnp.round(w * scale), -1.0, 1.0) / scale

        def bitlinear(x, w):
            return jnp.einsum('bsd,hd->bsh', act_quant(x), weight_quant(w))
        key = jax.random.key(seed)
        k0, k1, k2, k3 = jax.random.split(key, 4)
        d_model, hidden_dim = (256, 704)
        B, S = (4, 256)
        x = jax.random.normal(k0, (B, S, d_model), dtype=jnp.float32)
        std = 0.02
        w1 = jax.random.normal(k1, (hidden_dim, d_model), dtype=jnp.float32) * std
        w2 = jax.random.normal(k2, (d_model, hidden_dim), dtype=jnp.float32) * std
        w3 = jax.random.normal(k3, (hidden_dim, d_model), dtype=jnp.float32) * std
        return {'x': x, 'w1': w1, 'w2': w2, 'w3': w3}
    _L0_ffn_all = _L0_ffn_setup()
    _L0_ffn_in = {k: v for k, v in _L0_ffn_all.items() if k in ('w1', 'w2', 'w3')}
    del _L0_ffn_all

    def _L1_xattn_setup():
        import jax, jax.numpy as jnp
        import numpy as np
        N_HEADS = 16
        N_KV_HEADS = 8
        HEAD_DIM = 128
        D_TEXT = 256
        D_VISION = 128
        GROUPS = N_HEADS // N_KV_HEADS
        key = jax.random.key(seed)
        ks = jax.random.split(key, 6)
        B, T_text, T_vis = (4, 256, 72)
        text_hidden = jax.random.normal(ks[0], (B, T_text, D_TEXT), dtype=jnp.float32)
        vision_tokens = jax.random.normal(ks[1], (B, T_vis, D_VISION), dtype=jnp.float32)
        vision_mask = jnp.ones((B, T_vis), dtype=bool)
        s = 0.02
        Wq = jax.random.normal(ks[2], (D_TEXT, N_HEADS * HEAD_DIM), dtype=jnp.float32) * s
        Wk = jax.random.normal(ks[3], (D_VISION, N_KV_HEADS * HEAD_DIM), dtype=jnp.float32) * s
        Wv = jax.random.normal(ks[4], (D_VISION, N_KV_HEADS * HEAD_DIM), dtype=jnp.float32) * s
        Wo = jax.random.normal(ks[5], (N_HEADS * HEAD_DIM, D_TEXT), dtype=jnp.float32) * s
        return {'text_hidden': text_hidden, 'vision_tokens': vision_tokens, 'vision_mask': vision_mask, 'Wq': Wq, 'Wk': Wk, 'Wv': Wv, 'Wo': Wo}
    _L1_xattn_all = _L1_xattn_setup()
    _L1_xattn_in = {k: v for k, v in _L1_xattn_all.items() if k in ('Wq', 'Wk', 'Wv', 'Wo')}
    del _L1_xattn_all

    def _L1_ffn_setup():
        import jax, jax.numpy as jnp
        import numpy as np
        B_, S, D = (2, 256, 256)
        F_ = 1024
        R = 16
        H = 16
        HD = D // H
        MOD_SCALE = 0.1
        EPS = 1e-06

        def _rmsnorm(x, w):
            v = jnp.mean(x * x, axis=-1, keepdims=True)
            return x * jax.lax.rsqrt(v + EPS) * w

        def _attention(x, Wq, Wk, Wv, Wo):
            b, s, d = x.shape
            q = (x @ Wq.T).reshape(b, s, H, HD)
            k = (x @ Wk.T).reshape(b, s, H, HD)
            v = (x @ Wv.T).reshape(b, s, H, HD)
            scores = jnp.einsum('bqhd,bkhd->bhqk', q, k) / np.sqrt(HD).astype(np.float32)
            causal = jnp.tril(jnp.ones((s, s), bool))
            scores = jnp.where(causal, scores, jnp.finfo(scores.dtype).min)
            probs = jax.nn.softmax(scores, axis=-1)
            out = jnp.einsum('bhqk,bkhd->bqhd', probs, v).reshape(b, s, d)
            return out @ Wo.T
        key = jax.random.key(seed)
        ks = jax.random.split(key, 12)
        sd = 0.02
        return {'hidden_states': jax.random.normal(ks[0], (B_, S, D), jnp.float32), 'ln1_w': jnp.ones((D,), jnp.float32), 'ln2_w': jnp.ones((D,), jnp.float32), 'Wq': jax.random.normal(ks[1], (D, D), jnp.float32) * sd, 'Wk': jax.random.normal(ks[2], (D, D), jnp.float32) * sd, 'Wv': jax.random.normal(ks[3], (D, D), jnp.float32) * sd, 'Wo': jax.random.normal(ks[4], (D, D), jnp.float32) * sd, 'A': jax.random.normal(ks[5], (D, R), jnp.float32) * (0.01 / np.sqrt(D)), 'B': jax.random.normal(ks[6], (R, F_), jnp.float32) * (0.01 / np.sqrt(R)), 'W_in_base': jax.random.normal(ks[7], (F_, D), jnp.float32) * sd, 'W_up_base': jax.random.normal(ks[8], (F_, D), jnp.float32) * sd, 'W_down': jax.random.normal(ks[9], (D, F_), jnp.float32) * sd}
    _L1_ffn_all = _L1_ffn_setup()
    _L1_ffn_in = {k: v for k, v in _L1_ffn_all.items() if k in ('ln1_w', 'ln2_w', 'Wq', 'Wk', 'Wv', 'Wo', 'A', 'B', 'W_in_base', 'W_up_base', 'W_down')}
    del _L1_ffn_all

    def _L2_xattn_setup():
        import jax, jax.numpy as jnp
        import numpy as np
        EPS = 1e-05

        def rmsnorm(x, g, eps=EPS):
            var = jnp.mean(jnp.square(x), axis=-1, keepdims=True)
            return x * jax.lax.rsqrt(var + eps) * g
        key = jax.random.key(seed)
        ks = jax.random.split(key, 8)
        B, Sq, Skv = (2, 512, 64)
        dim, cdim, H, D = (256, 128, 16, 128)
        inner = H * D
        s = lambda f: 1.0 / np.sqrt(f)
        return {'hidden_states': jax.random.normal(ks[0], (B, Sq, dim), jnp.float32), 'encoder_hidden_states': jax.random.normal(ks[1], (B, Skv, cdim), jnp.float32), 'Wq': jax.random.normal(ks[2], (dim, inner), jnp.float32) * s(dim), 'Wk': jax.random.normal(ks[3], (cdim, inner), jnp.float32) * s(cdim), 'Wv': jax.random.normal(ks[4], (cdim, inner), jnp.float32) * s(cdim), 'Wo': jax.random.normal(ks[5], (inner, dim), jnp.float32) * s(inner), 'gq': jnp.ones((D,), jnp.float32), 'gk': jnp.ones((D,), jnp.float32)}
    _L2_xattn_all = _L2_xattn_setup()
    _L2_xattn_in = {k: v for k, v in _L2_xattn_all.items() if k in ('Wq', 'Wk', 'Wv', 'Wo', 'gq', 'gk')}
    del _L2_xattn_all

    def _L2_ffn_setup():
        import jax, jax.numpy as jnp
        import numpy as np
        DIM_IN = 256
        DIM_HIDDEN = 1024
        key = jax.random.key(seed)
        k_x, k_g, k_u, k_d = jax.random.split(key, 4)
        s_in = 1.0 / np.sqrt(DIM_IN)
        s_hid = 1.0 / np.sqrt(DIM_HIDDEN)
        x = jax.random.normal(k_x, (4, 256, DIM_IN), dtype=jnp.float32)
        w_gate = jax.random.uniform(k_g, (DIM_HIDDEN, DIM_IN), jnp.float32, -s_in, s_in)
        w_up = jax.random.uniform(k_u, (DIM_HIDDEN, DIM_IN), jnp.float32, -s_in, s_in)
        w_down = jax.random.uniform(k_d, (DIM_IN, DIM_HIDDEN), jnp.float32, -s_hid, s_hid)
        return {'x': x, 'w_gate': w_gate, 'w_up': w_up, 'w_down': w_down}
    _L2_ffn_all = _L2_ffn_setup()
    _L2_ffn_in = {k: v for k, v in _L2_ffn_all.items() if k in ('w_gate', 'w_up', 'w_down')}
    del _L2_ffn_all

    def _L3_xattn_setup():
        import jax, jax.numpy as jnp
        import numpy as np
        B, S1, S2, DCA = (2, 256, 128, 16)
        QDIM, KDIM, H = (256, 128, 16)
        HD = QDIM // H
        SCALE = HD ** (-0.5)
        EPS = 1e-06
        DCA_WEIGHT = 1.0

        def _ln(t, w, b):
            m = jnp.mean(t, axis=-1, keepdims=True)
            v = jnp.var(t, axis=-1, keepdims=True)
            return (t - m) * jax.lax.rsqrt(v + EPS) * w + b

        def _attn(q, k, v):
            s = jnp.einsum('bhqd,bhkd->bhqk', q, k) * SCALE
            p = jax.nn.softmax(s, axis=-1)
            return jnp.einsum('bhqk,bhkd->bhqd', p, v)
        key = jax.random.key(seed)
        ks = jax.random.split(key, 8)
        w = lambda k, shape: jax.random.normal(k, shape, jnp.float32) * 0.02
        return {'x': jax.random.normal(ks[0], (B, S1, QDIM), jnp.float32), 'y': jax.random.normal(ks[1], (B, S2 + DCA, KDIM), jnp.float32), 'Wq': w(ks[2], (QDIM, QDIM)), 'bq': jnp.zeros((QDIM,), jnp.float32), 'Wk': w(ks[3], (KDIM, QDIM)), 'bk': jnp.zeros((QDIM,), jnp.float32), 'Wv': w(ks[4], (KDIM, QDIM)), 'bv': jnp.zeros((QDIM,), jnp.float32), 'Wkv_dca': w(ks[5], (KDIM, 2 * QDIM)), 'bkv_dca': jnp.zeros((2 * QDIM,), jnp.float32), 'qn_w': jnp.ones((HD,), jnp.float32), 'qn_b': jnp.zeros((HD,), jnp.float32), 'kn_w': jnp.ones((HD,), jnp.float32), 'kn_b': jnp.zeros((HD,), jnp.float32), 'kn_dca_w': jnp.ones((HD,), jnp.float32), 'kn_dca_b': jnp.zeros((HD,), jnp.float32), 'Wo': w(ks[6], (QDIM, QDIM)), 'bo': jnp.zeros((QDIM,), jnp.float32)}
    _L3_xattn_all = _L3_xattn_setup()
    _L3_xattn_in = {k: v for k, v in _L3_xattn_all.items() if k in ('Wq', 'bq', 'Wk', 'bk', 'Wv', 'bv', 'Wkv_dca', 'bkv_dca', 'qn_w', 'qn_b', 'kn_w', 'kn_b', 'kn_dca_w', 'kn_dca_b', 'Wo', 'bo')}
    del _L3_xattn_all

    def _L3_ffn_setup():
        import jax, jax.numpy as jnp
        import numpy as np
        B, S, H = (4, 256, 256)
        INTER = 512
        E = 8
        TOPK = 2
        SHARED_I = INTER * 2

        def moe_forward(hidden_states, router_w, w1, w2, w_gate, w_up, w_down):
            b, s, h = hidden_states.shape
            x = hidden_states.reshape(-1, h)
            T = x.shape[0]
            logits = x @ router_w
            top_logits, top_indices = jax.lax.top_k(logits, TOPK)
            scores = jax.nn.softmax(top_logits, axis=-1)
            flat_idx = top_indices.reshape(-1)
            sorted_pos = jnp.argsort(flat_idx, stable=True)
            permuted = x[sorted_pos // TOPK]
            expert_ids = flat_idx[sorted_pos]
            out = jnp.zeros((T * TOPK, h), x.dtype)
            for e in range(E):
                mask = (expert_ids == e)[:, None]
                f1 = permuted * mask @ w1[e]
                g, u = jnp.split(f1, 2, axis=-1)
                act = jax.nn.silu(g) * u
                out = out + jnp.where(mask, act @ w2[e], 0.0)
            unperm = jnp.zeros_like(out).at[sorted_pos].set(out)
            combined = (unperm.reshape(T, TOPK, h) * scores[..., None]).sum(axis=1)
            shared = jax.nn.silu(x @ w_gate) * (x @ w_up) @ w_down
            return (combined + shared).reshape(b, s, h)
        key = jax.random.key(seed)
        ks = jax.random.split(key, 7)
        s = 0.02
        return {'hidden_states': jax.random.normal(ks[0], (B, S, H), jnp.float32), 'router_w': jax.random.normal(ks[1], (H, E), jnp.float32) * s, 'w1': jax.random.normal(ks[2], (E, H, 2 * INTER), jnp.float32) * s, 'w2': jax.random.normal(ks[3], (E, INTER, H), jnp.float32) * s, 'w_gate': jax.random.normal(ks[4], (H, SHARED_I), jnp.float32) * s, 'w_up': jax.random.normal(ks[5], (H, SHARED_I), jnp.float32) * s, 'w_down': jax.random.normal(ks[6], (SHARED_I, H), jnp.float32) * s}
    _L3_ffn_all = _L3_ffn_setup()
    _L3_ffn_in = {k: v for k, v in _L3_ffn_all.items() if k in ('router_w', 'w1', 'w2', 'w_gate', 'w_up', 'w_down')}
    del _L3_ffn_all
    return {'x': x, 'ctx_1024': ctx_1024, 'fside_BxSx2_0': fside_BxSx2_0, 'mask_BxS2_bf1': mask_BxS2_bf1, 'g_xattn': g_xattn, 'g_ffn': g_ffn, 'L0_xattn_Wq': _L0_xattn_in['Wq'], 'L0_xattn_Wkv': _L0_xattn_in['Wkv'], 'L0_xattn_Wout': _L0_xattn_in['Wout'], 'L0_xattn_bout': _L0_xattn_in['bout'], 'L0_ffn_w1': _L0_ffn_in['w1'], 'L0_ffn_w2': _L0_ffn_in['w2'], 'L0_ffn_w3': _L0_ffn_in['w3'], 'L1_xattn_Wq': _L1_xattn_in['Wq'], 'L1_xattn_Wk': _L1_xattn_in['Wk'], 'L1_xattn_Wv': _L1_xattn_in['Wv'], 'L1_xattn_Wo': _L1_xattn_in['Wo'], 'L1_ffn_ln1_w': _L1_ffn_in['ln1_w'], 'L1_ffn_ln2_w': _L1_ffn_in['ln2_w'], 'L1_ffn_Wq': _L1_ffn_in['Wq'], 'L1_ffn_Wk': _L1_ffn_in['Wk'], 'L1_ffn_Wv': _L1_ffn_in['Wv'], 'L1_ffn_Wo': _L1_ffn_in['Wo'], 'L1_ffn_A': _L1_ffn_in['A'], 'L1_ffn_B': _L1_ffn_in['B'], 'L1_ffn_W_in_base': _L1_ffn_in['W_in_base'], 'L1_ffn_W_up_base': _L1_ffn_in['W_up_base'], 'L1_ffn_W_down': _L1_ffn_in['W_down'], 'L2_xattn_Wq': _L2_xattn_in['Wq'], 'L2_xattn_Wk': _L2_xattn_in['Wk'], 'L2_xattn_Wv': _L2_xattn_in['Wv'], 'L2_xattn_Wo': _L2_xattn_in['Wo'], 'L2_xattn_gq': _L2_xattn_in['gq'], 'L2_xattn_gk': _L2_xattn_in['gk'], 'L2_ffn_w_gate': _L2_ffn_in['w_gate'], 'L2_ffn_w_up': _L2_ffn_in['w_up'], 'L2_ffn_w_down': _L2_ffn_in['w_down'], 'L3_xattn_Wq': _L3_xattn_in['Wq'], 'L3_xattn_bq': _L3_xattn_in['bq'], 'L3_xattn_Wk': _L3_xattn_in['Wk'], 'L3_xattn_bk': _L3_xattn_in['bk'], 'L3_xattn_Wv': _L3_xattn_in['Wv'], 'L3_xattn_bv': _L3_xattn_in['bv'], 'L3_xattn_Wkv_dca': _L3_xattn_in['Wkv_dca'], 'L3_xattn_bkv_dca': _L3_xattn_in['bkv_dca'], 'L3_xattn_qn_w': _L3_xattn_in['qn_w'], 'L3_xattn_qn_b': _L3_xattn_in['qn_b'], 'L3_xattn_kn_w': _L3_xattn_in['kn_w'], 'L3_xattn_kn_b': _L3_xattn_in['kn_b'], 'L3_xattn_kn_dca_w': _L3_xattn_in['kn_dca_w'], 'L3_xattn_kn_dca_b': _L3_xattn_in['kn_dca_b'], 'L3_xattn_Wo': _L3_xattn_in['Wo'], 'L3_xattn_bo': _L3_xattn_in['bo'], 'L3_ffn_router_w': _L3_ffn_in['router_w'], 'L3_ffn_w1': _L3_ffn_in['w1'], 'L3_ffn_w2': _L3_ffn_in['w2'], 'L3_ffn_w_gate': _L3_ffn_in['w_gate'], 'L3_ffn_w_up': _L3_ffn_in['w_up'], 'L3_ffn_w_down': _L3_ffn_in['w_down']}

def reference(x, ctx_1024, fside_BxSx2_0, mask_BxS2_bf1, g_xattn, g_ffn, L0_xattn_Wq, L0_xattn_Wkv, L0_xattn_Wout, L0_xattn_bout, L0_ffn_w1, L0_ffn_w2, L0_ffn_w3, L1_xattn_Wq, L1_xattn_Wk, L1_xattn_Wv, L1_xattn_Wo, L1_ffn_ln1_w, L1_ffn_ln2_w, L1_ffn_Wq, L1_ffn_Wk, L1_ffn_Wv, L1_ffn_Wo, L1_ffn_A, L1_ffn_B, L1_ffn_W_in_base, L1_ffn_W_up_base, L1_ffn_W_down, L2_xattn_Wq, L2_xattn_Wk, L2_xattn_Wv, L2_xattn_Wo, L2_xattn_gq, L2_xattn_gk, L2_ffn_w_gate, L2_ffn_w_up, L2_ffn_w_down, L3_xattn_Wq, L3_xattn_bq, L3_xattn_Wk, L3_xattn_bk, L3_xattn_Wv, L3_xattn_bv, L3_xattn_Wkv_dca, L3_xattn_bkv_dca, L3_xattn_qn_w, L3_xattn_qn_b, L3_xattn_kn_w, L3_xattn_kn_b, L3_xattn_kn_dca_w, L3_xattn_kn_dca_b, L3_xattn_Wo, L3_xattn_bo, L3_ffn_router_w, L3_ffn_w1, L3_ffn_w2, L3_ffn_w_gate, L3_ffn_w_up, L3_ffn_w_down):
    import jax
    import jax.numpy as jnp

    def _L0_xattn_ref(x, ctx, pos_map, ctx_pos_map, Wq, Wkv, Wout, bout):
        import jax, jax.numpy as jnp
        import numpy as np
        DIM = 256
        CTX_DIM = 128
        N_HEADS = 32
        HEAD_DIM = DIM // N_HEADS
        POS_DIM = 2
        B, N, CTXN = (2, 256, 256)
        ROPE_BASE = 10000.0

        def apply_axial_rope(x, pos):
            b, n, h, d = x.shape
            p = pos.shape[-1]
            dpa = d // p
            half = dpa // 2
            freqs = ROPE_BASE ** (-jnp.arange(half, dtype=x.dtype) / half)
            ang = pos[..., :, None] * freqs
            cos = jnp.cos(ang)[:, :, None, :, :]
            sin = jnp.sin(ang)[:, :, None, :, :]
            xr = x.reshape(b, n, h, p, half, 2)
            x1, x2 = (xr[..., 0], xr[..., 1])
            out = jnp.stack([x1 * cos - x2 * sin, x1 * sin + x2 * cos], axis=-1)
            return out.reshape(b, n, h, d)
        b, n, _ = x.shape
        ctx_n = ctx.shape[1]
        q = (x @ Wq).reshape(b, n, N_HEADS, HEAD_DIM)
        k, v = jnp.split(ctx @ Wkv, 2, axis=-1)
        k = k.reshape(b, ctx_n, N_HEADS, HEAD_DIM)
        v = v.reshape(b, ctx_n, N_HEADS, HEAD_DIM)
        q = apply_axial_rope(q, pos_map)
        k = apply_axial_rope(k, ctx_pos_map)
        scale = 1.0 / np.sqrt(HEAD_DIM).astype(np.float32)
        logits = jnp.einsum('bqhd,bkhd->bhqk', q, k) * scale
        w = jax.nn.softmax(logits, axis=-1)
        attn = jnp.einsum('bhqk,bkhd->bqhd', w, v)
        attn = attn.reshape(b, n, N_HEADS * HEAD_DIM)
        return attn @ Wout + bout

    def _L0_ffn_ref(x, w1, w2, w3):
        import jax, jax.numpy as jnp
        import numpy as np
        EPS = 1e-05

        def act_quant(x):
            scale = 127.0 / jnp.clip(jnp.max(jnp.abs(x), axis=-1, keepdims=True), EPS)
            return jnp.clip(jnp.round(x * scale), -128.0, 127.0) / scale

        def weight_quant(w):
            scale = 1.0 / jnp.clip(jnp.mean(jnp.abs(w)), EPS)
            return jnp.clip(jnp.round(w * scale), -1.0, 1.0) / scale

        def bitlinear(x, w):
            return jnp.einsum('bsd,hd->bsh', act_quant(x), weight_quant(w))
        h = jax.nn.silu(bitlinear(x, w1)) * bitlinear(x, w3)
        return bitlinear(h, w2)

    def _L1_xattn_ref(text_hidden, vision_tokens, vision_mask, Wq, Wk, Wv, Wo):
        import jax, jax.numpy as jnp
        import numpy as np
        N_HEADS = 16
        N_KV_HEADS = 8
        HEAD_DIM = 128
        D_TEXT = 256
        D_VISION = 128
        GROUPS = N_HEADS // N_KV_HEADS
        B, T_text, _ = text_hidden.shape
        T_vis = vision_tokens.shape[1]
        scale = jnp.float32(np.sqrt(HEAD_DIM))
        q = (text_hidden @ Wq).reshape(B, T_text, N_HEADS, HEAD_DIM).transpose(0, 2, 1, 3)
        k = (vision_tokens @ Wk).reshape(B, T_vis, N_KV_HEADS, HEAD_DIM).transpose(0, 2, 1, 3)
        v = (vision_tokens @ Wv).reshape(B, T_vis, N_KV_HEADS, HEAD_DIM).transpose(0, 2, 1, 3)
        k = jnp.repeat(k, GROUPS, axis=1)
        v = jnp.repeat(v, GROUPS, axis=1)
        scores = jnp.einsum('bhtd,bhsd->bhts', q, k) / scale
        mask = vision_mask[:, None, None, :]
        scores = jnp.where(mask, scores, -jnp.inf)
        attn = jax.nn.softmax(scores, axis=-1)
        attn = jnp.nan_to_num(attn, nan=0.0)
        out = jnp.einsum('bhts,bhsd->bhtd', attn, v)
        out = out.transpose(0, 2, 1, 3).reshape(B, T_text, N_HEADS * HEAD_DIM)
        return out @ Wo

    def _L1_ffn_ref(hidden_states, ln1_w, ln2_w, Wq, Wk, Wv, Wo, A, B, W_in_base, W_up_base, W_down):
        import jax, jax.numpy as jnp
        import numpy as np
        B_, S, D = (2, 256, 256)
        F_ = 1024
        R = 16
        H = 16
        HD = D // H
        MOD_SCALE = 0.1
        EPS = 1e-06

        def _rmsnorm(x, w):
            v = jnp.mean(x * x, axis=-1, keepdims=True)
            return x * jax.lax.rsqrt(v + EPS) * w

        def _attention(x, Wq, Wk, Wv, Wo):
            b, s, d = x.shape
            q = (x @ Wq.T).reshape(b, s, H, HD)
            k = (x @ Wk.T).reshape(b, s, H, HD)
            v = (x @ Wv.T).reshape(b, s, H, HD)
            scores = jnp.einsum('bqhd,bkhd->bhqk', q, k) / np.sqrt(HD).astype(np.float32)
            causal = jnp.tril(jnp.ones((s, s), bool))
            scores = jnp.where(causal, scores, jnp.finfo(scores.dtype).min)
            probs = jax.nn.softmax(scores, axis=-1)
            out = jnp.einsum('bhqk,bkhd->bqhd', probs, v).reshape(b, s, d)
            return out @ Wo.T
        residual = hidden_states
        x = _rmsnorm(hidden_states, ln1_w)
        attn = _attention(x, Wq, Wk, Wv, Wo)
        mod = MOD_SCALE * jnp.tanh(attn @ A)
        h = _rmsnorm(residual, ln2_w)
        gate_pre = h @ W_in_base.T + mod * (h @ A) @ B
        gate = jax.nn.silu(gate_pre)
        up = h @ W_up_base.T
        mlp_out = gate * up @ W_down.T
        return residual + mlp_out

    def _L2_xattn_ref(hidden_states, encoder_hidden_states, Wq, Wk, Wv, Wo, gq, gk):
        import jax, jax.numpy as jnp
        import numpy as np
        EPS = 1e-05

        def rmsnorm(x, g, eps=EPS):
            var = jnp.mean(jnp.square(x), axis=-1, keepdims=True)
            return x * jax.lax.rsqrt(var + eps) * g
        B, Sq, _ = hidden_states.shape
        Skv = encoder_hidden_states.shape[1]
        D = gq.shape[0]
        H = Wq.shape[1] // D
        scale = 1.0 / np.sqrt(D)
        q = (hidden_states @ Wq).reshape(B, Sq, H, D)
        k = (encoder_hidden_states @ Wk).reshape(B, Skv, H, D)
        v = (encoder_hidden_states @ Wv).reshape(B, Skv, H, D)
        q = rmsnorm(q, gq)
        k = rmsnorm(k, gk)
        scores = jnp.einsum('bqhd,bkhd->bhqk', q, k) * scale
        attn = jax.nn.softmax(scores, axis=-1)
        out = jnp.einsum('bhqk,bkhd->bqhd', attn, v)
        out = out.reshape(B, Sq, H * D)
        return out @ Wo

    def _L2_ffn_ref(x, w_gate, w_up, w_down):
        import jax, jax.numpy as jnp
        import numpy as np
        DIM_IN = 256
        DIM_HIDDEN = 1024
        gate = jnp.einsum('bsd,hd->bsh', x, w_gate)
        up = jnp.einsum('bsd,hd->bsh', x, w_up)
        gated = jax.nn.silu(gate) * up
        return jnp.einsum('bsh,dh->bsd', gated, w_down)

    def _L3_xattn_ref(x, y, Wq, bq, Wk, bk, Wv, bv, Wkv_dca, bkv_dca, qn_w, qn_b, kn_w, kn_b, kn_dca_w, kn_dca_b, Wo, bo):
        import jax, jax.numpy as jnp
        import numpy as np
        B, S1, S2, DCA = (2, 256, 128, 16)
        QDIM, KDIM, H = (256, 128, 16)
        HD = QDIM // H
        SCALE = HD ** (-0.5)
        EPS = 1e-06
        DCA_WEIGHT = 1.0

        def _ln(t, w, b):
            m = jnp.mean(t, axis=-1, keepdims=True)
            v = jnp.var(t, axis=-1, keepdims=True)
            return (t - m) * jax.lax.rsqrt(v + EPS) * w + b

        def _attn(q, k, v):
            s = jnp.einsum('bhqd,bhkd->bhqk', q, k) * SCALE
            p = jax.nn.softmax(s, axis=-1)
            return jnp.einsum('bhqk,bhkd->bhqd', p, v)
        b, s1, _ = x.shape
        y_dca = y[:, -DCA:, :]
        y_main = y[:, :-DCA, :]
        kv_dca = (y_dca @ Wkv_dca + bkv_dca).reshape(b, DCA, 2, H, HD)
        k_dca = _ln(kv_dca[:, :, 0], kn_dca_w, kn_dca_b)
        v_dca = kv_dca[:, :, 1]
        s2 = y_main.shape[1]
        q = _ln((x @ Wq + bq).reshape(b, s1, H, HD), qn_w, qn_b)
        kv = jnp.concatenate([y_main @ Wk + bk, y_main @ Wv + bv], axis=-1)
        kv = kv.reshape(b, s2, H, 2 * HD)
        k = _ln(kv[..., :HD], kn_w, kn_b)
        v = kv[..., HD:]
        qT = q.transpose(0, 2, 1, 3)
        ctx = _attn(qT, k.transpose(0, 2, 1, 3), v.transpose(0, 2, 1, 3))
        ctx = ctx.transpose(0, 2, 1, 3).reshape(b, s1, QDIM)
        ctx_dca = _attn(qT, k_dca.transpose(0, 2, 1, 3), v_dca.transpose(0, 2, 1, 3))
        ctx_dca = ctx_dca.transpose(0, 2, 1, 3).reshape(b, s1, QDIM)
        ctx = ctx + DCA_WEIGHT * ctx_dca
        return ctx @ Wo + bo

    def _L3_ffn_ref(hidden_states, router_w, w1, w2, w_gate, w_up, w_down):
        import jax, jax.numpy as jnp
        import numpy as np
        B, S, H = (4, 256, 256)
        INTER = 512
        E = 8
        TOPK = 2
        SHARED_I = INTER * 2

        def moe_forward(hidden_states, router_w, w1, w2, w_gate, w_up, w_down):
            b, s, h = hidden_states.shape
            x = hidden_states.reshape(-1, h)
            T = x.shape[0]
            logits = x @ router_w
            top_logits, top_indices = jax.lax.top_k(logits, TOPK)
            scores = jax.nn.softmax(top_logits, axis=-1)
            flat_idx = top_indices.reshape(-1)
            sorted_pos = jnp.argsort(flat_idx, stable=True)
            permuted = x[sorted_pos // TOPK]
            expert_ids = flat_idx[sorted_pos]
            out = jnp.zeros((T * TOPK, h), x.dtype)
            for e in range(E):
                mask = (expert_ids == e)[:, None]
                f1 = permuted * mask @ w1[e]
                g, u = jnp.split(f1, 2, axis=-1)
                act = jax.nn.silu(g) * u
                out = out + jnp.where(mask, act @ w2[e], 0.0)
            unperm = jnp.zeros_like(out).at[sorted_pos].set(out)
            combined = (unperm.reshape(T, TOPK, h) * scores[..., None]).sum(axis=1)
            shared = jax.nn.silu(x @ w_gate) * (x @ w_up) @ w_down
            return (combined + shared).reshape(b, s, h)
        return moe_forward(hidden_states, router_w, w1, w2, w_gate, w_up, w_down)
    x = x + jnp.tanh(g_xattn[0]) * _L0_xattn_ref(_layernorm(x, axis=-1), ctx_1024, fside_BxSx2_0, fside_BxSx2_0, L0_xattn_Wq, L0_xattn_Wkv, L0_xattn_Wout, L0_xattn_bout)
    x = x + jnp.tanh(g_ffn[0]) * _L0_ffn_ref(_layernorm(x, axis=-1), L0_ffn_w1, L0_ffn_w2, L0_ffn_w3)
    x = x + jnp.tanh(g_xattn[1]) * _L1_xattn_ref(_layernorm(x, axis=-1), ctx_1024, mask_BxS2_bf1, L1_xattn_Wq, L1_xattn_Wk, L1_xattn_Wv, L1_xattn_Wo)
    x = x + jnp.tanh(g_ffn[1]) * _L1_ffn_ref(_layernorm(x, axis=-1), L1_ffn_ln1_w, L1_ffn_ln2_w, L1_ffn_Wq, L1_ffn_Wk, L1_ffn_Wv, L1_ffn_Wo, L1_ffn_A, L1_ffn_B, L1_ffn_W_in_base, L1_ffn_W_up_base, L1_ffn_W_down)
    x = x + jnp.tanh(g_xattn[2]) * _L2_xattn_ref(_layernorm(x, axis=-1), ctx_1024, L2_xattn_Wq, L2_xattn_Wk, L2_xattn_Wv, L2_xattn_Wo, L2_xattn_gq, L2_xattn_gk)
    x = x + jnp.tanh(g_ffn[2]) * _L2_ffn_ref(_layernorm(x, axis=-1), L2_ffn_w_gate, L2_ffn_w_up, L2_ffn_w_down)
    x = x + jnp.tanh(g_xattn[3]) * _L3_xattn_ref(_layernorm(x, axis=-1), ctx_1024, L3_xattn_Wq, L3_xattn_bq, L3_xattn_Wk, L3_xattn_bk, L3_xattn_Wv, L3_xattn_bv, L3_xattn_Wkv_dca, L3_xattn_bkv_dca, L3_xattn_qn_w, L3_xattn_qn_b, L3_xattn_kn_w, L3_xattn_kn_b, L3_xattn_kn_dca_w, L3_xattn_kn_dca_b, L3_xattn_Wo, L3_xattn_bo)
    x = x + jnp.tanh(g_ffn[3]) * _L3_ffn_ref(_layernorm(x, axis=-1), L3_ffn_router_w, L3_ffn_w1, L3_ffn_w2, L3_ffn_w_gate, L3_ffn_w_up, L3_ffn_w_down)
    return x

_drawn_inputs = setup_inputs


def setup_inputs(seed=0):
    import zlib

    import numpy as np

    out = dict(_drawn_inputs(seed))
    spreads = {'L0_xattn_bout': (0.0, 0.1),
     'L1_ffn_ln1_w': (1.0, 0.6),
     'L1_ffn_ln2_w': (1.0, 0.6),
     'L2_xattn_gq': (1.0, 0.6),
     'L2_xattn_gk': (1.0, 0.6),
     'L3_xattn_bq': (0.0, 2.0),
     'L3_xattn_bk': (0.0, 0.8),
     'L3_xattn_bv': (0.0, 0.8),
     'L3_xattn_bkv_dca': (0.0, 0.778),
     'L3_xattn_qn_w': (1.0, 0.6),
     'L3_xattn_qn_b': (0.0, 0.8),
     'L3_xattn_kn_w': (1.0, 0.6),
     'L3_xattn_kn_b': (0.0, 2.0),
     'L3_xattn_kn_dca_w': (1.0, 0.6),
     'L3_xattn_kn_dca_b': (0.0, 2.0),
     'L3_xattn_bo': (0.0, 0.1)}
    factors = {'g_ffn': 25.424,
     'L0_ffn_w1': 8.0,
     'L0_ffn_w2': 8.0,
     'L0_ffn_w3': 8.0,
     'L1_xattn_Wq': 8.0,
     'L1_xattn_Wk': 8.0,
     'L1_ffn_Wq': 64.0,
     'L1_ffn_Wk': 55.222,
     'L1_ffn_Wv': 36.871,
     'L1_ffn_Wo': 49.514,
     'L1_ffn_A': 55.239,
     'L1_ffn_B': 55.244,
     'L1_ffn_W_in_base': 3.566,
     'L1_ffn_W_up_base': 3.535,
     'L1_ffn_W_down': 3.536,
     'L3_xattn_Wq': 7.906,
     'L3_xattn_Wk': 5.6,
     'L3_xattn_Wv': 5.65,
     'L3_xattn_Wkv_dca': 3.57,
     'L3_ffn_router_w': 8.0,
     'L3_ffn_w1': 7.841,
     'L3_ffn_w2': 7.862,
     'L3_ffn_w_gate': 4.031,
     'L3_ffn_w_up': 3.975,
     'L3_ffn_w_down': 3.976}
    for name, (base, spread) in spreads.items():
        noise = np.random.default_rng([zlib.crc32(name.encode()), seed]).standard_normal(out[name].shape)
        drawn = base * np.exp(spread * noise) if base else spread * noise
        out[name] = jnp.asarray(drawn.astype(out[name].dtype))
    for name, factor in factors.items():
        out[name] = (out[name] * factor).astype(out[name].dtype)
    return out
```

```python
from contextlib import ExitStack

import numpy as np

import concourse.bass as bass
from concourse import mybir

ALU = mybir.AluOpType
ACT = mybir.ActivationFunctionType
F32 = mybir.dt.float32
BF16 = mybir.dt.bfloat16
U8 = mybir.dt.uint8
AX = mybir.AxisListType.X

BATCH, TOK, DIM, CDIM = 16, 128, 256, 128
P = 128
KD = DIM // P
GROUP = 4
TURNS = BATCH // GROUP
GT = GROUP * TOK
SLOT = 32
HID0 = 704
HID0P = 768
FF = 1024
EXPERTS, INTER = 8, 512
MAIN = 112
DCA = TOK - MAIN
MAGIC = 12582912.0
BIG = 1e30
PI = float(np.pi)
INPUTS = 4

LAYOUT = [
    [("wq", KD * DIM), ("wk", DIM), ("wv", DIM), ("wo", KD * DIM), ("bo", DIM)],
    [("w1", KD * HID0), ("w3", KD * HID0), ("w2", HID0P // P * DIM)],
    [("wq", KD * 2048), ("wk", 1024), ("wv", 1024), ("wo", 16 * DIM)],
    [("wq", KD * DIM), ("wk", KD * DIM), ("wv", KD * DIM), ("wo", KD * DIM), ("a", KD * 16), ("a2", KD * 16), ("bm", FF),
     ("gate", KD * FF), ("up", KD * FF), ("down", FF // P * DIM), ("ln1", KD), ("ln2", KD)],
    [("wq", KD * 2048), ("wk", 2048), ("wv", 2048), ("wo", 16 * DIM), ("gq", 1), ("gk", 1)],
    [("gate", KD * FF), ("up", KD * FF), ("down", FF // P * DIM)],
    [("wq", KD * DIM), ("wk", DIM), ("wv", DIM), ("wkd", DIM), ("wvd", DIM), ("wo", KD * DIM), ("bq", DIM),
     ("bk", DIM), ("bv", DIM), ("bkd", DIM), ("bvd", DIM), ("bo", DIM), ("norms", 6)],
    [("gate", KD * FF), ("up", KD * FF), ("down", FF // P * DIM), ("router", KD * EXPERTS)],
    [("gate", 4 * KD * INTER), ("up", 4 * KD * INTER), ("down", 4 * INTER // P * DIM)],
    [("gate", 4 * KD * INTER), ("up", 4 * KD * INTER), ("down", 4 * INTER // P * DIM)],
]
WIDTH = [sum(c for _, c in part) for part in LAYOUT]
WMAX = max(WIDTH)


class Count:

    def __init__(self, sem):
        self.sem, self.base, self.per, self.turns = sem, 1, 0, 0

    def begin(self, per, turns=TURNS):
        self.base += self.per * self.turns
        self.per, self.turns = per, turns

    def at(self, i, n):
        return i * self.per + (self.base + n)


def build(nc, stop, x_in, ctxT_in, pos_in, mrow_in, mcol_in, gates_in, freq_in, weights, out):
    with ExitStack() as ctx:
        def sb(name, shape, dt=F32):
            return ctx.enter_context(nc.sbuf_tensor(name, shape, dt))

        def count(name):
            return Count(ctx.enter_context(nc.semaphore(name)))

        X = sb("X", [P, BATCH, DIM])
        XNT = sb("XNT", [P, KD, BATCH * TOK])
        WREG = [sb(f"WREG{r}", [P, WMAX]) for r in range(2)]
        TG = sb("TG", [P, 8])
        SINCOS = sb("SINCOS", [P, 2, BATCH, 4])
        MCOL = sb("MCOL", [P, BATCH])
        IDENT = sb("IDENT", [P, P])
        IDENTB = sb("IDENTB", [P, P], BF16)
        CAUSAL = sb("CAUSAL", [P, P], BF16)
        ONES = sb("ONES", [P, P])
        ONESB = sb("ONESB", [1, P], BF16)
        SEG = sb("SEG", [1, 2, P])
        MHALF = sb("MHALF", [P, 64])
        AQ = sb("AQ", [P, BATCH])
        RW = sb("RW", [P, BATCH, EXPERTS])
        XS = sb("XS", [P, KD, GT])
        CS = sb("CS", [P, 2, GT])
        QT = sb("QT", [P, 4096])
        KT = sb("KT", [P, 4096])
        VS = sb("VS", [P, 4096])
        MODT = KT[0:16, 2048:4096]
        QP = sb("QP", [P, 1024])
        KP = sb("KP", [P, 1024])
        PR = sb("PR", [P, 2, 512])
        PTS = sb("PTS", [P, 2, 512])
        T1 = PTS[:, :, :].rearrange("p a n -> p (a n)")
        OTOK = sb("OTOK", [P, DIM])
        OT = sb("OT", [P, KD, TOK])
        STAT = sb("STAT", [P, 256])
        PS = [ctx.enter_context(nc.psum_tensor(f"PS{b}", [P, 512], F32)) for b in range(8)]
        PSB = [b[:, :].bitcast(BF16) for b in PS]

        w_loaded = [count(f"w_loaded{s}") for s in range(10)]
        inputs_loaded = count("inputs_loaded")
        stored = count("stored")
        dve_step, act_step, pool_step = count("dve_step"), count("act_step"), count("pool_step")
        rstd_in, rstd_out = count("rstd_in"), count("rstd_out")
        xn_ready, xnT_ps, xnT_sb = count("xn_ready"), count("xnT_ps"), count("xnT_sb")
        copied = count("copied")
        ctx_loaded = count("ctx_loaded")
        qk_ps, v_ps, qk_pad, qkT_ps, qkT_sb, v_sb = (count(n) for n in ("qk_ps", "v_ps", "qk_pad", "qkT_ps", "qkT_sb", "v_sb"))
        s_ps, s_sub, p_exp, p_norm, pT_ps, pT_sb, av_ps = (count(n) for n in ("s_ps", "s_sub", "p_exp", "p_norm", "pT_ps", "pT_sb", "av_ps"))
        o_tok, oT_ps, oT_sb, out_ps, x_done = (count(n) for n in ("o_tok", "oT_ps", "oT_sb", "out_ps", "x_done"))
        gu_ps, silu_done, h_done, down_ps = (count(n) for n in ("gu_ps", "silu_done", "h_done", "down_ps"))
        sq_done = count("sq_done")
        gained = count("gained")
        mask_loaded = count("mask_loaded")
        quant_step = count("quant_step")
        q_ps, qT_sb = count("q_ps"), count("qT_sb")

        STEPS = 256

        def apart(eng):
            eng.memset(STAT[:, 255:256], 0.0)

        class Chain:

            def __init__(self, eng, cnt, i=0):
                self.eng, self.cnt, self.i, self.n = eng, cnt, i, 0

            def step(self, ins):
                self.n += 1
                ins.then_inc(self.cnt.sem, 1)

            def settle(self):
                self.eng.wait_ge(self.cnt.sem, self.cnt.at(self.i, self.n))

            def link(self, ins):
                self.step(ins)
                self.settle()

            def close(self):
                self.settle()
                self.eng.sem_inc(self.cnt.sem, STEPS - self.n)

        def w(s, name):
            at = 0
            for n, c in LAYOUT[s]:
                if n == name:
                    return WREG[s % 2][:, at:at + c]
                at += c
            raise KeyError(name)

        def wk(s, name, k):
            return w(s, name).rearrange("p (k n) -> p k n", k=k)

        def load_weights(sp, s):
            half = WIDTH[s] // 2
            for a, b in ((0, half), (half, WIDTH[s])):
                sp.dma_start(WREG[s % 2][:, a:b], weights[s][:, a:b]).then_inc(w_loaded[s].sem, 16)

        def begin(turns, **per):
            for name, n in per.items():
                named[name].begin(n, turns)

        named = dict(dve_step=dve_step, act_step=act_step, pool_step=pool_step, rstd_in=rstd_in, rstd_out=rstd_out,
                     xn_ready=xn_ready, xnT_ps=xnT_ps, xnT_sb=xnT_sb, copied=copied, qk_ps=qk_ps, v_ps=v_ps,
                     qk_pad=qk_pad, qkT_ps=qkT_ps, qkT_sb=qkT_sb, v_sb=v_sb, s_ps=s_ps, s_sub=s_sub, p_exp=p_exp,
                     p_norm=p_norm, pT_ps=pT_ps, pT_sb=pT_sb, av_ps=av_ps, o_tok=o_tok, oT_ps=oT_ps, oT_sb=oT_sb,
                     out_ps=out_ps, x_done=x_done, gu_ps=gu_ps, silu_done=silu_done, h_done=h_done,
                     down_ps=down_ps, sq_done=sq_done, gained=gained, ctx_loaded=ctx_loaded, q_ps=q_ps, qT_sb=qT_sb)

        def first_block():
            begin(1, dve_step=STEPS, act_step=STEPS, pool_step=STEPS, p_exp=1, s_sub=1)
            ang = T1[:, 0:128].rearrange("p (c b f) -> p c b f", c=2, b=BATCH)
            turn = T1[:, 128:256].rearrange("p (c b f) -> p c b f", c=2, b=BATCH)
            pos = QP[:, 0:BATCH * 2].rearrange("p (b a) -> p b a", a=2)
            mcol8 = QT[:, 1024:1028].bitcast(U8)
            with nc.Block() as block:
                @block.sync
                def _(sp):
                    sp.dma_start(pos, pos_in).then_inc(inputs_loaded.sem, 16)
                    sp.dma_start(mcol8, mcol_in).then_inc(inputs_loaded.sem, 16)
                    sp.dma_start(QP[:, 512:520], gates_in).then_inc(inputs_loaded.sem, 16)
                    sp.dma_start(X[:, :, :], x_in).then_inc(inputs_loaded.sem, 16)
                    load_weights(sp, 0)

                @block.gpsimd
                def _(pool):
                    for c in named.values():
                        pool.sem_inc(c.sem, 1)
                    ch = Chain(pool, pool_step)
                    ch.step(pool.memset(IDENT[:, :], 0.0))
                    ch.step(pool.memset(IDENTB[:, :], 0.0))
                    ch.step(pool.memset(CAUSAL[:, :], 0.0))
                    ch.step(pool.memset(ONES[:, :], 1.0))
                    ch.step(pool.memset(ONESB[:, :], 1.0))
                    ch.step(pool.memset(SEG[:, 0, :], 1.0))
                    ch.step(pool.memset(SEG[:, 1, :], 0.0))
                    ch.step(pool.memset(MHALF[:, :], -0.5))
                    ch.step(pool.memset(KP[:, :], 0.0))
                    ch.settle()
                    for m in (IDENT, IDENTB):
                        ch.step(pool.affine_select(out=m[:, :], in_=m[:, :], compare_op=ALU.not_equal, fill=1.0,
                                                   base=0, pattern=[[-1, P]], channel_multiplier=1))
                    ch.step(pool.affine_select(out=CAUSAL[:, :], in_=CAUSAL[:, :], compare_op=ALU.is_ge, fill=-BIG,
                                               base=0, pattern=[[-1, P]], channel_multiplier=1))
                    ch.step(pool.memset(SEG[:, 0, MAIN:P], 0.0))
                    ch.step(pool.memset(SEG[:, 1, MAIN:P], 1.0))
                    ch.close()

                @block.vector
                def _(dve):
                    ch = Chain(dve, dve_step)
                    dve.wait_ge(inputs_loaded.sem, 16 * INPUTS)
                    for f, freq in enumerate((1.0, 10000.0 ** -0.5)):
                        for c in range(2):
                            dst = ang[:, c, :, :].rearrange("p b (a f) -> p b a f", f=2)[:, :, :, f]
                            ch.step(dve.tensor_scalar(dst, pos, freq, 0.5 * PI * c, ALU.mult, ALU.add))
                    ch.settle()
                    ch.link(dve.tensor_scalar(turn, ang, 0.5 / PI, MAGIC, ALU.mult, ALU.add))
                    ch.link(dve.tensor_scalar(turn, turn, MAGIC, -2.0 * PI, ALU.subtract, ALU.mult))
                    ch.link(dve.tensor_tensor(ang, ang, turn, ALU.add))
                    ch.link(dve.tensor_scalar(ang, ang, 3.1415925, -3.1415925, ALU.min, ALU.max))
                    ch.step(dve.tensor_copy(MCOL[:, :], mcol8[:, 0:BATCH]))
                    ch.step(dve.memset(QP[:, 0:512], 0.0))
                    ch.settle()
                    ch.link(dve.memset(STAT[:, :], 0.0))
                    dve.sem_inc(s_sub.sem, 1)
                    dve.wait_ge(p_exp.sem, p_exp.at(0, 1))
                    ch.link(dve.memset(QP[:, 512:1024], 0.0))
                    ch.close()

                @block.scalar
                def _(act):
                    act.wait_ge(s_sub.sem, s_sub.at(0, 1))
                    nc.scalar.activation(SINCOS[:, :, :, :], ang, ACT.Sin).then_inc(act_step.sem, 1)
                    nc.scalar.activation(TG[:, :], QP[:, 512:520], ACT.Tanh).then_inc(p_exp.sem, 1)
                    act.wait_ge(p_exp.sem, p_exp.at(0, 1))
                    act.sem_inc(act_step.sem, STEPS - 1)

        def norm_block(prefetch, kind="plain", tg=None):
            begin(TURNS, dve_step=STEPS, rstd_in=1 + (kind == "rms"), rstd_out=1 + (kind == "rms"), xn_ready=1,
                  xnT_ps=KD, xnT_sb=KD)
            XN = QT[:, 0:GROUP * DIM].rearrange("p (b d) -> p b d", d=DIM)
            SQ = QT[:, GROUP * DIM:2 * GROUP * DIM].rearrange("p (b d) -> p b d", d=DIM)
            st = STAT[:, 0:6 * GROUP].rearrange("p (b c) -> p b c", c=6)
            mv = STAT[:, 32:32 + 2 * GROUP].rearrange("p (b c) -> p b c", c=2)
            var, rstd = STAT[:, 48:48 + GROUP], STAT[:, 56:56 + GROUP]
            aux, rinv = STAT[:, 64:64 + GROUP], STAT[:, 72:72 + GROUP]
            XQT = XNT[:, 0, :].bitcast(BF16).rearrange("p (k t) -> p k t", k=KD)
            with nc.Block() as block:
                if prefetch is not None:
                    @block.sync
                    def _(sp):
                        load_weights(sp, prefetch)

                @block.vector
                def _(dve):
                    with dve.Fori(0, TURNS) as i:
                        ch = Chain(dve, dve_step, i)
                        for b in range(GROUP):
                            ch.step(dve.bn_stats(st[:, b, :], X[:, bass.ds(i * GROUP + b, 1), :].rearrange("p a d -> p (a d)")))
                        ch.settle()
                        apart(dve)
                        for b in range(GROUP):
                            ch.step(dve.bn_aggr(mv[:, b, :], st[:, b, :]))
                        ch.settle()
                        dve.tensor_scalar(var, mv[:, :, 1], 1e-5, None, ALU.add).then_inc(rstd_in.sem, 1)
                        dve.wait_ge(rstd_out.sem, rstd_out.at(i, 1))
                        dve.wait_ge(xnT_ps.sem, xnT_ps.at(i, 0))
                        for b in range(GROUP):
                            ins = dve.tensor_scalar(XN[:, b, :], X[:, bass.ds(i * GROUP + b, 1), :].rearrange("p a d -> p (a d)"),
                                                    mv[:, b, 0:1], rstd[:, b:b + 1], ALU.subtract, ALU.mult)
                            if kind == "plain" and b == GROUP - 1:
                                ins.then_inc(xn_ready.sem, 1)
                            else:
                                ch.step(ins)
                        if kind == "rms":
                            ch.settle()
                            for b in range(GROUP):
                                ch.step(dve.tensor_tensor_reduce(SQ[:, b, :], XN[:, b, :], XN[:, b, :], 1.0, 0.0,
                                                                 ALU.mult, ALU.add, aux[:, b:b + 1]))
                                xb = X[:, bass.ds(i * GROUP + b, 1), :].rearrange("p a d -> p (a d)")
                                ch.step(dve.scalar_tensor_tensor(out=xb, in0=XN[:, b, :], scalar=TG[:, tg:tg + 1],
                                                                 in1=xb, op0=ALU.mult, op1=ALU.add))
                            ch.settle()
                            dve.tensor_scalar(var, aux, 1.0 / DIM, 1e-6, ALU.mult, ALU.add).then_inc(rstd_in.sem, 1)
                            dve.wait_ge(rstd_out.sem, rstd_out.at(i, 2))
                            ch.settle()
                            dve.tensor_tensor(XN[:, :, :], XN[:, :, :], rstd.unsqueeze(2).broadcast_to([P, GROUP, DIM]),
                                              ALU.mult).then_inc(xn_ready.sem, 1)
                        if kind == "quant":
                            ch.settle()
                            ch.link(dve.tensor_reduce(aux, XN[:, :, :], AX, ALU.max, apply_absolute_value=True))
                            ch.link(dve.tensor_scalar(aux, aux, 1e-5, None, ALU.max))
                            ch.step(dve.tensor_scalar(AQ[:, bass.ds(i * GROUP, GROUP)], aux, 1.0 / 127.0, None, ALU.mult))
                            ch.link(dve.reciprocal(rinv, aux))
                            ch.link(dve.tensor_scalar(rinv, rinv, 127.0, None, ALU.mult))
                            for b in range(GROUP):
                                ch.step(dve.tensor_scalar(XN[:, b, :], XN[:, b, :], rinv[:, b:b + 1], MAGIC, ALU.mult, ALU.add))
                            ch.settle()
                            ch.link(dve.tensor_scalar(XN[:, :, :], XN[:, :, :], MAGIC + 127.0, MAGIC - 128.0, ALU.min, ALU.max))
                            dve.tensor_scalar(XN[:, :, :], XN[:, :, :], MAGIC, None, ALU.subtract).then_inc(xn_ready.sem, 1)
                        ch.close()

                @block.gpsimd
                def _(pool):
                    with pool.Fori(0, TURNS) as i:
                        for n in range(1 + (kind == "rms")):
                            pool.wait_ge(rstd_in.sem, rstd_in.at(i, n + 1))
                            pool.tensor_tensor(rstd, var, MHALF[:, 0:GROUP], ALU.pow).then_inc(rstd_out.sem, 1)

                @block.tensor
                def _(pe):
                    with pe.Fori(0, TURNS) as i:
                        pe.wait_ge(xn_ready.sem, xn_ready.at(i, 1))
                        for k in range(KD):
                            pe.wait_ge(xnT_sb.sem, xnT_sb.at(i, 0))
                            for b in range(GROUP):
                                ins = pe.transpose(PS[k][:, b * P:(b + 1) * P], XN[:, b, k * P:(k + 1) * P], IDENT[:, :])
                            ins.then_inc(xnT_ps.sem, 1)

                @block.scalar
                def _(act):
                    dst = XQT if kind == "quant" else XNT
                    with act.Fori(0, TURNS) as i:
                        for k in range(KD):
                            act.wait_ge(xnT_ps.sem, xnT_ps.at(i, k + 1))
                            act.copy(dst[:, k, bass.ds(i * GT, GT)], PS[k][:, :]).then_inc(xnT_sb.sem, 1)

        def small_attention(s, tg, NH, HD, kind, prefetch=None):
            NB, NS = NH // 4, NH // 4
            V = HD + 1
            N = GROUP * NS
            seg = kind == "dca"
            segs = ((0, MAIN), (MAIN, TOK)) if seg else ((0, TOK),)
            begin(TURNS, dve_step=STEPS, act_step=STEPS, copied=1, ctx_loaded=0 if kind == "causal" else 16 * len(segs), qk_ps=GROUP, v_ps=GROUP, qk_pad=GROUP,
                  qkT_ps=2 * GROUP, qkT_sb=2 * GROUP, v_sb=GROUP, s_ps=N, s_sub=N, p_exp=N, p_norm=N if seg else 0,
                  pT_ps=N, pT_sb=N, av_ps=N, o_tok=GROUP, oT_ps=GROUP, oT_sb=GROUP, out_ps=GROUP, x_done=GROUP,
                  rstd_in=2 * GROUP if seg else 0, rstd_out=2 * GROUP if seg else 0,
                  q_ps=GROUP if kind == "causal" else 0, qT_sb=GROUP if kind == "causal" else 0)
            begin(1, pool_step=1, gained=1 if kind == "causal" else 0)
            p_ready = p_norm if seg else p_exp
            wq, wo = wk(s, "wq", KD), wk(s, "wo", KD)
            qT = QT[:, 0:GROUP * NB * P].rearrange("p (b n t) -> p b n t", b=GROUP, n=NB)
            kT = KT[:, 0:GROUP * NB * P].rearrange("p (b n t) -> p b n t", b=GROUP, n=NB)
            vs = VS[:, 0:GROUP * NH * V].rearrange("p (b h v) -> p b h v", b=GROUP, h=NH)
            qp = QP[:, 0:NH * SLOT].rearrange("p (h e) -> p h e", e=SLOT)
            kp = KP[:, 0:NH * SLOT].rearrange("p (h e) -> p h e", e=SLOT)
            nmax = STAT[:, 0:8].rearrange("p (a h) -> p a h", a=2)
            nmax2 = STAT[:, 8:16].rearrange("p (a h) -> p a h", a=2)
            psums = STAT[:, 16:32].rearrange("p (a h) -> p a h", a=2)
            rsum = STAT[:, 32:32 + NH]
            hsum = STAT[:, 64:64 + 2 * NH].rearrange("p (a h) -> p a h", a=2)
            hvar = STAT[:, 128:128 + 2 * NH].rearrange("p (a h) -> p a h", a=2)
            hrstd = STAT[:, 192:192 + 2 * NH].rearrange("p (a h) -> p a h", a=2)
            segs = ((0, MAIN), (MAIN, TOK)) if seg else ((0, TOK),)
            END = N + 8

            with nc.Block() as block:
                @block.sync
                def _(sp):
                    if prefetch is not None:
                        load_weights(sp, prefetch)
                    if kind != "causal":
                        if seg:
                            sp.wait_ge(pool_step.sem, pool_step.at(0, 1))
                        with sp.Fori(0, TURNS) as i:
                            sp.wait_ge(v_ps.sem, v_ps.at(i, 0))
                            for a, (lo, hi) in enumerate(segs):
                                src = ctxT_in[:, bass.ds(i * GROUP, GROUP), lo:hi]
                                dst = CS[:, a, :].rearrange("p (b t) -> p b t", t=TOK)[:, :, lo:hi]
                                sp.dma_start(dst, src).then_inc(ctx_loaded.sem, 16)

                @block.gpsimd
                def _(pool):
                    if seg:
                        pool.memset(CS[:, :, :], 0.0).then_inc(pool_step.sem, 1)
                    else:
                        pool.memset(VS[:, 0:GROUP * NH * V], 1.0).then_inc(pool_step.sem, 1)
                    with pool.Fori(0, TURNS) as i:
                        pool.wait_ge(v_ps.sem, v_ps.at(i, 0))
                        pool.tensor_copy(XS[:, :, :], XNT[:, :, bass.ds(i * GT, GT)]).then_inc(copied.sem, 1)
                        if seg:
                            for n in range(2 * GROUP):
                                pool.wait_ge(rstd_in.sem, rstd_in.at(i, n + 1))
                                pool.tensor_tensor(hrstd[:, n % 2, :], hvar[:, n % 2, :], MHALF[:, 0:NH],
                                                   ALU.pow).then_inc(rstd_out.sem, 1)

                @block.tensor
                def _(pe):
                    pe.wait_ge(w_loaded[s].sem, 32)
                    if kind == "causal":
                        pe.wait_ge(gained.sem, gained.at(0, 1))

                    def project(i, b):
                        if b == 0:
                            pe.wait_ge(copied.sem, copied.at(i, 1))
                            if kind != "causal":
                                pe.wait_ge(ctx_loaded.sem, ctx_loaded.at(i, 16 * len(segs)))
                            pe.wait_ge(x_done.sem, x_done.at(i, 0))
                            if kind == "causal":
                                pe.wait_ge(qT_sb.sem, qT_sb.at(i, 0))
                        else:
                            pe.wait_ge(qk_pad.sem, qk_pad.at(i, b))
                        tok = slice(b * TOK, (b + 1) * TOK)
                        q, k, v = PS[6][:, 0:DIM], PS[6][:, DIM:2 * DIM], PS[7][:, 0:DIM]
                        for c in range(KD):
                            ins = pe.matmul(q, XS[:, c, tok], wq[:, c, :], start=(c == 0), stop=(c == KD - 1 and not seg))
                        if seg:
                            pe.matmul(q, ONES[0:1, :], w(s, "bq")[0:1, :], start=False, stop=True)

                        def context(dst, names, biases):
                            if kind == "causal":
                                for c in range(KD):
                                    ins = pe.matmul(dst, XS[:, c, tok], wk(s, names[0], KD)[:, c, :], start=(c == 0),
                                                    stop=(c == KD - 1))
                                return ins
                            if not seg:
                                return pe.matmul(dst, CS[:, 0, tok], w(s, names[0]), start=True, stop=True)
                            for a in range(2):
                                pe.matmul(dst, CS[:, a, tok], w(s, names[a]), start=(a == 0), stop=False)
                            for a in range(2):
                                ins = pe.matmul(dst, SEG[0:1, a, :], w(s, biases[a])[0:1, :], start=False, stop=(a == 1))
                            return ins

                        context(k, ("wk", "wkd"), ("bk", "bkd")).then_inc(qk_ps.sem, 1)
                        if b:
                            pe.wait_ge(v_sb.sem, v_sb.at(i, b))
                        context(v, ("wv", "wvd"), ("bv", "bvd")).then_inc(v_ps.sem, 1)

                    def turn_heads(i, b):
                        pe.wait_ge(qkT_sb.sem, qkT_sb.at(i, 2 * b))
                        pe.wait_ge(qk_pad.sem, qk_pad.at(i, b + 1))
                        for src, bank in ((QP, 2), (KP, 0)):
                            for n in range(NB):
                                ins = pe.transpose(PS[bank + n // 4][:, n % 4 * P:(n % 4 + 1) * P],
                                                   src[:, n * P:(n + 1) * P], IDENT[:, :])
                            ins.then_inc(qkT_ps.sem, 1)

                    def scores(i, t):
                        b, u = divmod(t, NS)
                        j, half = u % 4, u // 4
                        if t == 0:
                            pe.wait_ge(qkT_sb.sem, qkT_sb.at(i, 2 * GROUP))
                        if t >= 2:
                            pe.wait_ge(s_sub.sem, s_sub.at(i, t - 1))
                        if kind == "causal":
                            pe.matmul(PS[t % 2][:, :].rearrange("p (h c) -> p h c", h=4), IDENTB[:, :],
                                      CAUSAL[:, :].unsqueeze(1).broadcast_to([P, 4, P]), start=True, stop=False,
                                      skip_group_check=True)
                        for c in range(4):
                            rows = slice(SLOT * j, SLOT * j + HD)
                            ins = pe.matmul(PS[t % 2][:, c * P:(c + 1) * P], qT[rows, b, 4 * half + c, :],
                                            kT[rows, b, 4 * half + c, :], start=(kind != "causal"), stop=True,
                                            skip_group_check=True)
                        ins.then_inc(s_ps.sem, 1)

                    def turn_probs(i, t):
                        pe.wait_ge(p_ready.sem, p_ready.at(i, t + 1))
                        if t >= 2:
                            pe.wait_ge(pT_sb.sem, pT_sb.at(i, t - 1))
                        for c in range(4):
                            ins = pe.transpose(PS[2 + t % 2][:, c * P:(c + 1) * P], PR[:, t % 2, c * P:(c + 1) * P], IDENT[:, :])
                        ins.then_inc(pT_ps.sem, 1)

                    def values(i, t):
                        b, u = divmod(t, NS)
                        j, half = u % 4, u // 4
                        pe.wait_ge(pT_sb.sem, pT_sb.at(i, t + 1))
                        if t == 0:
                            pe.wait_ge(v_sb.sem, v_sb.at(i, GROUP))
                        if u == 0 and b >= 2:
                            pe.wait_ge(o_tok.sem, o_tok.at(i, b - 1))
                        for c in range(4):
                            h = 4 * (4 * half + c) + j
                            ins = pe.matmul(PS[4 + b % 2][:, h * V:(h + 1) * V], PTS[:, t % 2, c * P:(c + 1) * P],
                                            vs[:, b, h, :], start=True, stop=True)
                        ins.then_inc(av_ps.sem, 1)

                    def turn_out(i, b):
                        pe.wait_ge(o_tok.sem, o_tok.at(i, b + 1))
                        if b:
                            pe.wait_ge(oT_sb.sem, oT_sb.at(i, b))
                            if kind == "causal":
                                pe.wait_ge(qT_sb.sem, qT_sb.at(i, b))
                        for c in range(KD):
                            ins = pe.transpose(PS[6][:, c * P:(c + 1) * P], OTOK[:, c * P:(c + 1) * P], IDENT[:, :])
                        ins.then_inc(oT_ps.sem, 1)

                    def project_out(i, b):
                        pe.wait_ge(oT_sb.sem, oT_sb.at(i, b + 1))
                        if b:
                            pe.wait_ge(x_done.sem, x_done.at(i, b))
                        if kind == "causal":
                            for m in range(KD):
                                for c in range(KD):
                                    ins = pe.matmul(PS[7][:, m * P:(m + 1) * P], wo[:, c, m * P:(m + 1) * P], OT[:, c, :],
                                                    start=(c == 0), stop=(c == KD - 1))
                            ins.then_inc(out_ps.sem, 1)
                            return
                        for c in range(KD):
                            pe.matmul(PS[7][:, 0:DIM], OT[:, c, :], wo[:, c, :], start=(c == 0), stop=False)
                        pe.matmul(PS[7][:, 0:DIM], ONES[0:1, :], w(s, "bo")[0:1, :], start=False,
                                  stop=True).then_inc(out_ps.sem, 1)

                    def modulation(i, b):
                        a = wk(s, "a", KD)
                        pe.wait_ge(x_done.sem, x_done.at(i, b + 1))
                        for c in range(KD):
                            ins = pe.matmul(PS[6][0:16, 256:256 + TOK], a[:, c, :], VS[:, 2048 + c * P:2048 + (c + 1) * P],
                                            start=(c == 0), stop=(c == KD - 1))
                        ins.then_inc(q_ps.sem, 1)

                    with pe.Fori(0, TURNS) as i:
                        project(i, 0)
                        for b in range(GROUP):
                            turn_heads(i, b)
                            if b + 1 < GROUP:
                                project(i, b + 1)
                        for t in range(END):
                            if t < N:
                                scores(i, t)
                            if 0 <= t - 2 < N:
                                turn_probs(i, t - 2)
                            if 0 <= t - 3 < N:
                                values(i, t - 3)
                            b, late = divmod(t - 5 - (NS - 1), NS)
                            if late == 0 and 0 <= b < GROUP:
                                turn_out(i, b)
                            b, late = divmod(t - 6 - (NS - 1), NS)
                            if late == 0 and 0 <= b < GROUP:
                                project_out(i, b)
                                if kind == "causal":
                                    modulation(i, b)

                @block.vector
                def _(dve):
                    def rope(ch, i, b, part, dst):
                        src = PS[6][:, part * DIM:(part + 1) * DIM].rearrange("p (h f e) -> p h f e", h=NH, e=2)
                        sin = STAT[:, 128:132].unsqueeze(1).broadcast_to([P, NH, 4])
                        cos = STAT[:, 132:136].unsqueeze(1).broadcast_to([P, NH, 4])
                        d = dst[:, :, 0:HD].rearrange("p h (f e) -> p h f e", e=2)
                        m = T1[:, part * 512:part * 512 + 512].rearrange("p (a h f) -> p a h f", a=4, f=4)
                        ch.step(dve.tensor_tensor(m[:, 0], src[:, :, :, 0], cos, ALU.mult))
                        ch.step(dve.tensor_tensor(m[:, 1], src[:, :, :, 1], sin, ALU.mult))
                        ch.step(dve.tensor_tensor(m[:, 2], src[:, :, :, 0], sin, ALU.mult))
                        ch.step(dve.tensor_tensor(m[:, 3], src[:, :, :, 1], cos, ALU.mult))
                        ch.settle()
                        ch.step(dve.tensor_tensor(d[:, :, :, 0], m[:, 0], m[:, 1], ALU.subtract))
                        ch.step(dve.tensor_tensor(d[:, :, :, 1], m[:, 2], m[:, 3], ALU.add))

                    def head_norm(ch, i, b, part, dst):
                        src = PS[6][:, part * DIM:(part + 1) * DIM].rearrange("p (h e) -> p h e", h=NH)
                        cen = T1[:, part * 512:part * 512 + DIM].rearrange("p (h e) -> p h e", h=NH)
                        sq = T1[:, part * 512 + DIM:part * 512 + 512].rearrange("p (h e) -> p h e", h=NH)
                        mean = hsum[:, part, :]
                        ch.link(dve.tensor_reduce(mean, src, AX, ALU.add))
                        ch.link(dve.tensor_scalar(mean, mean, 1.0 / HD, None, ALU.mult))
                        ch.link(dve.tensor_tensor(cen, src, mean.unsqueeze(2).broadcast_to([P, NH, HD]), ALU.subtract))
                        ch.link(dve.tensor_tensor(sq, cen, cen, ALU.mult))
                        ch.link(dve.tensor_reduce(mean, sq, AX, ALU.add))
                        dve.tensor_scalar(hvar[:, part, :], mean, 1.0 / HD, 1e-6, ALU.mult, ALU.add).then_inc(rstd_in.sem, 1)

                    def head_scale(ch, i, b, part, dst):
                        cen = T1[:, part * 512:part * 512 + DIM].rearrange("p (h e) -> p h e", h=NH)
                        dve.wait_ge(rstd_out.sem, rstd_out.at(i, 2 * b + part + 1))
                        ch.step(dve.tensor_tensor(dst[:, :, 0:HD], cen, hrstd[:, part, :].unsqueeze(2).broadcast_to([P, NH, HD]),
                                                  ALU.mult))

                    def heads(ch, i, b):
                        dve.wait_ge(qk_ps.sem, qk_ps.at(i, b + 1))
                        if b:
                            dve.wait_ge(qkT_ps.sem, qkT_ps.at(i, 2 * b))
                        if kind == "rope":
                            ch.link(dve.tensor_copy(STAT[:, 128:136].rearrange("p (c f) -> p c f", c=2),
                                                    SINCOS[:, :, bass.ds(i * GROUP + b, 1), :].rearrange("p c b f -> p c (b f)")))
                            rope(ch, i, b, 0, qp)
                            rope(ch, i, b, 1, kp)
                        elif kind == "causal":
                            for part, dst in enumerate((qp, kp)):
                                src = PS[6][:, part * DIM:(part + 1) * DIM].rearrange("p (h e) -> p h e", h=NH)
                                ch.step(dve.tensor_copy(dst[:, :, 0:HD], src))
                        else:
                            for part, dst in enumerate((qp, kp)):
                                head_norm(ch, i, b, part, dst)
                            for part, dst in enumerate((qp, kp)):
                                head_scale(ch, i, b, part, dst)
                        ch.settle()
                        dve.sem_inc(qk_pad.sem, 1)

                    def subtract_max(ch, i, t):
                        S = PS[t % 2][:, :].rearrange("p (h c) -> p h c", h=4)
                        pr = PR[:, t % 2, :].rearrange("p (h c) -> p h c", h=4)
                        dve.wait_ge(s_ps.sem, s_ps.at(i, t + 1))
                        for (lo, hi), nm in zip(segs, (nmax, nmax2)):
                            ch.step(dve.tensor_reduce(nm[:, t % 2, :], S[:, :, lo:hi], AX, ALU.max, negate=True))
                        ch.settle()
                        if t >= 2:
                            dve.wait_ge(pT_ps.sem, pT_ps.at(i, t - 1))
                        for n, ((lo, hi), nm) in enumerate(zip(segs, (nmax, nmax2))):
                            ins = dve.tensor_tensor(pr[:, :, lo:hi], S[:, :, lo:hi],
                                                    nm[:, t % 2, :].unsqueeze(2).broadcast_to([P, 4, hi - lo]), ALU.add)
                            if n < len(segs) - 1:
                                ch.step(ins)
                        ins.then_inc(s_sub.sem, 1)

                    def normalise(ch, i, t):
                        pr = PR[:, t % 2, :].rearrange("p (h c) -> p h c", h=4)
                        psum_ = psums[:, t % 2, :]
                        dve.wait_ge(p_exp.sem, p_exp.at(i, t + 1))
                        for n, (lo, hi) in enumerate(segs):
                            ch.step(dve.tensor_reduce(psum_[:, 4 * n:4 * n + 4], pr[:, :, lo:hi], AX, ALU.add))
                        ch.settle()
                        ch.link(dve.reciprocal(psum_, psum_))
                        for n, (lo, hi) in enumerate(segs):
                            ins = dve.tensor_tensor(pr[:, :, lo:hi], pr[:, :, lo:hi],
                                                    psum_[:, 4 * n:4 * n + 4].unsqueeze(2).broadcast_to([P, 4, hi - lo]), ALU.mult)
                            if n < len(segs) - 1:
                                ch.step(ins)
                        ins.then_inc(p_norm.sem, 1)

                    def attended(ch, i, b):
                        O = PS[4 + b % 2][:, 0:NH * V].rearrange("p (h v) -> p h v", v=V)
                        dve.wait_ge(av_ps.sem, av_ps.at(i, (b + 1) * NS))
                        if not seg:
                            ch.link(dve.reciprocal(rsum, O[:, :, HD]))
                        if b:
                            dve.wait_ge(oT_ps.sem, oT_ps.at(i, b))
                        dst = OTOK[:, :].rearrange("p (h e) -> p h e", e=HD)
                        if seg:
                            dve.tensor_copy(dst, O[:, :, 0:HD]).then_inc(o_tok.sem, 1)
                        else:
                            dve.tensor_tensor(dst, O[:, :, 0:HD], rsum.unsqueeze(2).broadcast_to([P, NH, HD]),
                                              ALU.mult).then_inc(o_tok.sem, 1)

                    def add_out(ch, i, b):
                        dve.wait_ge(out_ps.sem, out_ps.at(i, b + 1))
                        if kind == "causal":
                            dve.wait_ge(q_ps.sem, q_ps.at(i, b))
                            dve.tensor_copy(VS[:, 2048:2048 + KD * P], PS[7][:, 0:KD * P]).then_inc(x_done.sem, 1)
                            return
                        xb = X[:, bass.ds(i * GROUP + b, 1), :].rearrange("p a d -> p (a d)")
                        dve.scalar_tensor_tensor(out=xb, in0=PS[7][:, 0:DIM], scalar=TG[:, tg:tg + 1], in1=xb,
                                                 op0=ALU.mult, op1=ALU.add).then_inc(x_done.sem, 1)

                    if kind == "causal":
                        dve.wait_ge(w_loaded[s].sem, 32)
                        gained_parts = (("wq", "ln1"), ("wk", "ln1"), ("wv", "ln1"), ("gate", "ln2"), ("up", "ln2"), ("a2", "ln2"))
                        for name, gain in gained_parts:
                            for c in range(KD):
                                part = wk(s, name, KD)[:, c, :]
                                ins = dve.tensor_scalar(part, part, w(s, gain)[:, c:c + 1], None, ALU.mult)
                        ins.then_inc(gained.sem, 1)
                    with dve.Fori(0, TURNS) as i:
                        ch = Chain(dve, dve_step, i)
                        for b in range(GROUP):
                            heads(ch, i, b)
                        for t in range(END):
                            if t < N:
                                subtract_max(ch, i, t)
                            if seg and 0 <= t - 1 < N:
                                normalise(ch, i, t - 1)
                            b, late = divmod(t - 4 - (NS - 1), NS)
                            if late == 0 and 0 <= b < GROUP:
                                attended(ch, i, b)
                            b, late = divmod(t - 6 - (NS - 1), NS)
                            if late == 0 and 0 <= b < GROUP:
                                add_out(ch, i, b)
                        ch.close()

                @block.scalar
                def _(act):
                    norms = w(s, "norms") if seg else None
                    if seg:
                        act.wait_ge(w_loaded[s].sem, 32)
                    else:
                        act.wait_ge(pool_step.sem, pool_step.at(0, 1))

                    def heads(ch, i, b):
                        act.wait_ge(v_ps.sem, v_ps.at(i, b + 1))
                        act.copy(vs[:, b, :, 0:HD], PS[7][:, 0:DIM].rearrange("p (h e) -> p h e", e=HD)).then_inc(v_sb.sem, 1)
                        for part, (dst, bank) in enumerate(((qT, 2), (kT, 0))):
                            act.wait_ge(qkT_ps.sem, qkT_ps.at(i, 2 * b + part + 1))
                            if seg:
                                src = PS[bank][:, :].rearrange("p (n t) -> p n t", t=P)
                                cuts = ((0, TOK),) if part == 0 else segs
                                for c, (lo, hi) in enumerate(cuts):
                                    at = 2 * (part + c)
                                    ins = act.activation(dst[:, b, :, lo:hi], src[:, :, lo:hi], ACT.Identity,
                                                         bias=norms[:, at + 1:at + 2], scale=norms[:, at:at + 1])
                                    if c < len(cuts) - 1:
                                        ch.step(ins)
                            else:
                                for n in range(NB // 4):
                                    ins = act.copy(dst[:, b, 4 * n:4 * n + 4, :], PS[bank + n][:, :].rearrange("p (n t) -> p n t", t=P))
                                    if n < NB // 4 - 1:
                                        ch.step(ins)
                            ins.then_inc(qkT_sb.sem, 1)

                    def exponent(i, t):
                        act.wait_ge(s_sub.sem, s_sub.at(i, t + 1))
                        act.activation(PR[:, t % 2, :], PR[:, t % 2, :], ACT.Exp, scale=float(HD) ** -0.5).then_inc(p_exp.sem, 1)

                    def probs_out(i, t):
                        act.wait_ge(pT_ps.sem, pT_ps.at(i, t + 1))
                        if t >= 2:
                            act.wait_ge(av_ps.sem, av_ps.at(i, t - 1))
                        act.copy(PTS[:, t % 2, :], PS[2 + t % 2][:, :]).then_inc(pT_sb.sem, 1)

                    with act.Fori(0, TURNS) as i:
                        ch = Chain(act, act_step, i)
                        for b in range(GROUP):
                            heads(ch, i, b)
                        for t in range(END):
                            if t < N:
                                exponent(i, t)
                            if 0 <= t - 2 < N:
                                probs_out(i, t - 2)
                            b, late = divmod(t - 5 - (NS - 1), NS)
                            if late == 0 and 0 <= b < GROUP:
                                act.wait_ge(oT_ps.sem, oT_ps.at(i, b + 1))
                                if b:
                                    act.wait_ge(out_ps.sem, out_ps.at(i, b))
                                act.copy(OT[:, :, :], PS[6][:, 0:DIM].rearrange("p (c t) -> p c t", c=KD)).then_inc(oT_sb.sem, 1)
                            b, late = divmod(t - 7 - (NS - 1), NS)
                            if kind == "causal" and late == 0 and 0 <= b < GROUP:
                                act.wait_ge(q_ps.sem, q_ps.at(i, b + 1))
                                act.activation(MODT[:, bass.ds(i * GT + b * TOK, TOK)], PS[6][0:16, 256:256 + TOK],
                                               ACT.Tanh).then_inc(qT_sb.sem, 1)
                        ch.close()

        def big_attention(s, tg, kind, prefetch=None):
            rms = kind == "rms"
            W = 2 if rms else GROUP
            turns = BATCH // W
            WT = W * TOK
            N = 4 * W
            NKV = N if rms else 16
            NR = 2 * N if rms else 0
            lag = 2 if rms else 1
            END = N + lag + 6
            begin(turns, dve_step=STEPS, act_step=STEPS, copied=1, ctx_loaded=16, v_ps=NKV, v_sb=NKV,
                  q_ps=NR if rms else N, sq_done=NR, rstd_in=NR, rstd_out=NR, qk_pad=NR, qkT_ps=NR,
                  qT_sb=NR if rms else N, s_ps=N, s_sub=N, p_exp=N, p_norm=N, pT_ps=N, pT_sb=N, av_ps=N, oT_sb=N,
                  out_ps=N, x_done=W)
            if not rms:
                begin(1, pool_step=0, gained=1)
            wq, wo = wk(s, "wq", KD), wk(s, "wo", 16)
            QN, SQ, QTS, OTS = (QT[:, n * 1024:(n + 1) * 1024].rearrange("p (a n) -> p a n", a=2) for n in range(4))
            kT = KT[:, :].rearrange("p (b h t) -> p b h t", b=W, t=TOK) if rms else KT[:, :].rearrange("p (h b t) -> p b h t", b=W, t=TOK)
            vs = VS[:, :].rearrange("p (b n) -> p b n", b=W)
            nmax = STAT[:, 0:8].rearrange("p (a h) -> p a h", a=2)
            psums = STAT[:, 16:24].rearrange("p (a h) -> p a h", a=2)
            qvar = STAT[:, 32:40].rearrange("p (a h) -> p a h", a=2)
            qrstd = STAT[:, 48:56].rearrange("p (a h) -> p a h", a=2)
            qsum = STAT[:, 64:68]
            mcol = STAT[:, 240:240 + GROUP]
            mraw = QP[0:1, 0:512].bitcast(U8)
            mrow = KP[0:1, :].bitcast(BF16)
            mgroup = QP[0:1, 512:768].bitcast(BF16)
            item_bank = lambda m: 6 if m >= N else (6, 4)[m % 2]
            itemT_bank = lambda m: 7 if m >= N else (7, 5)[m % 2]

            with nc.Block() as block:
                @block.sync
                def _(sp):
                    if not rms:
                        sp.dma_start(mraw, mrow_in).then_inc(mask_loaded.sem, 16)
                    if prefetch is not None:
                        load_weights(sp, prefetch)
                    with sp.Fori(0, turns) as i:
                        sp.wait_ge(v_ps.sem, v_ps.at(i, 0))
                        sp.dma_start(CS[:, 0, 0:WT].rearrange("p (b t) -> p b t", t=TOK),
                                     ctxT_in[:, bass.ds(i * W, W), :]).then_inc(ctx_loaded.sem, 16)

                @block.gpsimd
                def _(pool):
                    if not rms:
                        pool.wait_ge(gained.sem, gained.at(0, 1))
                    with pool.Fori(0, turns) as i:
                        pool.wait_ge(q_ps.sem, q_ps.at(i, 0))
                        if not rms:
                            pool.wait_ge(s_ps.sem, s_ps.at(i, 0))
                            pool.tensor_copy(mgroup, mrow[:, bass.ds(i * WT, WT)])
                            pool.tensor_copy(mcol, MCOL[:, bass.ds(i * W, W)])
                        pool.tensor_copy(XS[:, :, 0:WT], XNT[:, :, bass.ds(i * WT, WT)]).then_inc(copied.sem, 1)
                        for m in range(NR):
                            pool.wait_ge(rstd_in.sem, rstd_in.at(i, m + 1))
                            pool.tensor_tensor(qrstd[:, m % 2, :], qvar[:, m % 2, :], MHALF[:, 0:4],
                                               ALU.pow).then_inc(rstd_out.sem, 1)

                @block.tensor
                def _(pe):
                    pe.wait_ge(w_loaded[s].sem, 32)

                    def keys_values(i, n):
                        if n >= 4:
                            pe.wait_ge(v_sb.sem, v_sb.at(i, n - 3))
                        if n < 8:
                            ins = pe.matmul(PS[n % 4][:, :], w(s, "wk")[:, n * P:(n + 1) * P], CS[:, 0, :], start=True, stop=True)
                        else:
                            b, half = divmod(n - 8, 2)
                            ins = pe.matmul(PS[n % 4][:, :], CS[:, 0, b * TOK:(b + 1) * TOK],
                                            w(s, "wv")[:, half * 512:(half + 1) * 512], start=True, stop=True)
                        ins.then_inc(v_ps.sem, 1)

                    def values_of(i, n):
                        b, part = divmod(n, 4)
                        if n >= 4:
                            pe.wait_ge(v_sb.sem, v_sb.at(i, n - 3))
                        pe.matmul(PS[n % 4][:, :], CS[:, 0, b * TOK:(b + 1) * TOK], w(s, "wv")[:, part * 512:(part + 1) * 512],
                                  start=True, stop=True).then_inc(v_ps.sem, 1)

                    def item(i, m):
                        b, part = divmod(m % N, 4)
                        tok, cols = slice(b * TOK, (b + 1) * TOK), slice(part * 512, (part + 1) * 512)
                        back = 1 if m > N else 2
                        if m >= back:
                            pe.wait_ge(qk_pad.sem, qk_pad.at(i, m - back + 1))
                        bank = PS[item_bank(m)]
                        if m < N:
                            ins = pe.matmul(bank[:, :], CS[:, 0, tok], w(s, "wk")[:, cols], start=True, stop=True)
                        else:
                            for c in range(KD):
                                ins = pe.matmul(bank[:, :], XS[:, c, tok], wq[:, c, cols], start=(c == 0), stop=(c == KD - 1))
                        ins.then_inc(q_ps.sem, 1)

                    def turn_item(i, m):
                        pe.wait_ge(qk_pad.sem, qk_pad.at(i, m + 1))
                        back = 1 if m > N else 2
                        if m >= back:
                            pe.wait_ge(qT_sb.sem, qT_sb.at(i, m - back + 1))
                        for c in range(4):
                            ins = pe.transpose(PS[itemT_bank(m)][:, c * P:(c + 1) * P], QN[:, m % 2, c * P:(c + 1) * P], IDENT[:, :])
                        ins.then_inc(qkT_ps.sem, 1)

                    def queries(i, t):
                        b, part = divmod(t, 4)
                        if t >= 2:
                            pe.wait_ge(qT_sb.sem, qT_sb.at(i, t - 1))
                        for c in range(4):
                            h = 4 * part + c
                            for k in range(KD):
                                ins = pe.matmul(PS[6 + t % 2][:, c * P:(c + 1) * P], wq[:, k, h * P:(h + 1) * P],
                                                XS[:, k, b * TOK:(b + 1) * TOK], start=(k == 0), stop=(k == KD - 1))
                        ins.then_inc(q_ps.sem, 1)

                    def scores(i, t):
                        b, part = divmod(t, 4)
                        pe.wait_ge(qT_sb.sem, qT_sb.at(i, NR - N + t + 1 if rms else t + 1))
                        if t == 0:
                            pe.wait_ge(v_sb.sem, v_sb.at(i, NKV))
                        if t >= 2:
                            pe.wait_ge(s_sub.sem, s_sub.at(i, t - 1))
                        if not rms:
                            mask = mgroup[0:1, b * TOK:(b + 1) * TOK]
                            pe.matmul(PS[t % 2][:, :].rearrange("p (h c) -> p h c", h=4), ONESB[0:1, :],
                                      mask.unsqueeze(1).broadcast_to([1, 4, TOK]), start=True, stop=False,
                                      skip_group_check=True)
                        for c in range(4):
                            h = 4 * part + c
                            ins = pe.matmul(PS[t % 2][:, c * P:(c + 1) * P], QTS[:, t % 2, c * P:(c + 1) * P],
                                            kT[:, b, h if rms else h // 2, :], start=rms, stop=True, skip_group_check=True)
                        ins.then_inc(s_ps.sem, 1)

                    def turn_probs(i, t):
                        pe.wait_ge(p_norm.sem, p_norm.at(i, t + 1))
                        if t >= 2:
                            pe.wait_ge(pT_sb.sem, pT_sb.at(i, t - 1))
                        for c in range(4):
                            ins = pe.transpose(PS[2 + t % 2][:, c * P:(c + 1) * P], PR[:, t % 2, c * P:(c + 1) * P], IDENT[:, :])
                        ins.then_inc(pT_ps.sem, 1)

                    def values(i, t):
                        b, part = divmod(t, 4)
                        pe.wait_ge(pT_sb.sem, pT_sb.at(i, t + 1))
                        if t:
                            pe.wait_ge(oT_sb.sem, oT_sb.at(i, t))
                        n = 4 if rms else 2
                        for c in range(n):
                            cols = slice(c * 512 // n, (c + 1) * 512 // n)
                            g = n * part + c
                            ins = pe.matmul(PS[4][:, cols], vs[:, b, g * P:(g + 1) * P], PTS[:, t % 2, cols], start=True, stop=True)
                        ins.then_inc(av_ps.sem, 1)

                    def project_out(i, t):
                        b, part = divmod(t, 4)
                        pe.wait_ge(oT_sb.sem, oT_sb.at(i, t + 1))
                        if part == 0:
                            pe.wait_ge(x_done.sem, x_done.at(i, b))
                        for c in range(4):
                            ins = pe.matmul(PS[5][:, 0:DIM], OTS[:, t % 2, c * P:(c + 1) * P], wo[:, 4 * part + c, :],
                                            start=(part == 0 and c == 0), stop=(part == 3 and c == 3))
                        ins.then_inc(out_ps.sem, 1)

                    with pe.Fori(0, turns) as i:
                        pe.wait_ge(copied.sem, copied.at(i, 1))
                        pe.wait_ge(ctx_loaded.sem, ctx_loaded.at(i, 16))
                        pe.wait_ge(x_done.sem, x_done.at(i, 0))
                        if rms:
                            for m in range(N + 2):
                                if m < N:
                                    item(i, m)
                                    values_of(i, m)
                                if m == N:
                                    item(i, m)
                                if 1 <= m <= N:
                                    turn_item(i, m - 1)
                        else:
                            for n in range(NKV):
                                keys_values(i, n)
                        for t in range(END):
                            if rms:
                                if 1 <= t < N:
                                    item(i, N + t)
                                if t < N:
                                    pass
                                if 0 <= t - 1 < N:
                                    turn_item(i, N + t - 1)
                            elif t < N:
                                queries(i, t)
                            if 0 <= t - lag < N:
                                scores(i, t - lag)
                            if 0 <= t - lag - 2 < N:
                                turn_probs(i, t - lag - 2)
                            if 0 <= t - lag - 3 < N:
                                values(i, t - lag - 3)
                            if 0 <= t - lag - 4 < N:
                                project_out(i, t - lag - 4)

                @block.vector
                def _(dve):
                    if not rms:
                        dve.wait_ge(mask_loaded.sem, 16)
                        dve.tensor_scalar(mrow, mraw, 1.0, BIG, ALU.subtract, ALU.mult).then_inc(gained.sem, 1)

                    def norm_item(ch, i, m):
                        dve.wait_ge(sq_done.sem, sq_done.at(i, m + 1))
                        ch.link(dve.tensor_reduce(qsum, SQ[:, m % 2, :].rearrange("p (h c) -> p h c", h=4), AX, ALU.add))
                        dve.tensor_scalar(qvar[:, m % 2, :], qsum, 1.0 / P, 1e-5, ALU.mult, ALU.add).then_inc(rstd_in.sem, 1)

                    def scale_item(ch, i, m):
                        dve.wait_ge(rstd_out.sem, rstd_out.at(i, m + 1))
                        if m >= 2:
                            dve.wait_ge(qkT_ps.sem, qkT_ps.at(i, m - 1))
                        src = PS[item_bank(m)][:, :].rearrange("p (h c) -> p h c", h=4)
                        dve.tensor_tensor(QN[:, m % 2, :].rearrange("p (h c) -> p h c", h=4), src,
                                          qrstd[:, m % 2, :].unsqueeze(2).broadcast_to([P, 4, P]), ALU.mult).then_inc(qk_pad.sem, 1)

                    def subtract_max(ch, i, t):
                        S = PS[t % 2][:, :].rearrange("p (h c) -> p h c", h=4)
                        dve.wait_ge(s_ps.sem, s_ps.at(i, t + 1))
                        ch.link(dve.tensor_reduce(nmax[:, t % 2, :], S, AX, ALU.max, negate=True))
                        if t >= 2:
                            dve.wait_ge(pT_ps.sem, pT_ps.at(i, t - 1))
                        dve.tensor_tensor(PR[:, t % 2, :].rearrange("p (h c) -> p h c", h=4), S,
                                          nmax[:, t % 2, :].unsqueeze(2).broadcast_to([P, 4, P]), ALU.add).then_inc(s_sub.sem, 1)

                    def normalise(ch, i, t):
                        pr = PR[:, t % 2, :].rearrange("p (h c) -> p h c", h=4)
                        psum_ = psums[:, t % 2, :]
                        dve.wait_ge(p_exp.sem, p_exp.at(i, t + 1))
                        ch.link(dve.tensor_reduce(psum_, pr, AX, ALU.add))
                        ch.link(dve.reciprocal(psum_, psum_))
                        dve.tensor_tensor(pr, pr, psum_.unsqueeze(2).broadcast_to([P, 4, P]), ALU.mult).then_inc(p_norm.sem, 1)

                    with dve.Fori(0, turns) as i:
                        ch = Chain(dve, dve_step, i)
                        if rms:
                            for m in range(N):
                                norm_item(ch, i, m)
                                scale_item(ch, i, m)
                        for t in range(END):
                            if rms and t < N:
                                norm_item(ch, i, N + t)
                            if 0 <= t - lag < N:
                                subtract_max(ch, i, t - lag)
                            if rms and t < N:
                                scale_item(ch, i, N + t)
                            if 0 <= t - lag - 1 < N:
                                normalise(ch, i, t - lag - 1)
                            b, late = divmod(t - lag - 5 - 3, 4)
                            if late == 0 and 0 <= b < W:
                                dve.wait_ge(out_ps.sem, out_ps.at(i, 4 * b + 4))
                                xb = X[:, bass.ds(i * W + b, 1), :].rearrange("p a d -> p (a d)")
                                dve.scalar_tensor_tensor(out=xb, in0=PS[5][:, 0:DIM], scalar=TG[:, tg:tg + 1], in1=xb,
                                                         op0=ALU.mult, op1=ALU.add).then_inc(x_done.sem, 1)
                        ch.close()

                @block.scalar
                def _(act):
                    if rms:
                        act.wait_ge(w_loaded[s].sem, 32)

                    def square_item(i, m):
                        act.wait_ge(q_ps.sem, q_ps.at(i, m + 1))
                        if m >= 2:
                            act.wait_ge(rstd_in.sem, rstd_in.at(i, m - 1))
                        act.activation(SQ[:, m % 2, :], PS[item_bank(m)][:, :], ACT.Square).then_inc(sq_done.sem, 1)

                    def item_out(i, m):
                        act.wait_ge(qkT_ps.sem, qkT_ps.at(i, m + 1))
                        src = PS[itemT_bank(m)][:, :]
                        if m < N:
                            b, part = divmod(m, 4)
                            dst = kT[:, b, 4 * part:4 * part + 4, :]
                            src = src.rearrange("p (h t) -> p h t", h=4)
                        else:
                            if m >= N + 2:
                                act.wait_ge(s_ps.sem, s_ps.at(i, m - N - 1))
                            dst = QTS[:, m % 2, :]
                        act.activation(dst, src, ACT.Copy, scale=w(s, "gk" if m < N else "gq")).then_inc(qT_sb.sem, 1)

                    def keys_values_out(i, n):
                        act.wait_ge(v_ps.sem, v_ps.at(i, n + 1))
                        if rms:
                            b, part = divmod(n, 4)
                            act.copy(vs[:, b, part * 512:(part + 1) * 512], PS[n % 4][:, :]).then_inc(v_sb.sem, 1)
                        elif n < 8:
                            act.copy(kT[:, :, n, :], PS[n % 4][:, :].rearrange("p (b t) -> p b t", b=W)).then_inc(v_sb.sem, 1)
                        else:
                            b, half = divmod(n - 8, 2)
                            act.activation(vs[:, b, half * 512:(half + 1) * 512], PS[n % 4][:, :], ACT.Copy,
                                           scale=mcol[:, b:b + 1]).then_inc(v_sb.sem, 1)

                    def queries_out(i, t):
                        act.wait_ge(q_ps.sem, q_ps.at(i, t + 1))
                        if t >= 2:
                            act.wait_ge(s_ps.sem, s_ps.at(i, t - 1))
                        act.copy(QTS[:, t % 2, :], PS[6 + t % 2][:, :]).then_inc(qT_sb.sem, 1)

                    def exponent(i, t):
                        act.wait_ge(s_sub.sem, s_sub.at(i, t + 1))
                        act.activation(PR[:, t % 2, :], PR[:, t % 2, :], ACT.Exp, scale=float(P) ** -0.5).then_inc(p_exp.sem, 1)

                    def probs_out(i, t):
                        act.wait_ge(pT_ps.sem, pT_ps.at(i, t + 1))
                        if t >= 2:
                            act.wait_ge(av_ps.sem, av_ps.at(i, t - 1))
                        act.copy(PTS[:, t % 2, :], PS[2 + t % 2][:, :]).then_inc(pT_sb.sem, 1)

                    def attended(i, t):
                        act.wait_ge(av_ps.sem, av_ps.at(i, t + 1))
                        if t >= 2:
                            act.wait_ge(out_ps.sem, out_ps.at(i, t - 1))
                        act.copy(OTS[:, t % 2, :], PS[4][:, :]).then_inc(oT_sb.sem, 1)

                    with act.Fori(0, turns) as i:
                        if rms:
                            for m in range(N + 1):
                                if m < N:
                                    square_item(i, m)
                                    keys_values_out(i, m)
                                if m >= 1:
                                    item_out(i, m - 1)
                        else:
                            for n in range(NKV):
                                keys_values_out(i, n)
                        for t in range(END):
                            if rms and t < N:
                                square_item(i, N + t)
                            if not rms and t < N:
                                queries_out(i, t)
                            if 0 <= t - lag < N:
                                exponent(i, t - lag)
                            if rms and 0 <= t - 1 < N:
                                item_out(i, N + t - 1)
                            if 0 <= t - lag - 2 < N:
                                probs_out(i, t - lag - 2)
                            if 0 <= t - lag - 3 < N:
                                attended(i, t - lag - 3)
                        act.sem_inc(act_step.sem, STEPS)

        def ffn_block(s, kind, ne, nf, tg=None, first_expert=0, prefetch=None):
            N = ne * nf
            mod = kind == "mod"
            begin(TURNS, dve_step=STEPS, gu_ps=N, silu_done=N, h_done=N, down_ps=N, x_done=ne, q_ps=mod, qk_pad=mod)
            gate, up, down = wk(s, "gate", ne * KD), wk(s, "up", ne * KD), wk(s, "down", N)
            mh = QP[0:16, 0:512]
            with nc.Block() as block:
                if prefetch is not None:
                    @block.sync
                    def _(sp):
                        load_weights(sp, prefetch)

                @block.tensor
                def _(pe):
                    pe.wait_ge(w_loaded[s].sem, 32)

                    def gate_up(i, n):
                        e, f = divmod(n, nf)
                        if n >= 2:
                            pe.wait_ge(h_done.sem, h_done.at(i, n - 1))
                        cols = slice(f * P, (f + 1) * P)
                        for k in range(KD):
                            pe.matmul(PS[n % 2][:, :], gate[:, e * KD + k, cols], XNT[:, k, bass.ds(i * GT, GT)],
                                      start=(k == 0), stop=(k == KD - 1 and not mod))
                        if mod:
                            pe.matmul(PS[n % 2][:, :], w(s, "bm")[0:16, cols], mh, start=False, stop=True)
                        for k in range(KD):
                            ins = pe.matmul(PS[2 + n % 2][:, :], up[:, e * KD + k, cols], XNT[:, k, bass.ds(i * GT, GT)],
                                            start=(k == 0), stop=(k == KD - 1))
                        ins.then_inc(gu_ps.sem, 1)

                    def project_down(i, n):
                        e, f = divmod(n, nf)
                        pe.wait_ge(h_done.sem, h_done.at(i, n + 1))
                        if f == 0:
                            pe.wait_ge(x_done.sem, x_done.at(i, max(e - 1, 0)))
                        for b in range(GROUP):
                            bank = PS[4 + 2 * (e % 2) + b // 2]
                            ins = pe.matmul(bank[:, b % 2 * DIM:(b % 2 + 1) * DIM], PTS[:, n % 2, b * TOK:(b + 1) * TOK],
                                            down[:, n, :], start=(f == 0 and b % 2 == 0), stop=(f == nf - 1),
                                            skip_group_check=True)
                        ins.then_inc(down_ps.sem, 1)

                    with pe.Fori(0, TURNS) as i:
                        if mod:
                            for k in range(KD):
                                ins = pe.matmul(PS[6][0:16, :], wk(s, "a2", KD)[:, k, :], XNT[:, k, bass.ds(i * GT, GT)],
                                                start=(k == 0), stop=(k == KD - 1))
                            ins.then_inc(q_ps.sem, 1)
                            pe.wait_ge(qk_pad.sem, qk_pad.at(i, 1))
                        for n in range(N + 1):
                            if n < N:
                                gate_up(i, n)
                            if n:
                                project_down(i, n - 1)

                @block.scalar
                def _(act):
                    with act.Fori(0, TURNS) as i:
                        for n in range(N):
                            act.wait_ge(gu_ps.sem, gu_ps.at(i, n + 1))
                            if n >= 2:
                                act.wait_ge(h_done.sem, h_done.at(i, n - 1))
                            act.activation(PR[:, n % 2, :], PS[n % 2][:, :], ACT.Silu).then_inc(silu_done.sem, 1)

                @block.vector
                def _(dve):
                    def hidden(i, n):
                        dve.wait_ge(silu_done.sem, silu_done.at(i, n + 1))
                        if n >= 2:
                            dve.wait_ge(down_ps.sem, down_ps.at(i, n - 1))
                        dve.tensor_tensor(PTS[:, n % 2, :], PR[:, n % 2, :], PS[2 + n % 2][:, :], ALU.mult).then_inc(h_done.sem, 1)

                    def combine(ch, i, e):
                        dve.wait_ge(down_ps.sem, down_ps.at(i, (e + 1) * nf))
                        if e:
                            ch.settle()
                            dve.wait_ge(x_done.sem, x_done.at(i, e))
                        for b in range(GROUP):
                            xb = X[:, bass.ds(i * GROUP + b, 1), :].rearrange("p a d -> p (a d)")
                            bank = PS[4 + 2 * (e % 2) + b // 2]
                            if kind == "moe":
                                scale = rwg[:, b, first_expert + e:first_expert + e + 1]
                            else:
                                scale = TG[:, tg:tg + 1]
                            ins = dve.scalar_tensor_tensor(out=xb, in0=bank[:, b % 2 * DIM:(b % 2 + 1) * DIM], scalar=scale,
                                                           in1=xb, op0=ALU.mult, op1=ALU.add)
                            if b < GROUP - 1:
                                ch.step(ins)
                        ins.then_inc(x_done.sem, 1)

                    rwg = STAT[:, 0:GROUP * EXPERTS].rearrange("p (b e) -> p b e", e=EXPERTS)
                    with dve.Fori(0, TURNS) as i:
                        ch = Chain(dve, dve_step, i)
                        if kind == "moe":
                            dve.wait_ge(x_done.sem, x_done.at(i, 0))
                            ch.link(dve.tensor_copy(rwg, RW[:, bass.ds(i * GROUP, GROUP), :]))
                        if mod:
                            dve.wait_ge(q_ps.sem, q_ps.at(i, 1))
                            dve.scalar_tensor_tensor(out=mh, in0=PS[6][0:16, :], scalar=0.1, in1=MODT[:, bass.ds(i * GT, GT)],
                                                     op0=ALU.mult, op1=ALU.mult).then_inc(qk_pad.sem, 1)
                        for n in range(N):
                            hidden(i, n)
                            if n and n % nf == 0:
                                combine(ch, i, n // nf - 1)
                        combine(ch, i, ne - 1)
                        ch.close()

        def quant_block(s, tg, prefetch=None):
            begin(TURNS, dve_step=STEPS, act_step=STEPS, copied=1, gu_ps=GROUP, silu_done=GROUP, h_done=GROUP,
                  o_tok=GROUP, pT_ps=GROUP, pT_sb=GROUP, down_ps=GROUP, x_done=GROUP, rstd_in=1)
            begin(1, s_ps=1, s_sub=1, gained=1, p_exp=1)
            NCH = HID0P // P
            WB = QT[:, 0:WIDTH[s] // 2].bitcast(BF16)
            w1 = WB[:, 0:KD * HID0].rearrange("p (k n) -> p k n", k=KD)
            w3 = WB[:, KD * HID0:2 * KD * HID0].rearrange("p (k n) -> p k n", k=KD)
            w2 = WB[:, 2 * KD * HID0:].rearrange("p (k n) -> p k n", k=NCH)
            XQT = XNT[:, 0, :].bitcast(BF16).rearrange("p (k t) -> p k t", k=KD)
            XSB = XS[:, 0, :].bitcast(BF16).rearrange("p (k t) -> p k t", k=KD)
            SG = KT[:, 0:2 * HID0].rearrange("p (a n) -> p a n", a=2)
            H = VS[:, 0:HID0]
            Y = VS[:, 1024:1024 + HID0]
            HQ = KT[:, 2048:2048 + HID0P].bitcast(BF16).rearrange("p (a n) -> p a n", a=2)
            HT = KT[:, 3072:3072 + HID0P].bitcast(BF16).rearrange("p (a n) -> p a n", a=2)
            halves = ((0, 512), (512, HID0))
            wsum, wmean, wstep = STAT[:, 0:3], STAT[:, 4:7], STAT[:, 8:11]
            cg, cu = STAT[:, 16:16 + GROUP], STAT[:, 24:24 + GROUP]
            hmax, hinv, hout = STAT[:, 32:33], STAT[:, 34:35], STAT[:, 36:38]
            parts = (("w1", 0, KD * HID0), ("w3", KD * HID0, 2 * KD * HID0), ("w2", 2 * KD * HID0, WIDTH[s]))
            with nc.Block() as block:
                @block.sync
                def _(sp):
                    if prefetch is not None:
                        load_weights(sp, prefetch)

                @block.gpsimd
                def _(pool):
                    with pool.Fori(0, TURNS) as i:
                        pool.wait_ge(gu_ps.sem, gu_ps.at(i, 0))
                        pool.tensor_copy(XSB[:, :, :], XQT[:, :, bass.ds(i * GT, GT)]).then_inc(copied.sem, 1)

                @block.tensor
                def _(pe):
                    pe.wait_ge(s_ps.sem, s_ps.at(0, 1))
                    pe.matmul(PS[7][:, 0:3], ONES[:, :], wsum, start=True, stop=True).then_inc(s_sub.sem, 1)
                    pe.wait_ge(gained.sem, gained.at(0, 1))

                    def gate_up(i, b):
                        if b:
                            pe.wait_ge(h_done.sem, h_done.at(i, b))
                        tok = slice(b * TOK, (b + 1) * TOK)
                        for n, m in enumerate((w1, w3)):
                            for c, (lo, hi) in enumerate(halves):
                                for k in range(KD):
                                    ins = pe.matmul(PS[2 * n + c][:, 0:hi - lo], XSB[:, k, tok], m[:, k, lo:hi],
                                                    start=(k == 0), stop=(k == KD - 1))
                        ins.then_inc(gu_ps.sem, 1)

                    def turn_hidden(i, b):
                        pe.wait_ge(o_tok.sem, o_tok.at(i, b + 1))
                        pe.wait_ge(pT_sb.sem, pT_sb.at(i, b))
                        for c in range(NCH):
                            ins = pe.transpose(PSB[4][:, c * P:(c + 1) * P], HQ[:, b % 2, c * P:(c + 1) * P], IDENTB[:, :])
                        ins.then_inc(pT_ps.sem, 1)

                    def project_down(i, b):
                        pe.wait_ge(pT_sb.sem, pT_sb.at(i, b + 1))
                        pe.wait_ge(x_done.sem, x_done.at(i, b))
                        for c in range(NCH):
                            ins = pe.matmul(PS[5][:, 0:DIM], HT[:, b % 2, c * P:(c + 1) * P], w2[:, c, :],
                                            start=(c == 0), stop=(c == NCH - 1))
                        ins.then_inc(down_ps.sem, 1)

                    with pe.Fori(0, TURNS) as i:
                        pe.wait_ge(copied.sem, copied.at(i, 1))
                        gate_up(i, 0)
                        for b in range(GROUP):
                            if b + 1 < GROUP:
                                gate_up(i, b + 1)
                            turn_hidden(i, b)
                            project_down(i, b)

                @block.scalar
                def _(act):
                    with act.Fori(0, TURNS) as i:
                        act.wait_ge(rstd_in.sem, rstd_in.at(i, 1))
                        ch = Chain(act, act_step, i)

                        def hidden_out(b):
                            act.wait_ge(pT_ps.sem, pT_ps.at(i, b + 1))
                            act.copy(HT[:, b % 2, :], PSB[4][:, 0:HID0P]).then_inc(pT_sb.sem, 1)

                        for b in range(GROUP):
                            act.wait_ge(gu_ps.sem, gu_ps.at(i, b + 1))
                            for c, (lo, hi) in enumerate(halves):
                                ins = act.activation(SG[:, b % 2, lo:hi], PS[c][:, 0:hi - lo], ACT.Silu, scale=cg[:, b:b + 1])
                                if c == 0:
                                    ch.step(ins)
                            ins.then_inc(silu_done.sem, 1)
                            if b:
                                hidden_out(b - 1)
                        hidden_out(GROUP - 1)
                        ch.close()

                @block.vector
                def _(dve):
                    dve.wait_ge(w_loaded[s].sem, 32)
                    for n, (_, lo, hi) in enumerate(parts):
                        ins = dve.tensor_reduce(wsum[:, n:n + 1], WREG[s % 2][:, lo:hi], AX, ALU.add, apply_absolute_value=True)
                    ins.then_inc(s_ps.sem, 1)
                    dve.wait_ge(s_sub.sem, s_sub.at(0, 1))
                    ch = Chain(dve, p_exp)
                    dve.tensor_scalar(wmean, PS[7][:, 0:3], 1.0 / (HID0 * DIM), 1e-5, ALU.mult, ALU.max).then_inc(quant_step.sem, 1)
                    dve.wait_ge(quant_step.sem, 1)
                    dve.reciprocal(wstep, wmean).then_inc(quant_step.sem, 1)
                    dve.wait_ge(quant_step.sem, 2)
                    for n, (_, lo, hi) in enumerate(parts):
                        m = WREG[s % 2][:, lo:hi]
                        ins = dve.tensor_scalar(m, m, wstep[:, n:n + 1], MAGIC, ALU.mult, ALU.add)
                    ins.then_inc(quant_step.sem, 1)
                    dve.wait_ge(quant_step.sem, 3)
                    m = WREG[s % 2][:, 0:WIDTH[s]]
                    dve.tensor_scalar(m, m, MAGIC + 1.0, MAGIC - 1.0, ALU.min, ALU.max).then_inc(quant_step.sem, 1)
                    dve.memset(HQ[:, :, :], 0.0)
                    dve.wait_ge(quant_step.sem, 4)
                    dve.tensor_scalar(WB[:, :], m, MAGIC, None, ALU.subtract).then_inc(gained.sem, 1)

                    def hidden(ch, i, b):
                        dve.wait_ge(silu_done.sem, silu_done.at(i, b + 1))
                        for c, (lo, hi) in enumerate(halves):
                            ins = dve.scalar_tensor_tensor(out=H[:, lo:hi], in0=PS[2 + c][:, 0:hi - lo], scalar=cu[:, b:b + 1],
                                                           in1=SG[:, b % 2, lo:hi], op0=ALU.mult, op1=ALU.mult)
                            if c == 0:
                                ch.step(ins)
                        ins.then_inc(h_done.sem, 1)
                        ch.settle()
                        dve.wait_ge(h_done.sem, h_done.at(i, b + 1))
                        ch.link(dve.tensor_reduce(hmax, H, AX, ALU.max, apply_absolute_value=True))
                        ch.link(dve.tensor_scalar(hmax, hmax, 1e-5, None, ALU.max))
                        ch.step(dve.reciprocal(hinv, hmax))
                        ch.step(dve.tensor_scalar(hout[:, b % 2:b % 2 + 1], hmax, 1.0 / 127.0, wmean[:, 2:3], ALU.mult, ALU.mult))
                        ch.settle()
                        ch.step(dve.tensor_scalar(hinv, hinv, 127.0, None, ALU.mult))
                        ch.step(dve.tensor_scalar(hout[:, b % 2:b % 2 + 1], hout[:, b % 2:b % 2 + 1], TG[:, tg:tg + 1], None, ALU.mult))
                        ch.settle()
                        ch.link(dve.tensor_scalar(Y, H, hinv, MAGIC, ALU.mult, ALU.add))
                        ch.link(dve.tensor_scalar(Y, Y, MAGIC + 127.0, MAGIC - 128.0, ALU.min, ALU.max))
                        if b >= 2:
                            dve.wait_ge(pT_ps.sem, pT_ps.at(i, b - 1))
                        dve.tensor_scalar(HQ[:, b % 2, 0:HID0], Y, MAGIC, None, ALU.subtract).then_inc(o_tok.sem, 1)

                    def add_out(i, b):
                        dve.wait_ge(down_ps.sem, down_ps.at(i, b + 1))
                        xb = X[:, bass.ds(i * GROUP + b, 1), :].rearrange("p a d -> p (a d)")
                        dve.scalar_tensor_tensor(out=xb, in0=PS[5][:, 0:DIM], scalar=hout[:, b % 2:b % 2 + 1], in1=xb,
                                                 op0=ALU.mult, op1=ALU.add).then_inc(x_done.sem, 1)

                    with dve.Fori(0, TURNS) as i:
                        ch = Chain(dve, dve_step, i)
                        ch.step(dve.tensor_scalar(cu, AQ[:, bass.ds(i * GROUP, GROUP)], wmean[:, 1:2], None, ALU.mult))
                        dve.tensor_scalar(cg, AQ[:, bass.ds(i * GROUP, GROUP)], wmean[:, 0:1], None, ALU.mult).then_inc(rstd_in.sem, 1)
                        for b in range(GROUP):
                            hidden(ch, i, b)
                            if b:
                                add_out(i, b - 1)
                        add_out(i, GROUP - 1)
                        ch.close()
                    dve.sem_inc(p_exp.sem, 1)

        def router_block(s, tg, prefetch=None):
            begin(TURNS, copied=1, s_ps=1, s_sub=1)
            begin(1, dve_step=STEPS, p_exp=1)
            rt = wk(s, "router", KD)
            BE = BATCH * EXPERTS
            area = lambda n, c=BE: VS[:, n * BE:n * BE + c]
            three = lambda n: area(n).rearrange("p (b e) -> p b e", e=EXPERTS)
            eq, run, first1, rest, first2, wide = (three(n) for n in range(6))
            m1, m2, ex, s1, s2 = (area(6)[:, n * BATCH:(n + 1) * BATCH] for n in range(5))
            L = RW[:, :, :]

            def wide_of(v):
                return v.unsqueeze(2).broadcast_to([P, BATCH, EXPERTS])

            with nc.Block() as block:
                @block.sync
                def _(sp):
                    if prefetch is not None:
                        load_weights(sp, prefetch)

                @block.gpsimd
                def _(pool):
                    with pool.Fori(0, TURNS) as i:
                        pool.wait_ge(s_ps.sem, s_ps.at(i, 0))
                        pool.tensor_copy(XS[:, :, :], XNT[:, :, bass.ds(i * GT, GT)]).then_inc(copied.sem, 1)

                @block.tensor
                def _(pe):
                    pe.wait_ge(w_loaded[s].sem, 32)
                    with pe.Fori(0, TURNS) as i:
                        pe.wait_ge(copied.sem, copied.at(i, 1))
                        pe.wait_ge(s_sub.sem, s_sub.at(i, 0))
                        for b in range(GROUP):
                            for k in range(KD):
                                ins = pe.matmul(PS[0][:, b * EXPERTS:(b + 1) * EXPERTS], XS[:, k, b * TOK:(b + 1) * TOK],
                                                rt[:, k, :], start=(k == 0), stop=(k == KD - 1))
                        ins.then_inc(s_ps.sem, 1)

                @block.vector
                def _(dve):
                    with dve.Fori(0, TURNS) as i:
                        dve.wait_ge(s_ps.sem, s_ps.at(i, 1))
                        dve.tensor_copy(RW[:, bass.ds(i * GROUP, GROUP), :], PS[0][:, 0:GROUP * EXPERTS].rearrange(
                            "p (b e) -> p b e", e=EXPERTS)).then_inc(s_sub.sem, 1)
                    dve.wait_ge(s_sub.sem, s_sub.at(TURNS, 0))
                    ch = Chain(dve, dve_step)

                    def first_of(logits, top, dst):
                        ch.link(dve.tensor_reduce(top, logits, AX, ALU.max))
                        ch.link(dve.tensor_tensor(eq, logits, wide_of(top), ALU.is_equal))
                        ch.link(dve.tensor_copy(run[:, :, 0:1], eq[:, :, 0:1]))
                        for e in range(1, EXPERTS):
                            ch.link(dve.tensor_tensor(run[:, :, e:e + 1], run[:, :, e - 1:e], eq[:, :, e:e + 1], ALU.add))
                        ch.link(dve.tensor_scalar(run, run, 1.0, None, ALU.is_le))
                        ch.link(dve.tensor_tensor(dst, run, eq, ALU.mult))

                    first_of(L, m1, first1)
                    ch.link(dve.scalar_tensor_tensor(out=rest, in0=first1, scalar=-BIG, in1=L, op0=ALU.mult, op1=ALU.add))
                    first_of(rest, m2, first2)
                    dve.tensor_tensor(ex, m2, m1, ALU.subtract).then_inc(quant_step.sem, 1)
                    dve.wait_ge(p_exp.sem, p_exp.at(0, 1))
                    ch.link(dve.tensor_scalar(s1, ex, 1.0, None, ALU.add))
                    ch.link(dve.reciprocal(s1, s1))
                    ch.link(dve.tensor_scalar(s1, s1, TG[:, tg:tg + 1], None, ALU.mult))
                    ch.link(dve.tensor_tensor(s2, s1, ex, ALU.mult))
                    ch.step(dve.tensor_tensor(first1, first1, wide_of(s1), ALU.mult))
                    ch.step(dve.tensor_tensor(first2, first2, wide_of(s2), ALU.mult))
                    ch.settle()
                    ch.link(dve.tensor_tensor(L, first1, first2, ALU.add))
                    ch.close()

                @block.scalar
                def _(act):
                    act.wait_ge(quant_step.sem, 5)
                    act.activation(ex, ex, ACT.Exp).then_inc(p_exp.sem, 1)

        def last_block():
            with nc.Block() as block:
                @block.sync
                def _(sp):
                    sp.dma_start(out, X[:, :, :]).then_inc(stored.sem, 16)
                    sp.wait_ge(stored.sem, 16)

        first_block()
        program = [
            lambda: norm_block(1),
            lambda: small_attention(0, 0, 32, 8, "rope"),
            lambda: norm_block(2, "quant"),
            lambda: quant_block(1, 4),
            lambda: norm_block(3),
            lambda: big_attention(2, 1, "mask"),
            lambda: norm_block(4, "rms", 5),
            lambda: small_attention(3, None, 16, 16, "causal"),
            lambda: ffn_block(3, "mod", 1, 8, 5),
            lambda: norm_block(5),
            lambda: big_attention(4, 2, "rms"),
            lambda: norm_block(6),
            lambda: ffn_block(5, "plain", 1, 8, 6),
            lambda: norm_block(7),
            lambda: small_attention(6, 3, 16, 16, "dca"),
            lambda: norm_block(8),
            lambda: router_block(7, 7),
            lambda: ffn_block(7, "plain", 1, 8, 7),
            lambda: ffn_block(8, "moe", 4, 4, first_expert=0, prefetch=9),
            lambda: ffn_block(9, "moe", 4, 4, first_expert=4),
        ]
        for n, part in enumerate(program):
            if n < stop:
                part()
        last_block()


def rows(m):
    k, n = m.shape
    return m.reshape(k // P, P, n).transpose(1, 0, 2).reshape(P, -1)


def padded(m, k):
    z = np.zeros((k,) + m.shape[1:], m.dtype)
    z[:m.shape[0]] = m
    return z


def everywhere(v):
    return np.broadcast_to(v, (P, v.size))


def slots(v):
    z = np.zeros((4, SLOT), v.dtype)
    z[:, :v.size] = v
    return z.reshape(P, 1)


def lay_out(i):
    c = lambda n: np.asarray(i[n])
    kv = c("L0_xattn_Wkv")
    kvd = c("L3_xattn_Wkv_dca")
    kv3 = [c("L3_xattn_Wk"), c("L3_xattn_Wv")]
    cat = np.concatenate(kv3, 1).reshape(CDIM, 16, 2, 16)
    bcat = np.concatenate([c("L3_xattn_bk"), c("L3_xattn_bv")]).reshape(16, 2, 16)
    l3k, l3v = cat[:, :, 0].reshape(CDIM, DIM), cat[:, :, 1].reshape(CDIM, DIM)
    b3k, b3v = bcat[:, 0].reshape(DIM), bcat[:, 1].reshape(DIM)
    e1, e2 = c("L3_ffn_w1"), c("L3_ffn_w2")

    def experts(lo):
        return [np.concatenate([rows(e1[e][:, :INTER]) for e in range(lo, lo + 4)], 1),
                np.concatenate([rows(e1[e][:, INTER:]) for e in range(lo, lo + 4)], 1),
                np.concatenate([rows(e2[e]) for e in range(lo, lo + 4)], 1)]

    norms = np.concatenate([slots(c(f"L3_xattn_{n}")) for n in ("qn_w", "qn_b", "kn_w", "kn_b", "kn_dca_w", "kn_dca_b")], 1)
    col = lambda v: v.reshape(-1, P).T
    return [
        [rows(c("L0_xattn_Wq")), kv[:, :DIM], kv[:, DIM:], rows(c("L0_xattn_Wout")), everywhere(c("L0_xattn_bout"))],
        [rows(c("L0_ffn_w1").T), rows(c("L0_ffn_w3").T), rows(padded(c("L0_ffn_w2").T, HID0P))],
        [rows(c("L1_xattn_Wq")), c("L1_xattn_Wk"), c("L1_xattn_Wv"), rows(c("L1_xattn_Wo"))],
        [rows(c("L1_ffn_Wq").T), rows(c("L1_ffn_Wk").T), rows(c("L1_ffn_Wv").T), rows(c("L1_ffn_Wo").T),
         rows(c("L1_ffn_A")), rows(c("L1_ffn_A")), padded(c("L1_ffn_B"), P), rows(c("L1_ffn_W_in_base").T), rows(c("L1_ffn_W_up_base").T),
         rows(c("L1_ffn_W_down").T), col(c("L1_ffn_ln1_w")), col(c("L1_ffn_ln2_w"))],
        [rows(c("L2_xattn_Wq")), c("L2_xattn_Wk"), c("L2_xattn_Wv"), rows(c("L2_xattn_Wo")), col(c("L2_xattn_gq")),
         col(c("L2_xattn_gk"))],
        [rows(c("L2_ffn_w_gate").T), rows(c("L2_ffn_w_up").T), rows(c("L2_ffn_w_down").T)],
        [rows(c("L3_xattn_Wq")), l3k, l3v, kvd[:, :DIM], kvd[:, DIM:], rows(c("L3_xattn_Wo")),
         everywhere(c("L3_xattn_bq")), everywhere(b3k), everywhere(b3v), everywhere(c("L3_xattn_bkv_dca")[:DIM]),
         everywhere(c("L3_xattn_bkv_dca")[DIM:]), everywhere(c("L3_xattn_bo")), norms],
        [rows(c("L3_ffn_w_gate")), rows(c("L3_ffn_w_up")), rows(c("L3_ffn_w_down")), rows(c("L3_ffn_router_w"))],
        experts(0),
        experts(4),
    ]


STOP = 99


def kernel(**inputs):
    import concourse.bacc as bacc
    from concourse.bass_utils import run_bass_kernel_spmd

    nc = bacc.Bacc("TRN2", target_bir_lowering=False, num_devices=1)
    mask = np.asarray(inputs["mask_BxS2_bf1"]).view(np.uint8)
    arrays = {
        "x": np.asarray(inputs["x"]).transpose(1, 0, 2),
        "ctxT": np.asarray(inputs["ctx_1024"]).transpose(2, 0, 1),
        "pos": np.asarray(inputs["fside_BxSx2_0"]).transpose(1, 0, 2),
        "mask_row": mask.reshape(1, BATCH * TOK),
        "mask_col": mask.T,
        "gates": everywhere(np.concatenate([np.asarray(inputs["g_xattn"]), np.asarray(inputs["g_ffn"])])),
    }
    for s, parts in enumerate(lay_out(inputs)):
        assert [p.shape[1] for p in parts] == [c for _, c in LAYOUT[s]], s
        arrays[f"weights{s}"] = np.concatenate(parts, 1)
    arrays = {n: np.ascontiguousarray(a) for n, a in arrays.items()}
    aps = {n: nc.dram_tensor(n, a.shape, mybir.dt.from_np(a.dtype), kind="ExternalInput").ap() for n, a in arrays.items()}
    out = nc.dram_tensor("out", (TOK, BATCH, DIM), F32, kind="ExternalOutput").ap()
    build(nc, STOP, aps["x"], aps["ctxT"], aps["pos"], aps["mask_row"], aps["mask_col"], aps["gates"], None,
          [aps[f"weights{s}"] for s in range(10)], out)
    r = run_bass_kernel_spmd(nc, [arrays], core_ids=[0])
    return np.ascontiguousarray(r.results[0]["out"].transpose(1, 0, 2))
```

```python
from contextlib import ExitStack

import numpy as np

import concourse.bass as bass
from concourse import mybir

ALU = mybir.AluOpType
ACT = mybir.ActivationFunctionType
F32 = mybir.dt.float32
BF16 = mybir.dt.bfloat16
F32R = mybir.dt.float32r
U8 = mybir.dt.uint8
AX = mybir.AxisListType.X

BATCH, TOK, DIM, CDIM = 16, 128, 256, 128
P = 128
KD = DIM // P
GROUP = 4
TURNS = BATCH // GROUP
GT = GROUP * TOK
HID0 = 704
HID0P = 768
FF = 1024
EXPERTS, INTER = 8, 512
MAIN = 112
DCA = TOK - MAIN
MAGIC = 12582912.0
BIG = 1e30
PI = float(np.pi)
INPUTS = 4

UH = 512
UNIT = 2 * KD * UH + UH // P * DIM
LAYOUT = [
    [("wq", KD * DIM), ("wk", DIM), ("wv", DIM), ("wo", KD * DIM), ("bo", DIM)],
    [("w1", KD * HID0), ("w3", KD * HID0), ("w2", HID0P // P * DIM)],
    [("wq", KD * 2048), ("wk", 1024), ("wv", 1024)],
    [("wq", KD * DIM), ("wk", KD * DIM), ("wv", KD * DIM), ("wo", KD * DIM), ("a", KD * 16), ("a2", KD * 16), ("bm", FF),
     ("ln1", KD), ("ln2", KD), ("unit0", UNIT), ("unit1", UNIT)],
    [("wq", KD * 2048), ("wk", 2048), ("wv", 2048), ("gq", 1), ("gk", 1)],
    [("unit0", UNIT), ("unit1", UNIT)],
    [("wq", KD * DIM), ("wk", DIM), ("wv", DIM), ("wkd", DIM), ("wvd", DIM), ("wo", KD * DIM), ("bq", DIM),
     ("bk", DIM), ("bv", DIM), ("bvd", DIM), ("bo", DIM), ("qnw", DIM), ("qnb", DIM),
     ("knw", DIM), ("knb", DIM), ("segc", 4)],
    [("router", KD * EXPERTS), ("unit0", UNIT), ("unit1", UNIT)],
]
WIDTH = [sum(c for _, c in part) for part in LAYOUT]


class Count:

    def __init__(self, sem):
        self.sem, self.base, self.per, self.turns = sem, 1, 0, 0

    def begin(self, per, turns=TURNS):
        self.base += self.per * self.turns
        self.per, self.turns = per, turns

    def at(self, i, n):
        return i * self.per + (self.base + n)


def build(nc, stop, x_in, ctxT_in, pos_in, mrow_in, mcol_in, gates_in, weights, wo_in, experts_in, out):
    with ExitStack() as ctx:
        def sb(name, shape, dt=F32):
            return ctx.enter_context(nc.sbuf_tensor(name, shape, dt))

        def count(name):
            return Count(ctx.enter_context(nc.semaphore(name)))

        X = sb("X", [P, BATCH, DIM])
        XNT = sb("XNT", [P, KD, BATCH * TOK])
        WREG = [sb(f"WREG{r}", [P, max(WIDTH[r::2])]) for r in range(2)]
        TG = sb("TG", [P, 8])
        SINCOS = sb("SINCOS", [P, 2, BATCH, 4])
        MCOL = sb("MCOL", [P, BATCH])
        IDENT = sb("IDENT", [P, P])
        IDENTB = sb("IDENTB", [P, P], BF16)
        CAUSAL = sb("CAUSAL", [P, 2, P], BF16)
        ONES = sb("ONES", [P, P])
        ONESB = sb("ONESB", [1, P], BF16)
        MHALF = sb("MHALF", [P, 64])
        AQ = sb("AQ", [P, BATCH])
        RW = sb("RW", [P, BATCH, 2 + EXPERTS])
        STAT = sb("STAT", [P, 256])
        PS = [ctx.enter_context(nc.psum_tensor(f"PS{b}", [P, 512], F32)) for b in range(8)]
        PSB = [b[:, :].bitcast(BF16) for b in PS]

        w_loaded = [count(f"w_loaded{s}") for s in range(len(LAYOUT))]
        inputs_loaded = count("inputs_loaded")
        stored = count("stored")
        dve_step, act_step, pool_step = count("dve_step"), count("act_step"), count("pool_step")
        rstd_in, rstd_out = count("rstd_in"), count("rstd_out")
        xn_ready, xnT_ps, xnT_sb = count("xn_ready"), count("xnT_ps"), count("xnT_sb")
        copied = count("copied")
        ctx_loaded = count("ctx_loaded")
        qk_ps, v_ps, qk_pad, qkT_ps, qkT_sb, v_sb = (count(n) for n in ("qk_ps", "v_ps", "qk_pad", "qkT_ps", "qkT_sb", "v_sb"))
        s_ps, s_sub, p_exp, p_norm, pT_ps, pT_sb, av_ps = (count(n) for n in ("s_ps", "s_sub", "p_exp", "p_norm", "pT_ps", "pT_sb", "av_ps"))
        o_tok, oT_ps, oT_sb, out_ps, x_done = (count(n) for n in ("o_tok", "oT_ps", "oT_sb", "out_ps", "x_done"))
        gu_ps, silu_done, h_done, down_ps = (count(n) for n in ("gu_ps", "silu_done", "h_done", "down_ps"))
        sq_done = count("sq_done")
        p_sum = count("p_sum")
        gained, zeroed = count("gained"), count("zeroed")
        s_max, m_pad, mT_ps, mT_sb, st_ps = (count(n) for n in ("s_max", "m_pad", "mT_ps", "mT_sb", "st_ps"))
        mask_loaded = count("mask_loaded")
        quant_step = count("quant_step")
        wo_loaded = [count("wo_loaded0"), count("wo_loaded1")]
        x_hi, x_lo, w_hi, w_lo = (count(n) for n in ("x_hi", "x_lo", "w_hi", "w_lo"))
        raw_loaded = [count("raw_loaded0"), count("raw_loaded1")]
        q_ps, qT_sb = count("q_ps"), count("qT_sb")

        STEPS = 256
        scope = [None, 0]

        MOD_END = 8

        def tile(name, shape, dt=F32):
            return scope[0].enter_context(nc.sbuf_tensor(f"{name}_{scope[1]}", shape, dt))

        def apart(eng):
            eng.memset(STAT[:, 255:256], 0.0)

        class Chain:

            def __init__(self, eng, cnt, i=0):
                self.eng, self.cnt, self.i, self.n = eng, cnt, i, 0

            def step(self, ins):
                self.n += 1
                ins.then_inc(self.cnt.sem, 1)

            def settle(self):
                self.eng.wait_ge(self.cnt.sem, self.cnt.at(self.i, self.n))

            def link(self, ins):
                self.step(ins)
                self.settle()

            def close(self):
                self.settle()
                self.eng.sem_inc(self.cnt.sem, STEPS - self.n)

        def w(s, name):
            at = 0
            for n, c in LAYOUT[s]:
                if n == name:
                    return WREG[s % 2][:, at:at + c]
                at += c
            raise KeyError(name)

        def wk(s, name, k):
            return w(s, name).rearrange("p (k n) -> p k n", k=k)

        def load_weights(sp, s):
            half = WIDTH[s] // 2
            for a, b in ((0, half), (half, WIDTH[s])):
                sp.dma_start(WREG[s % 2][:, a:b], weights[s][:, a:b]).then_inc(w_loaded[s].sem, 16)

        def begin(turns, **per):
            for name, n in per.items():
                named[name].begin(n, turns)

        named = dict(dve_step=dve_step, act_step=act_step, pool_step=pool_step, rstd_in=rstd_in, rstd_out=rstd_out,
                     xn_ready=xn_ready, xnT_ps=xnT_ps, xnT_sb=xnT_sb, copied=copied, qk_ps=qk_ps, v_ps=v_ps,
                     qk_pad=qk_pad, qkT_ps=qkT_ps, qkT_sb=qkT_sb, v_sb=v_sb, s_ps=s_ps, s_sub=s_sub, p_exp=p_exp,
                     p_norm=p_norm, pT_ps=pT_ps, pT_sb=pT_sb, av_ps=av_ps, o_tok=o_tok, oT_ps=oT_ps, oT_sb=oT_sb,
                     out_ps=out_ps, x_done=x_done, gu_ps=gu_ps, silu_done=silu_done, h_done=h_done,
                     down_ps=down_ps, sq_done=sq_done, gained=gained, zeroed=zeroed, p_sum=p_sum, s_max=s_max, m_pad=m_pad, mT_ps=mT_ps, mT_sb=mT_sb,
                     st_ps=st_ps, ctx_loaded=ctx_loaded, q_ps=q_ps, qT_sb=qT_sb,
                     x_hi=x_hi, x_lo=x_lo, w_hi=w_hi, w_lo=w_lo, raw_loaded0=raw_loaded[0], raw_loaded1=raw_loaded[1])

        def first_block():
            begin(1, dve_step=STEPS, act_step=STEPS, pool_step=STEPS, p_exp=1, s_sub=1)
            T1, QP = tile("angles", [P, 256]), tile("raw", [P, 1024])
            ang = T1[:, 0:128].rearrange("p (c b f) -> p c b f", c=2, b=BATCH)
            turn = T1[:, 128:256].rearrange("p (c b f) -> p c b f", c=2, b=BATCH)
            pos = QP[:, 0:BATCH * 2].rearrange("p (b a) -> p b a", a=2)
            mcol8 = tile("mcol8", [P, BATCH], U8)[:, :]
            with nc.Block() as block:
                @block.sync
                def _(sp):
                    sp.dma_start(pos, pos_in).then_inc(inputs_loaded.sem, 16)
                    sp.dma_start(mcol8, mcol_in).then_inc(inputs_loaded.sem, 16)
                    sp.dma_start(QP[:, 512:520], gates_in).then_inc(inputs_loaded.sem, 16)
                    sp.dma_start(X[:, :, :], x_in).then_inc(inputs_loaded.sem, 16)
                    load_weights(sp, 0)

                @block.gpsimd
                def _(pool):
                    for c in named.values():
                        pool.sem_inc(c.sem, 1)
                    ch = Chain(pool, pool_step)
                    ch.step(pool.memset(IDENT[:, :], 0.0))
                    ch.step(pool.memset(IDENTB[:, :], 0.0))
                    ch.step(pool.memset(CAUSAL[:, :, :], 0.0))
                    ch.step(pool.memset(ONES[:, :], 1.0))
                    ch.step(pool.memset(ONESB[:, :], 1.0))
                    ch.step(pool.memset(MHALF[:, :], -0.5))
                    ch.settle()
                    for m in (IDENT, IDENTB):
                        ch.step(pool.affine_select(out=m[:, :], in_=m[:, :], compare_op=ALU.not_equal, fill=1.0,
                                                   base=0, pattern=[[-1, P]], channel_multiplier=1))
                    for a, sign in enumerate((1, -1)):
                        ch.step(pool.affine_select(out=CAUSAL[:, a, :], in_=CAUSAL[:, a, :], compare_op=ALU.is_ge, fill=-BIG,
                                                   base=0, pattern=[[-sign, P]], channel_multiplier=sign))
                    ch.close()

                @block.vector
                def _(dve):
                    ch = Chain(dve, dve_step)
                    dve.wait_ge(inputs_loaded.sem, 16 * INPUTS)
                    for f, freq in enumerate((1.0, 10000.0 ** -0.5)):
                        for c in range(2):
                            dst = ang[:, c, :, :].rearrange("p b (a f) -> p b a f", f=2)[:, :, :, f]
                            ch.step(dve.tensor_scalar(dst, pos, freq, 0.5 * PI * c, ALU.mult, ALU.add))
                    ch.settle()
                    ch.link(dve.tensor_scalar(turn, ang, 0.5 / PI, MAGIC, ALU.mult, ALU.add))
                    ch.link(dve.tensor_scalar(turn, turn, MAGIC, -2.0 * PI, ALU.subtract, ALU.mult))
                    ch.link(dve.tensor_tensor(ang, ang, turn, ALU.add))
                    ch.link(dve.tensor_scalar(ang, ang, 3.1415925, -3.1415925, ALU.min, ALU.max))
                    ch.step(dve.tensor_copy(MCOL[:, :], mcol8))
                    ch.settle()
                    ch.link(dve.memset(STAT[:, :], 0.0))
                    dve.sem_inc(s_sub.sem, 1)
                    dve.wait_ge(p_exp.sem, p_exp.at(0, 1))
                    ch.close()

                @block.scalar
                def _(act):
                    act.wait_ge(s_sub.sem, s_sub.at(0, 1))
                    nc.scalar.activation(SINCOS[:, :, :, :], ang, ACT.Sin).then_inc(act_step.sem, 1)
                    nc.scalar.activation(TG[:, :], QP[:, 512:520], ACT.Tanh).then_inc(p_exp.sem, 1)
                    act.wait_ge(p_exp.sem, p_exp.at(0, 1))
                    act.sem_inc(act_step.sem, STEPS - 1)

        def norm_block(prefetch, kind="plain", tg=None):
            begin(TURNS, dve_step=STEPS, rstd_in=1 + (kind == "rms"), rstd_out=1 + (kind == "rms"), xn_ready=1,
                  xnT_ps=KD, xnT_sb=KD)
            XN, SQ = tile("xn", [P, GROUP, DIM]), tile("sq", [P, GROUP, DIM])
            st = STAT[:, 0:6 * GROUP].rearrange("p (b c) -> p b c", c=6)
            mv = STAT[:, 32:32 + 2 * GROUP].rearrange("p (b c) -> p b c", c=2)
            var, rstd = STAT[:, 48:48 + GROUP], STAT[:, 56:56 + GROUP]
            aux, rinv = STAT[:, 64:64 + GROUP], STAT[:, 72:72 + GROUP]
            XQT = XNT[:, 0, :].bitcast(BF16).rearrange("p (k t) -> p k t", k=KD)
            with nc.Block() as block:
                if prefetch is not None:
                    @block.sync
                    def _(sp):
                        load_weights(sp, prefetch)

                @block.vector
                def _(dve):
                    with dve.Fori(0, TURNS) as i:
                        ch = Chain(dve, dve_step, i)
                        for b in range(GROUP):
                            ch.step(dve.bn_stats(st[:, b, :], X[:, bass.ds(i * GROUP + b, 1), :].rearrange("p a d -> p (a d)")))
                        ch.settle()
                        apart(dve)
                        for b in range(GROUP):
                            ch.step(dve.bn_aggr(mv[:, b, :], st[:, b, :]))
                        ch.settle()
                        dve.tensor_scalar(var, mv[:, :, 1], 1e-5, None, ALU.add).then_inc(rstd_in.sem, 1)
                        dve.wait_ge(rstd_out.sem, rstd_out.at(i, 1))
                        dve.wait_ge(xnT_ps.sem, xnT_ps.at(i, 0))
                        for b in range(GROUP):
                            ins = dve.tensor_scalar(XN[:, b, :], X[:, bass.ds(i * GROUP + b, 1), :].rearrange("p a d -> p (a d)"),
                                                    mv[:, b, 0:1], rstd[:, b:b + 1], ALU.subtract, ALU.mult)
                            if kind == "plain" and b == GROUP - 1:
                                ins.then_inc(xn_ready.sem, 1)
                            else:
                                ch.step(ins)
                        if kind == "rms":
                            ch.settle()
                            for b in range(GROUP):
                                ch.step(dve.tensor_tensor_reduce(SQ[:, b, :], XN[:, b, :], XN[:, b, :], 1.0, 0.0,
                                                                 ALU.mult, ALU.add, aux[:, b:b + 1]))
                                xb = X[:, bass.ds(i * GROUP + b, 1), :].rearrange("p a d -> p (a d)")
                                ch.step(dve.scalar_tensor_tensor(out=xb, in0=XN[:, b, :], scalar=TG[:, tg:tg + 1],
                                                                 in1=xb, op0=ALU.mult, op1=ALU.add))
                            ch.settle()
                            dve.tensor_scalar(var, aux, 1.0 / DIM, 1e-6, ALU.mult, ALU.add).then_inc(rstd_in.sem, 1)
                            dve.wait_ge(rstd_out.sem, rstd_out.at(i, 2))
                            ch.settle()
                            dve.tensor_tensor(XN[:, :, :], XN[:, :, :], rstd.unsqueeze(2).broadcast_to([P, GROUP, DIM]),
                                              ALU.mult).then_inc(xn_ready.sem, 1)
                        if kind == "quant":
                            ch.settle()
                            ch.link(dve.tensor_reduce(aux, XN[:, :, :], AX, ALU.max, apply_absolute_value=True))
                            ch.link(dve.tensor_scalar(aux, aux, 1e-5, None, ALU.max))
                            ch.step(dve.tensor_scalar(AQ[:, bass.ds(i * GROUP, GROUP)], aux, 1.0 / 127.0, None, ALU.mult))
                            ch.link(dve.reciprocal(rinv, aux))
                            ch.link(dve.tensor_scalar(rinv, rinv, 127.0, None, ALU.mult))
                            for b in range(GROUP):
                                ch.step(dve.tensor_scalar(XN[:, b, :], XN[:, b, :], rinv[:, b:b + 1], MAGIC, ALU.mult, ALU.add))
                            ch.settle()
                            ch.link(dve.tensor_scalar(XN[:, :, :], XN[:, :, :], MAGIC + 127.0, MAGIC - 128.0, ALU.min, ALU.max))
                            dve.tensor_scalar(XN[:, :, :], XN[:, :, :], MAGIC, None, ALU.subtract).then_inc(xn_ready.sem, 1)
                        ch.close()

                @block.gpsimd
                def _(pool):
                    with pool.Fori(0, TURNS) as i:
                        for n in range(1 + (kind == "rms")):
                            pool.wait_ge(rstd_in.sem, rstd_in.at(i, n + 1))
                            pool.tensor_tensor(rstd, var, MHALF[:, 0:GROUP], ALU.pow).then_inc(rstd_out.sem, 1)

                @block.tensor
                def _(pe):
                    with pe.Fori(0, TURNS) as i:
                        pe.wait_ge(xn_ready.sem, xn_ready.at(i, 1))
                        for k in range(KD):
                            pe.wait_ge(xnT_sb.sem, xnT_sb.at(i, 0))
                            for b in range(GROUP):
                                ins = pe.transpose(PS[k][:, b * P:(b + 1) * P], XN[:, b, k * P:(k + 1) * P], IDENT[:, :])
                            ins.then_inc(xnT_ps.sem, 1)

                @block.scalar
                def _(act):
                    dst = XQT if kind == "quant" else XNT
                    with act.Fori(0, TURNS) as i:
                        for k in range(KD):
                            act.wait_ge(xnT_ps.sem, xnT_ps.at(i, k + 1))
                            act.copy(dst[:, k, bass.ds(i * GT, GT)], PS[k][:, :]).then_inc(xnT_sb.sem, 1)

        def small_attention(s, tg, NH, HD, kind, prefetch=None, MODT=None):
            seg, causal = kind == "dca", kind == "causal"
            SL = 4 * HD
            PER = P // SL
            NS = NH // 4
            MR = 3 * HD
            NM = 4 if seg else 2
            V = 2 * (HD + 1) if seg else HD + 1
            segs = ((0, MAIN), (MAIN, TOK)) if seg else ((0, TOK),)
            OFF = dict(project=-10 if NS == 4 else -9, heads=-9 if NS == 4 else -8, turn=-4, value=-1, score=0, pad_max=NS - 1, turn_max=NS,
                       score_t=NS + 1, av=NS + 3, attended=2 * NS + 3, turn_out=2 * NS + 4, out=2 * NS + 5,
                       add=2 * NS + 6, mod=2 * NS + 7)
            LASTP = BATCH - 1 + OFF["mod"] // NS
            FIRSTP = OFF["project"] // NS
            LOOP0 = 3
            LOOPS = (BATCH + FIRSTP - LOOP0) // 3
            S_BANK = (0, 0) if seg else (0, 1)
            begin(BATCH, copied=1, ctx_loaded=0 if causal else 16 * len(segs), qk_ps=1, v_ps=1, qk_pad=1, qkT_ps=4,
                  qkT_sb=4, v_sb=1, s_ps=NS, s_max=NS, m_pad=1, mT_ps=2, mT_sb=2, st_ps=NS, p_exp=NS, av_ps=NS,
                  o_tok=1, oT_ps=1, oT_sb=1, out_ps=1, x_done=1, rstd_in=2 * seg, rstd_out=2 * seg,
                  q_ps=int(causal), qT_sb=int(causal))
            begin(LASTP - FIRSTP + 1, dve_step=STEPS)
            begin(1, pool_step=1 if causal else 2, zeroed=1, gained=1)

            with nc.Block() as block:
                xs = tile("xs", [P, 3, KD, TOK])
                cs = None if causal else tile("cs", [P, 3, len(segs), TOK])
                qp, kp = tile("qp", [P, 3, NH, SL], F32R), tile("kp", [P, 3, NH, SL], F32R)
                qT, kT, qM = (tile(n, [P, 3, 8, TOK], F32R) for n in ("qT", "kT", "qM"))
                vs = tile("vs", [P, 3, NH, V])
                pT = tile("pT", [P, 2, 512])
                prod = None if causal else tile("prod", [P, 4, NH * HD // 2])
                fresh = tile("fresh", [P, 2, DIM])
                nmax = tile("nmax", [P, 2, NH])
                rsum = tile("rsum", [P, 2, NH])
                otok = tile("otok", [P, len(segs), DIM])
                oT = tile("oT", [P, KD, TOK])
                sc = tile("sc", [P, 2, 4])
                hsum, hvar, hrstd = (tile(n, [P, 2, NH]) for n in ("hsum", "hvar", "hrstd"))
                aT = tile("aT", [P, KD, TOK]) if causal else None
                vbias = tile("vbias", [P, DIM]) if seg else None
                obias = None if causal else tile("obias", [P, DIM])
                wq, wo = wk(s, "wq", KD), wk(s, "wo", KD)

                def slot_ops(beta, u):
                    for stage, count_ in STAGES:
                        for n in range(count_):
                            back, at = divmod(OFF[stage] + n, NS)
                            if at == u:
                                yield stage, back, n

                STAGES = [("attended", 1), ("add", 1), ("score", NS), ("score_t", NS), ("av", NS), ("pad_max", 1),
                          ("turn_max", 2), ("turn", 4), ("turn_out", 1), ("out", 1), ("mod", int(causal)),
                          ("value", 1), ("project", 1), ("heads", 3)]

                def run(eng, stages, start_of_period=None, end_of_period=None):
                    def period(beta, phase):
                        if start_of_period:
                            start_of_period(beta)
                        for u in range(NS):
                            for stage, back, n in slot_ops(beta, u):
                                if stage not in stages:
                                    continue
                                if isinstance(beta, int) and not 0 <= beta - back < BATCH:
                                    continue
                                stages[stage](beta - back, n, (phase - back) % 3)
                        if end_of_period:
                            end_of_period(beta)

                    for beta in range(FIRSTP, LOOP0):
                        period(beta, beta)
                    with eng.Fori(1, 1 + LOOPS) as i:
                        for r in range(3):
                            period(i * 3 + r, r)
                    for beta in range(LOOP0 + 3 * LOOPS, LASTP + 1):
                        period(beta, beta)

                @block.sync
                def _(sp):
                    if prefetch is not None:
                        load_weights(sp, prefetch)
                    if not causal:
                        sp.wait_ge(pool_step.sem, pool_step.at(0, 1))

                        def load(b, r, again):
                            if again:
                                if seg:
                                    sp.wait_ge(v_ps.sem, v_ps.at(b - 3, 1))
                                else:
                                    sp.wait_ge(qk_ps.sem, qk_ps.at(b - 1, 1))
                            elif b:
                                sp.wait_ge(ctx_loaded.sem, ctx_loaded.at(b - 1, 16 * len(segs)))
                            for a, (lo, hi) in enumerate(segs):
                                sp.dma_start(cs[:, r, a, lo:hi], ctxT_in[:, bass.ds(b, 1), lo:hi].rearrange("p b t -> p (b t)"))\
                                    .then_inc(ctx_loaded.sem, 16)

                        for b in range(3):
                            load(b, b, False)
                        with sp.Fori(1, 5) as i:
                            for r in range(3):
                                load(i * 3 + r, r, True)
                        load(BATCH - 1, 0, True)

                @block.gpsimd
                def _(pool):
                    if not causal:
                        pool.memset(cs[:, :, :, :], 0.0)
                    pool.memset(vs[:, :, :, :], 1.0).then_inc(pool_step.sem, 1)
                    if not causal:
                        pool.wait_ge(w_loaded[s].sem, 32)
                        pool.tensor_scalar(obias[:, :], w(s, "bo"), TG[:, tg:tg + 1], None, ALU.mult).then_inc(pool_step.sem, 1)
                        pool.wait_ge(pool_step.sem, pool_step.at(0, 2))

                    def copy(b, r, again):
                        if again:
                            pool.wait_ge(v_ps.sem, v_ps.at(b - 3, 1))
                        if not causal:
                            xb = X[:, bass.ds(b, 1), :].rearrange("p a d -> p (a d)")
                            pool.tensor_tensor(xb, xb, obias[:, :], ALU.add)
                        src = XNT[:, :, bass.ds(b * TOK, TOK)]
                        pool.tensor_copy(xs[:, r, :, :], src).then_inc(copied.sem, 1)

                    def head_rstd(b):
                        for n in range(2):
                            pool.wait_ge(rstd_in.sem, rstd_in.at(b, n + 1))
                            pool.tensor_tensor(hrstd[:, n, :], hvar[:, n, :], MHALF[:, 0:NH], ALU.pow).then_inc(rstd_out.sem, 1)

                    for b in range(3):
                        copy(b, b, False)
                    if seg:
                        head_rstd(0)
                    with pool.Fori(1, 5) as i:
                        for r in range(3):
                            if seg:
                                head_rstd(i * 3 + r - 2)
                            copy(i * 3 + r, r, True)
                    if seg:
                        head_rstd(BATCH - 3)
                    copy(BATCH - 1, 0, True)
                    if seg:
                        for b in range(BATCH - 2, BATCH):
                            head_rstd(b)

                @block.tensor
                def _(pe):
                    pe.wait_ge(w_loaded[s].sem, 32)
                    if causal:
                        pe.wait_ge(gained.sem, gained.at(0, 1))

                    def context(dst, r, name, dca_name=None):
                        if causal:
                            for c in range(KD):
                                ins = pe.matmul(dst, xs[:, r, c, :], wk(s, name, KD)[:, c, :], start=(c == 0), stop=(c == KD - 1))
                            return ins
                        if not seg:
                            return pe.matmul(dst, cs[:, r, 0, :], w(s, name), start=True, stop=True)
                        for a, nm in enumerate((name, dca_name)):
                            ins = pe.matmul(dst, cs[:, r, a, :], w(s, nm), start=(a == 0), stop=(a == 1))
                        return ins

                    def project(b, n, r):
                        pe.wait_ge(copied.sem, copied.at(b, 1))
                        if not causal:
                            pe.wait_ge(ctx_loaded.sem, ctx_loaded.at(b, 16 * len(segs)))
                        if not (isinstance(b, int) and b == 0):
                            pe.wait_ge(qk_pad.sem, qk_pad.at(b - 1, 1))
                        q, k = PS[6][:, 0:DIM], PS[6][:, DIM:2 * DIM]
                        for c in range(KD):
                            pe.matmul(q, xs[:, r, c, :], wq[:, c, :], start=(c == 0), stop=(c == KD - 1))
                        context(k, r, "wk", "wkd").then_inc(qk_ps.sem, 1)

                    def value(b, n, r):
                        before = OFF["add"] // NS + 1
                        if not (isinstance(b, int) and b < before):
                            pe.wait_ge(x_done.sem, x_done.at(b - before, 1))
                            if causal:
                                pe.wait_ge(qT_sb.sem, qT_sb.at(b - before, 1))
                        if not (isinstance(b, int) and b == 0):
                            pe.wait_ge(v_sb.sem, v_sb.at(b - 1, 1))
                        if seg:
                            for a, nm in enumerate(("wv", "wvd")):
                                dst = PS[7][:, a * DIM:(a + 1) * DIM]
                                ins = pe.matmul(dst, cs[:, r, a, :], w(s, nm), start=True, stop=True)
                        else:
                            ins = context(PS[7][:, 0:DIM], r, "wv")
                        ins.then_inc(v_ps.sem, 1)

                    def turn(b, n, r):
                        if n == 0:
                            pe.wait_ge(qk_pad.sem, qk_pad.at(b, 1))
                        if NS == 4 and n < 2:
                            if not (isinstance(b, int) and b < 2):
                                pe.wait_ge(mT_sb.sem, mT_sb.at(b - 2, n + 1))
                            elif n:
                                pe.wait_ge(qkT_sb.sem, qkT_sb.at(b, n))
                        elif n == 0:
                            if not (isinstance(b, int) and b < 2):
                                pe.wait_ge(mT_sb.sem, mT_sb.at(b - 2, 2))
                        else:
                            pe.wait_ge(qkT_sb.sem, qkT_sb.at(b, n))
                        if n == 0 and isinstance(b, int) and b == 1:
                            pe.wait_ge(qkT_sb.sem, qkT_sb.at(0, 4))
                        src = (qp, kp)[n // 2][:, r, :, :].bitcast(F32).rearrange("p h e -> p (h e)")
                        for c in range(4):
                            at = (4 * (n % 2) + c) * P
                            ins = pe.transpose(PS[5][:, c * P:(c + 1) * P], src[:, at:at + P], IDENT[:, :])
                        ins.then_inc(qkT_ps.sem, 1)

                    def turn_max(b, n, r):
                        if n == 0:
                            pe.wait_ge(m_pad.sem, m_pad.at(b, 1))
                        last = isinstance(b, int) and b == BATCH - 1
                        if n == 0:
                            pe.wait_ge(qkT_sb.sem, qkT_sb.at(b if last else b + 1, 4))
                        elif NS == 4 and not (isinstance(b, int) and b + 2 >= BATCH):
                            pe.wait_ge(qkT_sb.sem, qkT_sb.at(b + 2, 1))
                        else:
                            pe.wait_ge(mT_sb.sem, mT_sb.at(b, 1))
                        src = qp[:, r, :, :].bitcast(F32).rearrange("p h e -> p (h e)")
                        for c in range(4):
                            at = (4 * n + c) * P
                            ins = pe.transpose(PS[5][:, c * P:(c + 1) * P], src[:, at:at + P], IDENT[:, :])
                        ins.then_inc(mT_ps.sem, 1)

                    def score(b, u, r):
                        j, half = u % PER, u // PER
                        if u == 0:
                            pe.wait_ge(qkT_sb.sem, qkT_sb.at(b, 4))
                        d = 1 if seg else 2
                        if u >= d:
                            pe.wait_ge(s_max.sem, s_max.at(b, u - d + 1))
                        elif not (isinstance(b, int) and b == 0):
                            pe.wait_ge(s_max.sem, s_max.at(b - 1, NS + u - d + 1))
                        bank = PS[S_BANK[u % 2]]
                        if causal:
                            pe.matmul(bank[:, :].rearrange("p (h c) -> p h c", h=4), IDENTB[:, :],
                                      CAUSAL[:, 0, :].unsqueeze(1).broadcast_to([P, 4, P]), start=True, stop=False,
                                      skip_group_check=True)
                        rows = slice(SL * j, SL * j + MR)
                        for c in range(4):
                            ins = pe.matmul(bank[:, c * P:(c + 1) * P], qT[rows, r, 4 * half + c, :],
                                            kT[rows, r, 4 * half + c, :], start=not causal, stop=True, skip_group_check=True)
                        ins.then_inc(s_ps.sem, 1)

                    def score_t(b, u, r):
                        j, half = u % PER, u // PER
                        pe.wait_ge(mT_sb.sem, mT_sb.at(b, half + 1))
                        if u >= 2:
                            pe.wait_ge(p_exp.sem, p_exp.at(b, u - 1))
                        elif not (isinstance(b, int) and b == 0):
                            pe.wait_ge(p_exp.sem, p_exp.at(b - 1, NS + u - 1))
                        bank = PS[2 + u % 2]
                        if causal:
                            pe.matmul(bank[:, :].rearrange("p (h c) -> p h c", h=4), IDENTB[:, :],
                                      CAUSAL[:, 1, :].unsqueeze(1).broadcast_to([P, 4, P]), start=True, stop=False,
                                      skip_group_check=True)
                        rows = slice(SL * j, SL * j + MR + NM)
                        for c in range(4):
                            ins = pe.matmul(bank[:, c * P:(c + 1) * P], kT[rows, r, 4 * half + c, :],
                                            qM[rows, r, 4 * half + c, :], start=not causal, stop=True, skip_group_check=True)
                        ins.then_inc(st_ps.sem, 1)

                    def av(b, u, r):
                        j, half = u % PER, u // PER
                        pe.wait_ge(p_exp.sem, p_exp.at(b, u + 1))
                        if u == 0:
                            pe.wait_ge(v_sb.sem, v_sb.at(b, 1))
                            if not (isinstance(b, int) and b == 0):
                                pe.wait_ge(o_tok.sem, o_tok.at(b - 1, 1))
                        for c in range(4):
                            h = PER * (4 * half + c) + j
                            if seg:
                                dst = PS[(4, 1)[h // 8]][:, h % 8 * V:(h % 8 + 1) * V]
                            else:
                                dst = PS[4][:, h * V:(h + 1) * V]
                            ins = pe.matmul(dst, pT[:, u % 2, c * P:(c + 1) * P], vs[:, r, h, :], start=True, stop=True)
                        ins.then_inc(av_ps.sem, 1)

                    def turn_out(b, n, r):
                        pe.wait_ge(o_tok.sem, o_tok.at(b, 1))
                        ahead = OFF["turn_out"] // NS
                        if not isinstance(b, int) or b + ahead < BATCH:
                            pe.wait_ge(v_sb.sem, v_sb.at(b + ahead, 1))
                        elif b + ahead == BATCH:
                            pe.wait_ge(v_sb.sem, v_sb.at(BATCH - 1, 1))
                        if not (isinstance(b, int) and b == 0):
                            pe.wait_ge(x_done.sem, x_done.at(b - 1, 1))
                            if causal:
                                pe.wait_ge(qT_sb.sem, qT_sb.at(b - 1, 1))
                        for c in range(KD):
                            ins = pe.transpose(PS[7][:, c * P:(c + 1) * P], otok[:, 0, c * P:(c + 1) * P], IDENT[:, :])
                        ins.then_inc(oT_ps.sem, 1)

                    def out_(b, n, r):
                        pe.wait_ge(oT_sb.sem, oT_sb.at(b, 1))
                        dst = PS[7][:, DIM:2 * DIM]
                        if causal:
                            for m in range(KD):
                                for c in range(KD):
                                    ins = pe.matmul(dst[:, m * P:(m + 1) * P], wo[:, c, m * P:(m + 1) * P], oT[:, c, :],
                                                    start=(c == 0), stop=(c == KD - 1))
                        else:
                            for c in range(KD):
                                ins = pe.matmul(dst, oT[:, c, :], wo[:, c, :], start=(c == 0), stop=(c == KD - 1))
                        ins.then_inc(out_ps.sem, 1)

                    def mod(b, n, r):
                        pe.wait_ge(x_done.sem, x_done.at(b, 1))
                        a = wk(s, "a", KD)
                        for c in range(KD):
                            ins = pe.matmul(PS[7][0:16, 0:TOK], a[:, c, :], aT[:, c, :], start=(c == 0), stop=(c == KD - 1))
                        ins.then_inc(q_ps.sem, 1)

                    run(pe, dict(score=score, score_t=score_t, av=av, turn=turn, turn_max=turn_max, turn_out=turn_out,
                                 out=out_, mod=mod, value=value, project=project))

                @block.vector
                def _(dve):
                    dve.memset(qp[:, :, :, MR:SL].bitcast(F32), 0.0)
                    dve.memset(kp[:, :, :, MR:SL].bitcast(F32), 0.0).then_inc(zeroed.sem, 1)
                    dve.wait_ge(zeroed.sem, zeroed.at(0, 1))
                    dve.wait_ge(pool_step.sem, pool_step.at(0, 1))
                    if seg:
                        dve.wait_ge(w_loaded[s].sem, 32)
                        for r in range(3):
                            dve.tensor_copy(kp[:, r, :, MR:MR + NM], w(s, "segc").unsqueeze(1).broadcast_to([P, NH, NM]))
                        for r in range(3):
                            for a in range(2):
                                ins = dve.tensor_copy(vs[:, r, :, a * (HD + 1) + HD],
                                                      w(s, "segc")[:, 2 * a:2 * a + 1].broadcast_to([P, NH]))
                        ins = dve.tensor_tensor(vbias[:, :], w(s, "bv"), w(s, "bvd"), ALU.add)
                        ins.then_inc(gained.sem, 1)
                    else:
                        for r in range(3):
                            ins = dve.tensor_copy(kp[:, r, :, MR:MR + NM], ONES[:, 0:NM].unsqueeze(1).broadcast_to([P, NH, NM]))
                        if not causal:
                            ins.then_inc(gained.sem, 1)
                    if causal:
                        dve.wait_ge(w_loaded[s].sem, 32)
                        gained_parts = [(wk(s, n, KD), "ln1") for n in ("wq", "wk", "wv")] + [(wk(s, "a2", KD), "ln2")]
                        for u in ("unit0", "unit1"):
                            for lo in (0, KD * UH):
                                gained_parts.append((w(s, u)[:, lo:lo + KD * UH].rearrange("p (k n) -> p k n", k=KD), "ln2"))
                        for part, gain in gained_parts:
                            for c in range(KD):
                                ins = dve.tensor_scalar(part[:, c, :], part[:, c, :], w(s, gain)[:, c:c + 1], None, ALU.mult)
                        ins.then_inc(gained.sem, 1)
                    dve.wait_ge(gained.sem, gained.at(0, 1))
                    chain = [None]
                    both = PS[6][:, :].rearrange("p (a h e) -> p a h e", a=2, h=NH)

                    def split(ch, part, r):
                        dst = (qp, kp)[part][:, r, :, :]
                        src = fresh[:, part, :].rearrange("p (h e) -> p h e", h=NH)
                        step = (1, 2)[part] * HD
                        for at in (0, step):
                            ch.step(dve.tensor_copy(dst[:, :, at:at + HD], src))
                        ch.settle()
                        lo = (2, 1)[part] * HD
                        ch.step(dve.tensor_tensor(dst[:, :, lo:lo + HD], src, dst[:, :, 0:HD].bitcast(F32), ALU.subtract))

                    def heads(b, n, r):
                        ch = chain[0]
                        if n == 0:
                            dve.wait_ge(qk_ps.sem, qk_ps.at(b, 1))
                        if kind == "rope":
                            if n == 0:
                                ch.link(dve.tensor_copy(sc[:, :, :], SINCOS[:, :, bass.ds(b, 1), :].rearrange("p c b f -> p c (b f)")))
                            if n < 2:
                                src = both[:, n].rearrange("p h (f e) -> p h f e", e=2)
                                sin = sc[:, 0, :].unsqueeze(1).broadcast_to([P, NH, 4])
                                cos = sc[:, 1, :].unsqueeze(1).broadcast_to([P, NH, 4])
                                m = prod[:, :, :].rearrange("p a (h f) -> p a h f", f=4)
                                ch.step(dve.tensor_tensor(m[:, 0], src[:, :, :, 0], cos, ALU.mult))
                                ch.step(dve.tensor_tensor(m[:, 1], src[:, :, :, 1], sin, ALU.mult))
                                ch.step(dve.tensor_tensor(m[:, 2], src[:, :, :, 0], sin, ALU.mult))
                                ch.step(dve.tensor_tensor(m[:, 3], src[:, :, :, 1], cos, ALU.mult))
                                ch.settle()
                                d = fresh[:, n, :].rearrange("p (h f e) -> p h f e", f=4, e=2)
                                ch.step(dve.tensor_tensor(d[:, :, :, 0], m[:, 0], m[:, 1], ALU.subtract))
                                ch.step(dve.tensor_tensor(d[:, :, :, 1], m[:, 2], m[:, 3], ALU.add))
                                ch.settle()
                        elif causal:
                            if n < 2:
                                ch.link(dve.tensor_copy(fresh[:, n, :], PS[6][:, n * DIM:(n + 1) * DIM]))
                        else:
                            if n < 2:
                                cen = fresh[:, n, :].rearrange("p (h e) -> p h e", h=NH)
                                ch.link(dve.tensor_tensor(fresh[:, n, :], PS[6][:, n * DIM:(n + 1) * DIM],
                                                          w(s, ("bq", "bk")[n]), ALU.add))
                                sq = prod[:, 2 * n:2 * n + 2, :].rearrange("p a (h e) -> p (a h) e", e=HD)
                                mean = hsum[:, n, :]
                                ch.link(dve.tensor_reduce(mean, cen, AX, ALU.add))
                                ch.link(dve.tensor_scalar(mean, mean, 1.0 / HD, None, ALU.mult))
                                ch.link(dve.tensor_tensor(cen, cen, mean.unsqueeze(2).broadcast_to([P, NH, HD]), ALU.subtract))
                                ch.link(dve.tensor_tensor(sq, cen, cen, ALU.mult))
                                ch.link(dve.tensor_reduce(mean, sq, AX, ALU.add))
                                dve.tensor_scalar(hvar[:, n, :], mean, 1.0 / HD, 1e-6, ALU.mult, ALU.add).then_inc(rstd_in.sem, 1)
                            else:
                                for p in range(2):
                                    cen = fresh[:, p, :].rearrange("p (h e) -> p h e", h=NH)
                                    dve.wait_ge(rstd_out.sem, rstd_out.at(b, p + 1))
                                    ch.step(dve.tensor_tensor(cen, cen, hrstd[:, p, :].unsqueeze(2).broadcast_to([P, NH, HD]), ALU.mult))
                                ch.settle()
                                for op, names in ((ALU.mult, ("qnw", "knw")), (ALU.add, ("qnb", "knb"))):
                                    for p in range(2):
                                        ch.step(dve.tensor_tensor(fresh[:, p, :], fresh[:, p, :], w(s, names[p]), op))
                                    ch.settle()
                        if n == 2:
                            if not (isinstance(b, int) and b < 3):
                                dve.wait_ge(mT_ps.sem, mT_ps.at(b - 3, 2))
                            split(ch, 0, r)
                            split(ch, 1, r)
                            ch.settle()
                            dve.sem_inc(qk_pad.sem, 1)

                    def score(b, u, r):
                        ch = chain[0]
                        j, half = u % PER, u // PER
                        dve.wait_ge(s_ps.sem, s_ps.at(b, u + 1))
                        S = PS[S_BANK[u % 2]][:, :].rearrange("p (h c) -> p h c", h=4)
                        for a, (lo, hi) in enumerate(segs):
                            first = PER * 4 * half + j
                            dst = nmax[:, a, first:first + 3 * PER + 1:PER]
                            ins = dve.tensor_reduce(dst, S[:, :, lo:hi], AX, ALU.max, negate=True)
                            if a < len(segs) - 1:
                                ch.step(ins)
                        ins.then_inc(s_max.sem, 1)

                    def pad_max(b, n, r):
                        ch = chain[0]
                        ch.settle()
                        dve.wait_ge(s_max.sem, s_max.at(b, NS))
                        dve.wait_ge(qkT_ps.sem, qkT_ps.at(b, 4))
                        for a in range(len(segs)):
                            ch.step(dve.tensor_copy(qp[:, r, :, MR + 2 * a], nmax[:, a, :]))
                        ch.settle()
                        for a in range(len(segs)):
                            ch.step(dve.tensor_tensor(qp[:, r, :, MR + 2 * a + 1], nmax[:, a, :],
                                                      qp[:, r, :, MR + 2 * a].bitcast(F32), ALU.subtract))
                        ch.settle()
                        dve.sem_inc(m_pad.sem, 1)

                    def attended(b, n, r):
                        ch = chain[0]
                        dve.wait_ge(av_ps.sem, av_ps.at(b, NS))
                        if not (isinstance(b, int) and b == 0):
                            dve.wait_ge(oT_ps.sem, oT_ps.at(b - 1, 1))
                        if seg:
                            for g, bank in enumerate((4, 1)):
                                O = PS[bank][:, 0:8 * V].rearrange("p (h a v) -> p h a v", h=8, a=2)
                                R = rsum[:, :, 8 * g:8 * g + 8].rearrange("p a h -> p h a")
                                ch.step(dve.reciprocal(R, O[:, :, :, HD]))
                            ch.settle()
                            for g, bank in enumerate((4, 1)):
                                O = PS[bank][:, 0:8 * V].rearrange("p (h a v) -> p h a v", h=8, a=2)
                                for a in range(2):
                                    dst = otok[:, a, 8 * HD * g:8 * HD * (g + 1)].rearrange("p (h e) -> p h e", e=HD)
                                    ch.step(dve.tensor_tensor(dst, O[:, :, a, 0:HD],
                                                              rsum[:, a, 8 * g:8 * g + 8].unsqueeze(2).broadcast_to([P, 8, HD]), ALU.mult))
                            ch.settle()
                            ch.link(dve.tensor_tensor(otok[:, 0, :], otok[:, 0, :], otok[:, 1, :], ALU.add))
                            dve.tensor_tensor(otok[:, 0, :], otok[:, 0, :], vbias[:, :], ALU.add).then_inc(o_tok.sem, 1)
                        else:
                            O = PS[4][:, 0:NH * V].rearrange("p (h v) -> p h v", v=V)
                            ch.link(dve.reciprocal(rsum[:, 0, :], O[:, :, HD]))
                            dve.tensor_tensor(otok[:, 0, :].rearrange("p (h e) -> p h e", e=HD), O[:, :, 0:HD],
                                              rsum[:, 0, :].unsqueeze(2).broadcast_to([P, NH, HD]), ALU.mult).then_inc(o_tok.sem, 1)

                    def add(b, n, r):
                        dve.wait_ge(out_ps.sem, out_ps.at(b, 1))
                        src = PS[7][:, DIM:2 * DIM]
                        if causal:
                            if not (isinstance(b, int) and b == 0):
                                dve.wait_ge(q_ps.sem, q_ps.at(b - 1, 1))
                            dve.tensor_copy(aT[:, :, :].rearrange("p c t -> p (c t)"), src).then_inc(x_done.sem, 1)
                            return
                        xb = X[:, bass.ds(b, 1), :].rearrange("p a d -> p (a d)")
                        dve.scalar_tensor_tensor(out=xb, in0=src, scalar=TG[:, tg:tg + 1], in1=xb,
                                                 op0=ALU.mult, op1=ALU.add).then_inc(x_done.sem, 1)

                    def start_of_period(beta):
                        chain[0] = Chain(dve, dve_step, beta - FIRSTP)

                    def end_of_period(beta):
                        chain[0].close()

                    run(dve, dict(score=score, pad_max=pad_max, heads=heads, attended=attended, add=add), start_of_period, end_of_period)

                @block.scalar
                def _(act):
                    act.wait_ge(pool_step.sem, pool_step.at(0, 1))

                    def turn(b, n, r):
                        act.wait_ge(qkT_ps.sem, qkT_ps.at(b, n + 1))
                        dst = (qT, kT)[n // 2][:, r, 4 * (n % 2):4 * (n % 2) + 4, :].rearrange("p n t -> p (n t)")
                        act.copy(dst, PS[5][:, :]).then_inc(qkT_sb.sem, 1)

                    def turn_max(b, n, r):
                        act.wait_ge(mT_ps.sem, mT_ps.at(b, n + 1))
                        act.copy(qM[:, r, 4 * n:4 * n + 4, :].rearrange("p n t -> p (n t)"), PS[5][:, :]).then_inc(mT_sb.sem, 1)

                    def value(b, n, r):
                        act.wait_ge(v_ps.sem, v_ps.at(b, 1))
                        if not (isinstance(b, int) and b < 3):
                            act.wait_ge(av_ps.sem, av_ps.at(b - 3, NS))
                        if seg:
                            src = PS[7][:, :].rearrange("p (a h e) -> p h a e", a=2, h=NH)
                            dst = vs[:, r, :, :].rearrange("p h (a v) -> p h a v", a=2)[:, :, :, 0:HD]
                        else:
                            src = PS[7][:, 0:DIM].rearrange("p (h e) -> p h e", h=NH)
                            dst = vs[:, r, :, 0:HD]
                        act.copy(dst, src).then_inc(v_sb.sem, 1)

                    def score_t(b, u, r):
                        act.wait_ge(st_ps.sem, st_ps.at(b, u + 1))
                        if u >= 2:
                            act.wait_ge(av_ps.sem, av_ps.at(b, u - 1))
                        elif not (isinstance(b, int) and b == 0):
                            act.wait_ge(av_ps.sem, av_ps.at(b - 1, NS + u - 1))
                        act.activation(pT[:, u % 2, :], PS[2 + u % 2][:, :], ACT.Exp, scale=float(HD) ** -0.5).then_inc(p_exp.sem, 1)

                    def turn_out(b, n, r):
                        act.wait_ge(oT_ps.sem, oT_ps.at(b, 1))
                        if not (isinstance(b, int) and b == 0):
                            act.wait_ge(out_ps.sem, out_ps.at(b - 1, 1))
                        act.copy(oT[:, :, :], PS[7][:, 0:DIM].rearrange("p (c t) -> p c t", c=KD)).then_inc(oT_sb.sem, 1)

                    def mod(b, n, r):
                        act.wait_ge(q_ps.sem, q_ps.at(b, 1))
                        act.activation(MODT[:, bass.ds(b * TOK, TOK)], PS[7][0:16, 0:TOK], ACT.Tanh).then_inc(qT_sb.sem, 1)

                    run(act, dict(score_t=score_t, turn=turn, turn_max=turn_max, value=value, turn_out=turn_out, mod=mod))

        def big_attention(s, tg, kind, prefetch=None):
            rms = kind == "rms"
            W = 2 if rms else GROUP
            turns = BATCH // W
            WT = W * TOK
            N = 4 * W
            NKV = N if rms else 16
            NR = 2 * N if rms else 0
            lag = 2 if rms else 1
            END = N + lag + 6
            begin(turns, dve_step=STEPS, act_step=STEPS, copied=1, ctx_loaded=16, v_ps=NKV, v_sb=NKV,
                  q_ps=NR if rms else N, sq_done=NR, rstd_in=NR, rstd_out=NR, qk_pad=NR, qkT_ps=NR,
                  qT_sb=NR if rms else N, s_ps=N, s_sub=N, p_exp=N, p_sum=N, p_norm=N, pT_ps=N, pT_sb=N, av_ps=N, oT_sb=N,
                  out_ps=N, x_done=W)
            if not rms:
                begin(1, pool_step=0, gained=1)
            wq = wk(s, "wq", KD)
            WO = tile("WO", [P, 16 * DIM])
            wo = WO[:, :].rearrange("p (k n) -> p k n", k=16)
            XS, CS = tile("XS", [P, KD, WT]), tile("CS", [P, 1, WT])
            QT, KT, VS = tile("QT", [P, 4096]), tile("KT", [P, 4096]), tile("VS", [P, 4096])
            QP, KP = tile("QP", [P, 1024]), tile("KP", [P, 1024])
            PR, PTS = tile("PR", [P, 2, 512]), tile("PTS", [P, 2, 512])
            QN, SQ, QTS, OTS = (QT[:, n * 1024:(n + 1) * 1024].rearrange("p (a n) -> p a n", a=2) for n in range(4))
            kT = KT[:, :].rearrange("p (b h t) -> p b h t", b=W, t=TOK) if rms else KT[:, :].rearrange("p (h b t) -> p b h t", b=W, t=TOK)
            vs = VS[:, :].rearrange("p (b n) -> p b n", b=W)
            nmax = STAT[:, 0:8].rearrange("p (a h) -> p a h", a=2)
            psums = STAT[:, 16:24].rearrange("p (a h) -> p a h", a=2)
            qvar = STAT[:, 32:40].rearrange("p (a h) -> p a h", a=2)
            qrstd = STAT[:, 48:56].rearrange("p (a h) -> p a h", a=2)
            qsum = STAT[:, 64:72].rearrange("p (a h) -> p a h", a=2)
            mcol = STAT[:, 240:240 + GROUP]
            mraw = QP[0:1, 0:512].bitcast(U8)
            mrow = KP[0:1, :].bitcast(BF16)
            mgroup = QP[0:1, 512:768].bitcast(BF16)
            item_bank = lambda m: (6, 3)[m % 2] if m >= N else (6, 4, 3)[m % 3]
            value_bank = lambda n: n % 3 if rms else n % 4
            probs_bank = lambda t: 2 if rms else 2 + t % 2
            itemT_bank = lambda m: 7 if m >= N else (7, 5)[m % 2]

            with nc.Block() as block:
                @block.sync
                def _(sp):
                    sp.dma_start(WO[:, :], wo_in[int(rms)]).then_inc(wo_loaded[int(rms)].sem, 16)
                    if not rms:
                        sp.dma_start(mraw, mrow_in).then_inc(mask_loaded.sem, 16)
                    if prefetch is not None:
                        load_weights(sp, prefetch)
                    with sp.Fori(0, turns) as i:
                        sp.wait_ge(v_ps.sem, v_ps.at(i, 0))
                        sp.dma_start(CS[:, 0, 0:WT].rearrange("p (b t) -> p b t", t=TOK),
                                     ctxT_in[:, bass.ds(i * W, W), :]).then_inc(ctx_loaded.sem, 16)

                @block.gpsimd
                def _(pool):
                    if not rms:
                        pool.wait_ge(gained.sem, gained.at(0, 1))
                    with pool.Fori(0, turns) as i:
                        pool.wait_ge(q_ps.sem, q_ps.at(i, 0))
                        if not rms:
                            pool.wait_ge(s_ps.sem, s_ps.at(i, 0))
                            pool.tensor_copy(mgroup, mrow[:, bass.ds(i * WT, WT)])
                            pool.tensor_copy(mcol, MCOL[:, bass.ds(i * W, W)])
                        pool.tensor_copy(XS[:, :, 0:WT], XNT[:, :, bass.ds(i * WT, WT)]).then_inc(copied.sem, 1)


                        def item_rstd(m):
                            pool.wait_ge(rstd_in.sem, rstd_in.at(i, m + 1))
                            pool.tensor_tensor(qrstd[:, m % 2, :], qvar[:, m % 2, :], MHALF[:, 0:4],
                                               ALU.pow).then_inc(rstd_out.sem, 1)

                        def normalise(t):
                            pool.wait_ge(p_sum.sem, p_sum.at(i, t + 1))
                            pr = PR[:, t % 2, :].rearrange("p (h c) -> p h c", h=4)
                            pool.tensor_tensor(pr, pr, psums[:, t % 2, :].unsqueeze(2).broadcast_to([P, 4, P]),
                                               ALU.mult).then_inc(p_norm.sem, 1)

                        for m in range(NR - N if rms else 0):
                            item_rstd(m)
                        for t in range(END):
                            if rms and t < N:
                                item_rstd(N + t)
                            if 0 <= t - lag - 1 < N:
                                normalise(t - lag - 1)

                @block.tensor
                def _(pe):
                    pe.wait_ge(w_loaded[s].sem, 32)
                    pe.wait_ge(wo_loaded[int(rms)].sem, 16)

                    def keys_values(i, n):
                        if n >= 4:
                            pe.wait_ge(v_sb.sem, v_sb.at(i, n - 3))
                        if n < 8:
                            ins = pe.matmul(PS[n % 4][:, :], w(s, "wk")[:, n * P:(n + 1) * P], CS[:, 0, :], start=True, stop=True)
                        else:
                            b, half = divmod(n - 8, 2)
                            ins = pe.matmul(PS[n % 4][:, :], CS[:, 0, b * TOK:(b + 1) * TOK],
                                            w(s, "wv")[:, half * 512:(half + 1) * 512], start=True, stop=True)
                        ins.then_inc(v_ps.sem, 1)

                    def values_of(i, n):
                        b, part = divmod(n, 4)
                        if n >= 3:
                            pe.wait_ge(v_sb.sem, v_sb.at(i, n - 2))
                        pe.matmul(PS[value_bank(n)][:, :], CS[:, 0, b * TOK:(b + 1) * TOK], w(s, "wv")[:, part * 512:(part + 1) * 512],
                                  start=True, stop=True).then_inc(v_ps.sem, 1)

                    def item(i, m):
                        b, part = divmod(m % N, 4)
                        tok, cols = slice(b * TOK, (b + 1) * TOK), slice(part * 512, (part + 1) * 512)
                        back = 3 if m < N else 2
                        if m >= back:
                            pe.wait_ge(qk_pad.sem, qk_pad.at(i, m - back + 1))
                        bank = PS[item_bank(m)]
                        if m < N:
                            ins = pe.matmul(bank[:, :], CS[:, 0, tok], w(s, "wk")[:, cols], start=True, stop=True)
                        else:
                            for c in range(KD):
                                ins = pe.matmul(bank[:, :], XS[:, c, tok], wq[:, c, cols], start=(c == 0), stop=(c == KD - 1))
                        ins.then_inc(q_ps.sem, 1)

                    def turn_item(i, m):
                        pe.wait_ge(qk_pad.sem, qk_pad.at(i, m + 1))
                        back = 1 if m > N else 2
                        if m >= back:
                            pe.wait_ge(qT_sb.sem, qT_sb.at(i, m - back + 1))
                        for c in range(4):
                            ins = pe.transpose(PS[itemT_bank(m)][:, c * P:(c + 1) * P], QN[:, m % 2, c * P:(c + 1) * P], IDENT[:, :])
                        ins.then_inc(qkT_ps.sem, 1)

                    def queries(i, t):
                        b, part = divmod(t, 4)
                        if t >= 2:
                            pe.wait_ge(qT_sb.sem, qT_sb.at(i, t - 1))
                        for c in range(4):
                            h = 4 * part + c
                            for k in range(KD):
                                ins = pe.matmul(PS[6 + t % 2][:, c * P:(c + 1) * P], wq[:, k, h * P:(h + 1) * P],
                                                XS[:, k, b * TOK:(b + 1) * TOK], start=(k == 0), stop=(k == KD - 1))
                        ins.then_inc(q_ps.sem, 1)

                    def scores(i, t):
                        b, part = divmod(t, 4)
                        pe.wait_ge(qT_sb.sem, qT_sb.at(i, NR - N + t + 1 if rms else t + 1))
                        if t == 0:
                            pe.wait_ge(v_sb.sem, v_sb.at(i, NKV))
                        if t >= 2:
                            pe.wait_ge(s_sub.sem, s_sub.at(i, t - 1))
                        if not rms:
                            mask = mgroup[0:1, b * TOK:(b + 1) * TOK]
                            pe.matmul(PS[t % 2][:, :].rearrange("p (h c) -> p h c", h=4), ONESB[0:1, :],
                                      mask.unsqueeze(1).broadcast_to([1, 4, TOK]), start=True, stop=False,
                                      skip_group_check=True)
                        for c in range(4):
                            h = 4 * part + c
                            ins = pe.matmul(PS[t % 2][:, c * P:(c + 1) * P], QTS[:, t % 2, c * P:(c + 1) * P],
                                            kT[:, b, h if rms else h // 2, :], start=rms, stop=True, skip_group_check=True)
                        ins.then_inc(s_ps.sem, 1)

                    def turn_probs(i, t):
                        pe.wait_ge(p_norm.sem, p_norm.at(i, t + 1))
                        d = 1 if rms else 2
                        if t >= d:
                            pe.wait_ge(pT_sb.sem, pT_sb.at(i, t - d + 1))
                        for c in range(4):
                            ins = pe.transpose(PS[probs_bank(t)][:, c * P:(c + 1) * P], PR[:, t % 2, c * P:(c + 1) * P], IDENT[:, :])
                        ins.then_inc(pT_ps.sem, 1)

                    def values(i, t):
                        b, part = divmod(t, 4)
                        pe.wait_ge(pT_sb.sem, pT_sb.at(i, t + 1))
                        if t:
                            pe.wait_ge(oT_sb.sem, oT_sb.at(i, t))
                        n = 4 if rms else 2
                        for c in range(n):
                            cols = slice(c * 512 // n, (c + 1) * 512 // n)
                            g = n * part + c
                            ins = pe.matmul(PS[4][:, cols], vs[:, b, g * P:(g + 1) * P], PTS[:, t % 2, cols], start=True, stop=True)
                        ins.then_inc(av_ps.sem, 1)

                    def project_out(i, t):
                        b, part = divmod(t, 4)
                        pe.wait_ge(oT_sb.sem, oT_sb.at(i, t + 1))
                        if part == 0:
                            pe.wait_ge(x_done.sem, x_done.at(i, b))
                        for c in range(4):
                            ins = pe.matmul(PS[5][:, 0:DIM], OTS[:, t % 2, c * P:(c + 1) * P], wo[:, 4 * part + c, :],
                                            start=(part == 0 and c == 0), stop=(part == 3 and c == 3))
                        ins.then_inc(out_ps.sem, 1)

                    with pe.Fori(0, turns) as i:
                        pe.wait_ge(copied.sem, copied.at(i, 1))
                        pe.wait_ge(ctx_loaded.sem, ctx_loaded.at(i, 16))
                        pe.wait_ge(x_done.sem, x_done.at(i, 0))
                        if rms:
                            for m in range(N + 2):
                                if m < N:
                                    item(i, m)
                                    values_of(i, m)
                                if m == N:
                                    item(i, m)
                                if m >= 2:
                                    turn_item(i, m - 2)
                        else:
                            for n in range(NKV):
                                keys_values(i, n)
                        for t in range(END):
                            if rms:
                                if 1 <= t < N:
                                    item(i, N + t)
                                if t < N:
                                    pass
                                if 0 <= t - 1 < N:
                                    turn_item(i, N + t - 1)
                            elif t < N:
                                queries(i, t)
                            if 0 <= t - lag < N:
                                scores(i, t - lag)
                            if 0 <= t - lag - 2 < N:
                                turn_probs(i, t - lag - 2)
                            if 0 <= t - lag - 3 < N:
                                values(i, t - lag - 3)
                            if 0 <= t - lag - 4 < N:
                                project_out(i, t - lag - 4)

                @block.vector
                def _(dve):
                    if not rms:
                        dve.wait_ge(mask_loaded.sem, 16)
                        dve.tensor_scalar(mrow, mraw, 1.0, BIG, ALU.subtract, ALU.mult).then_inc(gained.sem, 1)

                    def norm_item(ch, i, m):
                        dve.wait_ge(sq_done.sem, sq_done.at(i, m + 1))
                        ch.link(dve.tensor_reduce(qsum[:, m % 2, :], SQ[:, m % 2, :].rearrange("p (h c) -> p h c", h=4), AX, ALU.add))
                        dve.tensor_scalar(qvar[:, m % 2, :], qsum[:, m % 2, :], 1.0 / P, 1e-5, ALU.mult, ALU.add).then_inc(rstd_in.sem, 1)

                    def scale_item(ch, i, m):
                        dve.wait_ge(rstd_out.sem, rstd_out.at(i, m + 1))
                        if m >= 2:
                            dve.wait_ge(qkT_ps.sem, qkT_ps.at(i, m - 1))
                        src = PS[item_bank(m)][:, :].rearrange("p (h c) -> p h c", h=4)
                        dve.tensor_tensor(QN[:, m % 2, :].rearrange("p (h c) -> p h c", h=4), src,
                                          qrstd[:, m % 2, :].unsqueeze(2).broadcast_to([P, 4, P]), ALU.mult).then_inc(qk_pad.sem, 1)

                    def subtract_max(ch, i, t):
                        S = PS[t % 2][:, :].rearrange("p (h c) -> p h c", h=4)
                        dve.wait_ge(s_ps.sem, s_ps.at(i, t + 1))
                        ch.link(dve.tensor_reduce(nmax[:, t % 2, :], S, AX, ALU.max, negate=True))
                        if t >= 2:
                            dve.wait_ge(pT_ps.sem, pT_ps.at(i, t - 1))
                        dve.tensor_tensor(PR[:, t % 2, :].rearrange("p (h c) -> p h c", h=4), S,
                                          nmax[:, t % 2, :].unsqueeze(2).broadcast_to([P, 4, P]), ALU.add).then_inc(s_sub.sem, 1)

                    def sums(ch, i, t):
                        pr = PR[:, t % 2, :].rearrange("p (h c) -> p h c", h=4)
                        psum_ = psums[:, t % 2, :]
                        dve.wait_ge(p_exp.sem, p_exp.at(i, t + 1))
                        ch.link(dve.tensor_reduce(psum_, pr, AX, ALU.add))
                        dve.reciprocal(psum_, psum_).then_inc(p_sum.sem, 1)

                    with dve.Fori(0, turns) as i:
                        ch = Chain(dve, dve_step, i)
                        if rms:
                            norm_item(ch, i, 0)
                            for m in range(N):
                                if m + 1 < N:
                                    norm_item(ch, i, m + 1)
                                scale_item(ch, i, m)
                        for t in range(END):
                            b, late = divmod(t - lag - 5 - 3, 4)
                            if late == 0 and 0 <= b < W:
                                dve.wait_ge(out_ps.sem, out_ps.at(i, 4 * b + 4))
                                xb = X[:, bass.ds(i * W + b, 1), :].rearrange("p a d -> p (a d)")
                                dve.scalar_tensor_tensor(out=xb, in0=PS[5][:, 0:DIM], scalar=TG[:, tg:tg + 1], in1=xb,
                                                         op0=ALU.mult, op1=ALU.add).then_inc(x_done.sem, 1)
                            if rms and t < N:
                                norm_item(ch, i, N + t)
                            if 0 <= t - lag < N:
                                subtract_max(ch, i, t - lag)
                            if rms and t < N:
                                scale_item(ch, i, N + t)
                            if 0 <= t - lag - 1 < N:
                                sums(ch, i, t - lag - 1)
                        ch.close()

                @block.scalar
                def _(act):
                    if rms:
                        act.wait_ge(w_loaded[s].sem, 32)

                    def square_item(i, m):
                        act.wait_ge(q_ps.sem, q_ps.at(i, m + 1))
                        if m >= 2:
                            act.wait_ge(rstd_in.sem, rstd_in.at(i, m - 1))
                        act.activation(SQ[:, m % 2, :], PS[item_bank(m)][:, :], ACT.Square).then_inc(sq_done.sem, 1)

                    def item_out(i, m):
                        act.wait_ge(qkT_ps.sem, qkT_ps.at(i, m + 1))
                        src = PS[itemT_bank(m)][:, :]
                        if m < N:
                            b, part = divmod(m, 4)
                            dst = kT[:, b, 4 * part:4 * part + 4, :]
                            src = src.rearrange("p (h t) -> p h t", h=4)
                        else:
                            if m >= N + 2:
                                act.wait_ge(s_ps.sem, s_ps.at(i, m - N - 1))
                            dst = QTS[:, m % 2, :]
                        act.activation(dst, src, ACT.Copy, scale=w(s, "gk" if m < N else "gq")).then_inc(qT_sb.sem, 1)

                    def keys_values_out(i, n):
                        act.wait_ge(v_ps.sem, v_ps.at(i, n + 1))
                        if rms:
                            b, part = divmod(n, 4)
                            act.copy(vs[:, b, part * 512:(part + 1) * 512], PS[value_bank(n)][:, :]).then_inc(v_sb.sem, 1)
                        elif n < 8:
                            act.copy(kT[:, :, n, :], PS[n % 4][:, :].rearrange("p (b t) -> p b t", b=W)).then_inc(v_sb.sem, 1)
                        else:
                            b, half = divmod(n - 8, 2)
                            act.activation(vs[:, b, half * 512:(half + 1) * 512], PS[n % 4][:, :], ACT.Copy,
                                           scale=mcol[:, b:b + 1]).then_inc(v_sb.sem, 1)

                    def queries_out(i, t):
                        act.wait_ge(q_ps.sem, q_ps.at(i, t + 1))
                        if t >= 2:
                            act.wait_ge(s_ps.sem, s_ps.at(i, t - 1))
                        act.copy(QTS[:, t % 2, :], PS[6 + t % 2][:, :]).then_inc(qT_sb.sem, 1)

                    def exponent(i, t):
                        act.wait_ge(s_sub.sem, s_sub.at(i, t + 1))
                        act.activation(PR[:, t % 2, :], PR[:, t % 2, :], ACT.Exp, scale=float(P) ** -0.5).then_inc(p_exp.sem, 1)

                    def probs_out(i, t):
                        act.wait_ge(pT_ps.sem, pT_ps.at(i, t + 1))
                        if t >= 2:
                            act.wait_ge(av_ps.sem, av_ps.at(i, t - 1))
                        act.copy(PTS[:, t % 2, :], PS[probs_bank(t)][:, :]).then_inc(pT_sb.sem, 1)

                    def attended(i, t):
                        act.wait_ge(av_ps.sem, av_ps.at(i, t + 1))
                        if t >= 2:
                            act.wait_ge(out_ps.sem, out_ps.at(i, t - 1))
                        act.copy(OTS[:, t % 2, :], PS[4][:, :]).then_inc(oT_sb.sem, 1)

                    with act.Fori(0, turns) as i:
                        if rms:
                            for m in range(N + 2):
                                if m < N:
                                    square_item(i, m)
                                    keys_values_out(i, m)
                                if m >= 2:
                                    item_out(i, m - 2)
                        else:
                            for n in range(NKV):
                                keys_values_out(i, n)
                        for t in range(END):
                            if rms and t < N:
                                square_item(i, N + t)
                            if not rms and t < N:
                                queries_out(i, t)
                            if rms and 0 <= t - 1 < N:
                                item_out(i, N + t - 1)
                            if 0 <= t - lag < N:
                                exponent(i, t - lag)
                            if 0 <= t - lag - 2 < N:
                                probs_out(i, t - lag - 2)
                            if 0 <= t - lag - 3 < N:
                                attended(i, t - lag - 3)
                        act.sem_inc(act_step.sem, STEPS)

        def ffn_block(s, kind, pairs, tg=None, MODT=None):
            mod, moe = kind == "mod", kind == "moe"
            NF = UH // P
            T = 2 * TURNS
            HALF = UNIT // 2
            begin(pairs, dve_step=STEPS, gu_ps=T * NF, silu_done=T * NF, h_done=T * NF, down_ps=T * NF, x_done=T)
            begin(1, w_hi=4 * pairs, w_lo=4 * pairs, x_hi=1 + T * pairs, x_lo=1 + T * pairs, q_ps=TURNS * mod,
                  qk_pad=mod, raw_loaded0=16 * (pairs - 1), raw_loaded1=16 * (pairs - 1))
            WHI, WLO = tile("WHI", [P, 2, UNIT], F32R), tile("WLO", [P, 2, UNIT], F32R)
            XHI, XLO = tile("XHI", [P, 2, KD, GT], F32R), tile("XLO", [P, 2, KD, GT], F32R)
            H = tile("H", [P, 2, GT])
            HHI, HLO = tile("HHI", [P, 2, GT], F32R), tile("HLO", [P, 2, GT], F32R)
            scale = tile("scale", [P, 2, BATCH]) if moe else None
            raw = [w(s, "unit0"), w(s, "unit1")]

            def gate_or_up(tile_, a, which, k, f):
                at = which * KD * UH + k * UH + f * P
                return tile_[:, a, at:at + P]

            def down(tile_, a, f):
                at = 2 * KD * UH + f * DIM
                return tile_[:, a, at:at + DIM]

            def all_pairs(eng, body):
                if pairs == 1:
                    body(0)
                else:
                    with eng.Fori(0, pairs) as q:
                        body(q)

            def split_ahead(eng, first, x_part, w_part, per_step=None):
                def body(q, more):
                    for t in range(T):
                        a, g = divmod(t, TURNS)
                        for f in range(NF):
                            if per_step:
                                per_step(q, NF * t + f)
                            if f == 1:
                                x_part(q, t + 1)
                            if f == 2 and g in (1, 2) and (a == 0 or more):
                                w_part(q, a, g - 1)
                first()
                if pairs > 1:
                    with eng.Fori(0, pairs - 1) as q:
                        body(q, True)
                body(pairs - 1, False)

            with nc.Block() as block:
                if moe:
                    @block.sync
                    def _(sp):
                        with sp.Fori(1, pairs) as q:
                            for a in range(2):
                                sp.wait_ge(w_lo.sem, w_lo.at(0, 4 * q + (2 * a - 2)))
                                sp.dma_start(raw[a], experts_in[:, bass.ds(2 * q + (a - 2), 1), :].rearrange("p a n -> p (a n)"))\
                                    .then_inc(raw_loaded[a].sem, 16)

                @block.tensor
                def _(pe):
                    if mod:
                        for g in range(TURNS):
                            for k in range(KD):
                                ins = pe.matmul(PS[4 + g][0:16, :], wk(s, "a2", KD)[:, k, :], XNT[:, k, g * GT:(g + 1) * GT],
                                                start=(k == 0), stop=(k == KD - 1))
                            ins.then_inc(q_ps.sem, 1)
                        pe.wait_ge(qk_pad.sem, qk_pad.at(0, 1))

                    def gate_up(q, n):
                        t, f = divmod(n, NF)
                        a, g = divmod(t, TURNS)
                        if n >= 2:
                            pe.wait_ge(h_done.sem, h_done.at(q, n - 1))
                        for which in range(2):
                            bank = PS[2 * which + n % 2]
                            if mod and which == 0:
                                at = a * UH + f * P
                                pe.matmul(bank[:, :], w(s, "bm")[0:16, at:at + P], MODT[:, g * GT:(g + 1) * GT],
                                          start=True, stop=False)
                            for k in range(KD):
                                for m, (wt, xt) in enumerate(((WHI, XHI), (WLO, XHI), (WHI, XLO))):
                                    ins = pe.matmul(bank[:, :], gate_or_up(wt, a, which, k, f), xt[:, t % 2, k, :],
                                                    start=(k == 0 and m == 0 and not (mod and which == 0)),
                                                    stop=(k == KD - 1 and m == 2))
                        ins.then_inc(gu_ps.sem, 1)

                    def project_down(q, n):
                        t, f = divmod(n, NF)
                        a = t // TURNS
                        pe.wait_ge(h_done.sem, h_done.at(q, n + 1))
                        if f == 0:
                            pe.wait_ge(x_done.sem, x_done.at(q, max(t - 1, 0)))
                        for b in range(GROUP):
                            bank = PS[4 + 2 * (t % 2) + b // 2]
                            tok = slice(b * TOK, (b + 1) * TOK)
                            for m, (ht, wt) in enumerate(((HHI, WHI), (HLO, WHI), (HHI, WLO))):
                                ins = pe.matmul(bank[:, b % 2 * DIM:(b % 2 + 1) * DIM], ht[:, n % 2, tok], down(wt, a, f),
                                                start=(f == 0 and b % 2 == 0 and m == 0), stop=(f == NF - 1 and m == 2),
                                                skip_group_check=True)
                        ins.then_inc(down_ps.sem, 1)

                    def pair(q):
                        for n in range(T * NF):
                            if n % NF == 0:
                                pe.wait_ge(x_lo.sem, x_lo.at(0, T * q + (n // NF + 1)))
                                if n % (T * NF // 2) == 0:
                                    pe.wait_ge(w_lo.sem, w_lo.at(0, 4 * q + (2 * (n // (T * NF // 2)) + 2)))
                            gate_up(q, n)
                            if n:
                                project_down(q, n - 1)
                        project_down(q, T * NF - 1)

                    all_pairs(pe, pair)

                @block.scalar
                def _(act):
                    act.wait_ge(w_loaded[s].sem, 32)

                    def w_high(a, j):
                        cols = slice(j * HALF, (j + 1) * HALF)
                        act.copy(WHI[:, a, cols], raw[a][:, cols]).then_inc(w_hi.sem, 1)

                    def x_high(t):
                        g = t % TURNS
                        act.copy(XHI[:, t % 2, :, :], XNT[:, :, g * GT:(g + 1) * GT]).then_inc(x_hi.sem, 1)

                    def first():
                        w_high(0, 0)
                        x_high(0)
                        w_high(0, 1)

                    def x_part(q, t):
                        act.wait_ge(gu_ps.sem, gu_ps.at(q, NF * (t - 1)))
                        x_high(t)

                    def w_part(q, a, j):
                        if moe:
                            act.wait_ge(raw_loaded[1 - a].sem, raw_loaded[1 - a].at(0, 16 * (q + a)))
                        act.wait_ge(down_ps.sem, down_ps.at(q, a * T * NF // 2))
                        w_high(1 - a, j)

                    def silu(q, n):
                        act.wait_ge(gu_ps.sem, gu_ps.at(q, n + 1))
                        if n >= 2:
                            act.wait_ge(h_done.sem, h_done.at(q, n - 1))
                        act.activation(H[:, n % 2, :], PS[n % 2][:, :], ACT.Silu).then_inc(silu_done.sem, 1)

                    split_ahead(act, first, x_part, w_part, silu)

                @block.gpsimd
                def _(pool):
                    def w_low(count_, a, j):
                        pool.wait_ge(w_hi.sem, w_hi.at(0, count_))
                        cols = slice(j * HALF, (j + 1) * HALF)
                        pool.tensor_tensor(WLO[:, a, cols], raw[a][:, cols], WHI[:, a, cols].bitcast(F32),
                                           ALU.subtract).then_inc(w_lo.sem, 1)

                    def x_low(count_, t):
                        pool.wait_ge(x_hi.sem, x_hi.at(0, count_))
                        g = t % TURNS
                        pool.tensor_tensor(XLO[:, t % 2, :, :], XNT[:, :, g * GT:(g + 1) * GT],
                                           XHI[:, t % 2, :, :].bitcast(F32), ALU.subtract).then_inc(x_lo.sem, 1)

                    def first():
                        w_low(1, 0, 0)
                        x_low(1, 0)
                        w_low(2, 0, 1)

                    split_ahead(pool, first, lambda q, t: x_low(T * q + (t + 1), t),
                                lambda q, a, j: w_low(4 * q + (2 * a + 3 + j), 1 - a, j))

                @block.vector
                def _(dve):
                    if mod:
                        for g in range(TURNS):
                            dve.wait_ge(q_ps.sem, q_ps.at(0, g + 1))
                            m = MODT[:, g * GT:(g + 1) * GT]
                            ins = dve.scalar_tensor_tensor(out=m, in0=PS[4 + g][0:16, :], scalar=0.1, in1=m,
                                                           op0=ALU.mult, op1=ALU.mult)
                        ins.then_inc(qk_pad.sem, 1)

                    def hidden(ch, q, n):
                        dve.wait_ge(silu_done.sem, silu_done.at(q, n + 1))
                        h = H[:, n % 2, :]
                        ch.link(dve.tensor_tensor(h, h, PS[2 + n % 2][:, :], ALU.mult))
                        if n >= 2:
                            dve.wait_ge(down_ps.sem, down_ps.at(q, n - 1))
                        ch.link(dve.tensor_copy(HHI[:, n % 2, :], h))
                        dve.tensor_tensor(HLO[:, n % 2, :], h, HHI[:, n % 2, :].bitcast(F32), ALU.subtract).then_inc(h_done.sem, 1)

                    def combine(ch, q, t):
                        a, g = divmod(t, TURNS)
                        dve.wait_ge(down_ps.sem, down_ps.at(q, NF * (t + 1)))
                        dve.wait_ge(x_done.sem, x_done.at(q, t))
                        for b in range(GROUP):
                            xb = X[:, g * GROUP + b, :]
                            bank = PS[4 + 2 * (t % 2) + b // 2]
                            k = g * GROUP + b
                            ins = dve.scalar_tensor_tensor(out=xb, in0=bank[:, b % 2 * DIM:(b % 2 + 1) * DIM],
                                                           scalar=scale[:, a, k:k + 1] if moe else TG[:, tg:tg + 1],
                                                           in1=xb, op0=ALU.mult, op1=ALU.add)
                            if b < GROUP - 1:
                                ch.step(ins)
                        ins.then_inc(x_done.sem, 1)

                    def pair(q):
                        ch = Chain(dve, dve_step, q)
                        if moe:
                            dve.wait_ge(x_done.sem, x_done.at(q, 0))
                            for a in range(2):
                                ch.step(dve.tensor_copy(scale[:, a, :], RW[:, :, bass.ds(2 * q + a, 1)].rearrange("p b e -> p (b e)")))
                            ch.settle()
                        for n in range(T * NF):
                            hidden(ch, q, n)
                            if n % NF == 1 and n > NF:
                                combine(ch, q, n // NF - 1)
                        combine(ch, q, T - 1)
                        ch.close()

                    all_pairs(dve, pair)

        def quant_block(s, tg, prefetch=None):
            begin(TURNS, dve_step=STEPS, act_step=STEPS, copied=1, gu_ps=GROUP, silu_done=GROUP, h_done=GROUP,
                  o_tok=GROUP, pT_ps=GROUP, pT_sb=GROUP, down_ps=GROUP, x_done=GROUP, rstd_in=1)
            begin(1, s_ps=1, s_sub=1, gained=1, p_exp=1)
            NCH = HID0P // P
            WB = tile("WB", [P, WIDTH[s]], BF16)
            XS = tile("XS", [P, KD, GT])
            w1 = WB[:, 0:KD * HID0].rearrange("p (k n) -> p k n", k=KD)
            w3 = WB[:, KD * HID0:2 * KD * HID0].rearrange("p (k n) -> p k n", k=KD)
            w2 = WB[:, 2 * KD * HID0:].rearrange("p (k n) -> p k n", k=NCH)
            XQT = XNT[:, 0, :].bitcast(BF16).rearrange("p (k t) -> p k t", k=KD)
            XSB = XS[:, 0, :].bitcast(BF16).rearrange("p (k t) -> p k t", k=KD)
            SG = tile("SG", [P, 2, HID0])
            H, Y = tile("H", [P, HID0])[:, :], tile("Y", [P, HID0])[:, :]
            HQ, HT = tile("HQ", [P, 2, HID0P], BF16), tile("HT", [P, 2, HID0P], BF16)
            halves = ((0, 512), (512, HID0))
            wsum, wmean, wstep = STAT[:, 0:3], STAT[:, 4:7], STAT[:, 8:11]
            cg, cu = STAT[:, 16:16 + GROUP], STAT[:, 24:24 + GROUP]
            hmax, hinv, hout = STAT[:, 32:33], STAT[:, 34:35], STAT[:, 36:38]
            parts = (("w1", 0, KD * HID0), ("w3", KD * HID0, 2 * KD * HID0), ("w2", 2 * KD * HID0, WIDTH[s]))
            with nc.Block() as block:
                @block.sync
                def _(sp):
                    if prefetch is not None:
                        load_weights(sp, prefetch)

                @block.gpsimd
                def _(pool):
                    with pool.Fori(0, TURNS) as i:
                        pool.wait_ge(gu_ps.sem, gu_ps.at(i, 0))
                        pool.tensor_copy(XSB[:, :, :], XQT[:, :, bass.ds(i * GT, GT)]).then_inc(copied.sem, 1)

                @block.tensor
                def _(pe):
                    pe.wait_ge(s_ps.sem, s_ps.at(0, 1))
                    pe.matmul(PS[7][:, 0:3], ONES[:, :], wsum, start=True, stop=True).then_inc(s_sub.sem, 1)
                    pe.wait_ge(gained.sem, gained.at(0, 1))

                    def gate_up(i, b):
                        if b:
                            pe.wait_ge(h_done.sem, h_done.at(i, b))
                        tok = slice(b * TOK, (b + 1) * TOK)
                        for n, m in enumerate((w1, w3)):
                            for c, (lo, hi) in enumerate(halves):
                                for k in range(KD):
                                    ins = pe.matmul(PS[2 * n + c][:, 0:hi - lo], XSB[:, k, tok], m[:, k, lo:hi],
                                                    start=(k == 0), stop=(k == KD - 1))
                        ins.then_inc(gu_ps.sem, 1)

                    def turn_hidden(i, b):
                        pe.wait_ge(o_tok.sem, o_tok.at(i, b + 1))
                        pe.wait_ge(pT_sb.sem, pT_sb.at(i, b))
                        for c in range(NCH):
                            ins = pe.transpose(PSB[4][:, c * P:(c + 1) * P], HQ[:, b % 2, c * P:(c + 1) * P], IDENTB[:, :])
                        ins.then_inc(pT_ps.sem, 1)

                    def project_down(i, b):
                        pe.wait_ge(pT_sb.sem, pT_sb.at(i, b + 1))
                        pe.wait_ge(x_done.sem, x_done.at(i, b))
                        for c in range(NCH):
                            ins = pe.matmul(PS[5][:, 0:DIM], HT[:, b % 2, c * P:(c + 1) * P], w2[:, c, :],
                                            start=(c == 0), stop=(c == NCH - 1))
                        ins.then_inc(down_ps.sem, 1)

                    with pe.Fori(0, TURNS) as i:
                        pe.wait_ge(copied.sem, copied.at(i, 1))
                        gate_up(i, 0)
                        for b in range(GROUP):
                            if b + 1 < GROUP:
                                gate_up(i, b + 1)
                            turn_hidden(i, b)
                            project_down(i, b)

                @block.scalar
                def _(act):
                    with act.Fori(0, TURNS) as i:
                        act.wait_ge(rstd_in.sem, rstd_in.at(i, 1))
                        ch = Chain(act, act_step, i)

                        def hidden_out(b):
                            act.wait_ge(pT_ps.sem, pT_ps.at(i, b + 1))
                            act.copy(HT[:, b % 2, :], PSB[4][:, 0:HID0P]).then_inc(pT_sb.sem, 1)

                        for b in range(GROUP):
                            act.wait_ge(gu_ps.sem, gu_ps.at(i, b + 1))
                            for c, (lo, hi) in enumerate(halves):
                                ins = act.activation(SG[:, b % 2, lo:hi], PS[c][:, 0:hi - lo], ACT.Silu, scale=cg[:, b:b + 1])
                                if c == 0:
                                    ch.step(ins)
                            ins.then_inc(silu_done.sem, 1)
                            if b:
                                hidden_out(b - 1)
                        hidden_out(GROUP - 1)
                        ch.close()

                @block.vector
                def _(dve):
                    dve.wait_ge(w_loaded[s].sem, 32)
                    for n, (_, lo, hi) in enumerate(parts):
                        ins = dve.tensor_reduce(wsum[:, n:n + 1], WREG[s % 2][:, lo:hi], AX, ALU.add, apply_absolute_value=True)
                    ins.then_inc(s_ps.sem, 1)
                    dve.wait_ge(s_sub.sem, s_sub.at(0, 1))
                    ch = Chain(dve, p_exp)
                    dve.tensor_scalar(wmean, PS[7][:, 0:3], 1.0 / (HID0 * DIM), 1e-5, ALU.mult, ALU.max).then_inc(quant_step.sem, 1)
                    dve.wait_ge(quant_step.sem, 1)
                    dve.reciprocal(wstep, wmean).then_inc(quant_step.sem, 1)
                    dve.wait_ge(quant_step.sem, 2)
                    for n, (_, lo, hi) in enumerate(parts):
                        m = WREG[s % 2][:, lo:hi]
                        ins = dve.tensor_scalar(m, m, wstep[:, n:n + 1], MAGIC, ALU.mult, ALU.add)
                    ins.then_inc(quant_step.sem, 1)
                    dve.wait_ge(quant_step.sem, 3)
                    m = WREG[s % 2][:, 0:WIDTH[s]]
                    dve.tensor_scalar(m, m, MAGIC + 1.0, MAGIC - 1.0, ALU.min, ALU.max).then_inc(quant_step.sem, 1)
                    dve.memset(HQ[:, :, :], 0.0)
                    dve.wait_ge(quant_step.sem, 4)
                    dve.tensor_scalar(WB[:, :], m, MAGIC, None, ALU.subtract).then_inc(gained.sem, 1)

                    def hidden(ch, i, b):
                        dve.wait_ge(silu_done.sem, silu_done.at(i, b + 1))
                        for c, (lo, hi) in enumerate(halves):
                            ins = dve.scalar_tensor_tensor(out=H[:, lo:hi], in0=PS[2 + c][:, 0:hi - lo], scalar=cu[:, b:b + 1],
                                                           in1=SG[:, b % 2, lo:hi], op0=ALU.mult, op1=ALU.mult)
                            if c == 0:
                                ch.step(ins)
                        ins.then_inc(h_done.sem, 1)
                        ch.settle()
                        dve.wait_ge(h_done.sem, h_done.at(i, b + 1))
                        ch.link(dve.tensor_reduce(hmax, H, AX, ALU.max, apply_absolute_value=True))
                        ch.link(dve.tensor_scalar(hmax, hmax, 1e-5, None, ALU.max))
                        ch.step(dve.reciprocal(hinv, hmax))
                        ch.step(dve.tensor_scalar(hout[:, b % 2:b % 2 + 1], hmax, 1.0 / 127.0, wmean[:, 2:3], ALU.mult, ALU.mult))
                        ch.settle()
                        ch.step(dve.tensor_scalar(hinv, hinv, 127.0, None, ALU.mult))
                        ch.step(dve.tensor_scalar(hout[:, b % 2:b % 2 + 1], hout[:, b % 2:b % 2 + 1], TG[:, tg:tg + 1], None, ALU.mult))
                        ch.settle()
                        ch.link(dve.tensor_scalar(Y, H, hinv, MAGIC, ALU.mult, ALU.add))
                        ch.link(dve.tensor_scalar(Y, Y, MAGIC + 127.0, MAGIC - 128.0, ALU.min, ALU.max))
                        if b >= 2:
                            dve.wait_ge(pT_ps.sem, pT_ps.at(i, b - 1))
                        dve.tensor_scalar(HQ[:, b % 2, 0:HID0], Y, MAGIC, None, ALU.subtract).then_inc(o_tok.sem, 1)

                    def add_out(i, b):
                        dve.wait_ge(down_ps.sem, down_ps.at(i, b + 1))
                        xb = X[:, bass.ds(i * GROUP + b, 1), :].rearrange("p a d -> p (a d)")
                        dve.scalar_tensor_tensor(out=xb, in0=PS[5][:, 0:DIM], scalar=hout[:, b % 2:b % 2 + 1], in1=xb,
                                                 op0=ALU.mult, op1=ALU.add).then_inc(x_done.sem, 1)

                    with dve.Fori(0, TURNS) as i:
                        ch = Chain(dve, dve_step, i)
                        ch.step(dve.tensor_scalar(cu, AQ[:, bass.ds(i * GROUP, GROUP)], wmean[:, 1:2], None, ALU.mult))
                        dve.tensor_scalar(cg, AQ[:, bass.ds(i * GROUP, GROUP)], wmean[:, 0:1], None, ALU.mult).then_inc(rstd_in.sem, 1)
                        for b in range(GROUP):
                            hidden(ch, i, b)
                            if b:
                                add_out(i, b - 1)
                        add_out(i, GROUP - 1)
                        ch.close()
                    dve.sem_inc(p_exp.sem, 1)

        def router_block(s, tg, prefetch=None):
            begin(TURNS, copied=1, s_ps=1, s_sub=1)
            begin(1, dve_step=STEPS, p_exp=1)
            rt = wk(s, "router", KD)
            BE = BATCH * EXPERTS
            work, XS = tile("work", [P, 7 * BE]), tile("XS", [P, KD, GT])
            area = lambda n, c=BE: work[:, n * BE:n * BE + c]
            three = lambda n: area(n).rearrange("p (b e) -> p b e", e=EXPERTS)
            eq, run, first1, rest, first2, wide = (three(n) for n in range(6))
            m1, m2, ex, s1, s2 = (area(6)[:, n * BATCH:(n + 1) * BATCH] for n in range(5))
            L = RW[:, :, 2:2 + EXPERTS]

            def wide_of(v):
                return v.unsqueeze(2).broadcast_to([P, BATCH, EXPERTS])

            with nc.Block() as block:
                @block.sync
                def _(sp):
                    if prefetch is not None:
                        load_weights(sp, prefetch)

                @block.gpsimd
                def _(pool):
                    with pool.Fori(0, TURNS) as i:
                        pool.wait_ge(s_ps.sem, s_ps.at(i, 0))
                        pool.tensor_copy(XS[:, :, :], XNT[:, :, bass.ds(i * GT, GT)]).then_inc(copied.sem, 1)

                @block.tensor
                def _(pe):
                    pe.wait_ge(w_loaded[s].sem, 32)
                    with pe.Fori(0, TURNS) as i:
                        pe.wait_ge(copied.sem, copied.at(i, 1))
                        pe.wait_ge(s_sub.sem, s_sub.at(i, 0))
                        for b in range(GROUP):
                            for k in range(KD):
                                ins = pe.matmul(PS[0][:, b * EXPERTS:(b + 1) * EXPERTS], XS[:, k, b * TOK:(b + 1) * TOK],
                                                rt[:, k, :], start=(k == 0), stop=(k == KD - 1))
                        ins.then_inc(s_ps.sem, 1)

                @block.vector
                def _(dve):
                    with dve.Fori(0, TURNS) as i:
                        dve.wait_ge(s_ps.sem, s_ps.at(i, 1))
                        dve.tensor_copy(RW[:, bass.ds(i * GROUP, GROUP), 2:2 + EXPERTS], PS[0][:, 0:GROUP * EXPERTS].rearrange(
                            "p (b e) -> p b e", e=EXPERTS)).then_inc(s_sub.sem, 1)
                    dve.wait_ge(s_sub.sem, s_sub.at(TURNS, 0))
                    ch = Chain(dve, dve_step)

                    def first_of(logits, top, dst):
                        ch.link(dve.tensor_reduce(top, logits, AX, ALU.max))
                        ch.link(dve.tensor_tensor(eq, logits, wide_of(top), ALU.is_equal))
                        ch.link(dve.tensor_copy(run[:, :, 0:1], eq[:, :, 0:1]))
                        for e in range(1, EXPERTS):
                            ch.link(dve.tensor_tensor(run[:, :, e:e + 1], run[:, :, e - 1:e], eq[:, :, e:e + 1], ALU.add))
                        ch.link(dve.tensor_scalar(run, run, 1.0, None, ALU.is_le))
                        ch.link(dve.tensor_tensor(dst, run, eq, ALU.mult))

                    ch.step(dve.tensor_scalar(RW[:, :, 0:2], ONES[:, 0:2 * BATCH].rearrange("p (b e) -> p b e", e=2),
                                              TG[:, tg:tg + 1], None, ALU.mult))
                    first_of(L, m1, first1)
                    ch.link(dve.scalar_tensor_tensor(out=rest, in0=first1, scalar=-BIG, in1=L, op0=ALU.mult, op1=ALU.add))
                    first_of(rest, m2, first2)
                    dve.tensor_tensor(ex, m2, m1, ALU.subtract).then_inc(quant_step.sem, 1)
                    dve.wait_ge(p_exp.sem, p_exp.at(0, 1))
                    ch.link(dve.tensor_scalar(s1, ex, 1.0, None, ALU.add))
                    ch.link(dve.reciprocal(s1, s1))
                    ch.link(dve.tensor_scalar(s1, s1, TG[:, tg:tg + 1], None, ALU.mult))
                    ch.link(dve.tensor_tensor(s2, s1, ex, ALU.mult))
                    ch.step(dve.tensor_tensor(first1, first1, wide_of(s1), ALU.mult))
                    ch.step(dve.tensor_tensor(first2, first2, wide_of(s2), ALU.mult))
                    ch.settle()
                    ch.link(dve.tensor_tensor(L, first1, first2, ALU.add))
                    ch.close()

                @block.scalar
                def _(act):
                    act.wait_ge(quant_step.sem, 5)
                    act.activation(ex, ex, ACT.Exp).then_inc(p_exp.sem, 1)

        def last_block():
            with nc.Block() as block:
                @block.sync
                def _(sp):
                    sp.dma_start(out, X[:, :, :]).then_inc(stored.sem, 16)
                    sp.wait_ge(stored.sem, 16)

        with ExitStack() as area:
            scope[0] = area
            first_block()
        held = ExitStack()
        keep = []

        def modulation(first):
            if first:
                keep.append(held.enter_context(nc.sbuf_tensor("MODT", [16, BATCH * TOK], F32)))
            return keep[0]

        program = [
            lambda: norm_block(1),
            lambda: small_attention(0, 0, 32, 8, "rope"),
            lambda: norm_block(2, "quant"),
            lambda: quant_block(1, 4),
            lambda: norm_block(3),
            lambda: big_attention(2, 1, "mask"),
            lambda: norm_block(4, "rms", 5),
            lambda: small_attention(3, None, 16, 16, "causal", MODT=modulation(True)),
            lambda: ffn_block(3, "mod", 1, 5, MODT=modulation(False)),
            lambda: norm_block(5),
            lambda: big_attention(4, 2, "rms"),
            lambda: norm_block(6),
            lambda: ffn_block(5, "plain", 1, 6),
            lambda: norm_block(7),
            lambda: small_attention(6, 3, 16, 16, "dca"),
            lambda: norm_block(None),
            lambda: router_block(7, 7),
            lambda: ffn_block(7, "moe", (2 + EXPERTS) // 2),
        ]
        for n, part in enumerate(program):
            if n < stop:
                with ExitStack() as area:
                    scope[0], scope[1] = area, n + 1
                    part()
                if n == MOD_END:
                    held.close()
        held.close()
        last_block()


def rows(m):
    k, n = m.shape
    return m.reshape(k // P, P, n).transpose(1, 0, 2).reshape(P, -1)


def padded(m, k):
    z = np.zeros((k,) + m.shape[1:], m.dtype)
    z[:m.shape[0]] = m
    return z


def everywhere(v):
    return np.broadcast_to(v, (P, v.size))


def units(gate, up, down):
    return [np.concatenate([rows(gate[:, u:u + UH]), rows(up[:, u:u + UH]), rows(down[u:u + UH])], 1)
            for u in range(0, gate.shape[1], UH)]


def lay_out(i):
    c = lambda n: np.asarray(i[n])
    kv = c("L0_xattn_Wkv")
    kvd = c("L3_xattn_Wkv_dca")
    kv3 = [c("L3_xattn_Wk"), c("L3_xattn_Wv")]
    cat = np.concatenate(kv3, 1).reshape(CDIM, 16, 2, 16)
    bcat = np.concatenate([c("L3_xattn_bk"), c("L3_xattn_bv")]).reshape(16, 2, 16)
    l3k, l3v = cat[:, :, 0].reshape(CDIM, DIM), cat[:, :, 1].reshape(CDIM, DIM)
    b3k, b3v = bcat[:, 0].reshape(DIM), bcat[:, 1].reshape(DIM)

    heads = lambda n: everywhere(np.tile(c(f"L3_xattn_{n}"), 16))
    rows_of = lambda a, b: np.concatenate([a[:MAIN], b[MAIN:]], 0)
    segc = np.zeros((P, 4), np.float32)
    segc[:MAIN, 0:2] = 1
    segc[MAIN:, 2:4] = 1
    col = lambda v: v.reshape(-1, P).T
    return [
        [rows(c("L0_xattn_Wq")), kv[:, :DIM], kv[:, DIM:], rows(c("L0_xattn_Wout")), everywhere(c("L0_xattn_bout"))],
        [rows(c("L0_ffn_w1").T), rows(c("L0_ffn_w3").T), rows(padded(c("L0_ffn_w2").T, HID0P))],
        [rows(c("L1_xattn_Wq")), c("L1_xattn_Wk"), c("L1_xattn_Wv")],
        [rows(c("L1_ffn_Wq").T), rows(c("L1_ffn_Wk").T), rows(c("L1_ffn_Wv").T), rows(c("L1_ffn_Wo").T),
         rows(c("L1_ffn_A")), rows(c("L1_ffn_A")), padded(c("L1_ffn_B"), P), col(c("L1_ffn_ln1_w")), col(c("L1_ffn_ln2_w")),
         *units(c("L1_ffn_W_in_base").T, c("L1_ffn_W_up_base").T, c("L1_ffn_W_down").T)],
        [rows(c("L2_xattn_Wq")), c("L2_xattn_Wk"), c("L2_xattn_Wv"), col(c("L2_xattn_gq")),
         col(c("L2_xattn_gk"))],
        units(c("L2_ffn_w_gate").T, c("L2_ffn_w_up").T, c("L2_ffn_w_down").T),
        [rows(c("L3_xattn_Wq")), l3k, l3v, kvd[:, :DIM], kvd[:, DIM:], rows(c("L3_xattn_Wo")),
         everywhere(c("L3_xattn_bq")), rows_of(everywhere(b3k), everywhere(c("L3_xattn_bkv_dca")[:DIM])), everywhere(b3v),
         everywhere(c("L3_xattn_bkv_dca")[DIM:]), everywhere(c("L3_xattn_bo")), heads("qn_w"), heads("qn_b"), rows_of(heads("kn_w"), heads("kn_dca_w")),
         rows_of(heads("kn_b"), heads("kn_dca_b")), segc],
        [rows(c("L3_ffn_router_w")), *units(c("L3_ffn_w_gate"), c("L3_ffn_w_up"), c("L3_ffn_w_down"))],
    ]


STOP = 99


def kernel(**inputs):
    import concourse.bacc as bacc
    from concourse.bass_utils import run_bass_kernel_spmd

    nc = bacc.Bacc("TRN2", target_bir_lowering=False, num_devices=1)
    mask = np.asarray(inputs["mask_BxS2_bf1"]).view(np.uint8)
    arrays = {
        "x": np.asarray(inputs["x"]).transpose(1, 0, 2),
        "ctxT": np.asarray(inputs["ctx_1024"]).transpose(2, 0, 1),
        "pos": np.asarray(inputs["fside_BxSx2_0"]).transpose(1, 0, 2),
        "mask_row": mask.reshape(1, BATCH * TOK),
        "mask_col": mask.T,
        "gates": everywhere(np.concatenate([np.asarray(inputs["g_xattn"]), np.asarray(inputs["g_ffn"])])),
    }
    for s, parts in enumerate(lay_out(inputs)):
        assert [p.shape[1] for p in parts] == [c for _, c in LAYOUT[s]], s
        arrays[f"weights{s}"] = np.concatenate(parts, 1)
    for n, layer in enumerate((1, 2)):
        arrays[f"wo{n}"] = rows(np.asarray(inputs[f"L{layer}_xattn_Wo"]))
    w1, w2 = np.asarray(inputs["L3_ffn_w1"]), np.asarray(inputs["L3_ffn_w2"])
    arrays["experts"] = np.stack([units(w1[e][:, :INTER], w1[e][:, INTER:], w2[e])[0] for e in range(EXPERTS)], 1)
    arrays = {n: np.ascontiguousarray(a) for n, a in arrays.items()}
    aps = {n: nc.dram_tensor(n, a.shape, mybir.dt.from_np(a.dtype), kind="ExternalInput").ap() for n, a in arrays.items()}
    out = nc.dram_tensor("out", (TOK, BATCH, DIM), F32, kind="ExternalOutput").ap()
    build(nc, STOP, aps["x"], aps["ctxT"], aps["pos"], aps["mask_row"], aps["mask_col"], aps["gates"],
          [aps[f"weights{s}"] for s in range(len(LAYOUT))], [aps["wo0"], aps["wo1"]], aps["experts"], out)
    r = run_bass_kernel_spmd(nc, [arrays], core_ids=[0])
    return np.ascontiguousarray(r.results[0]["out"].transpose(1, 0, 2))
```

```python
from contextlib import ExitStack

import numpy as np

import concourse.bass as bass
from concourse import mybir

ALU = mybir.AluOpType
ACT = mybir.ActivationFunctionType
F32 = mybir.dt.float32
BF16 = mybir.dt.bfloat16
F32R = mybir.dt.float32r
U8 = mybir.dt.uint8
AX = mybir.AxisListType.X

BATCH, TOK, DIM, CDIM = 16, 128, 256, 128
P = 128
KD = DIM // P
GROUP = 4
TURNS = BATCH // GROUP
GT = GROUP * TOK
HID0 = 704
HID0P = 768
FF = 1024
EXPERTS, INTER = 8, 512
MAIN = 112
DCA = TOK - MAIN
MAGIC = 12582912.0
BIG = 1e30
PI = float(np.pi)
INPUTS = 3

UH = 512
RANK = 16
MODK = 2 * 32 + RANK
UNIT = 2 * KD * UH + UH // P * DIM
LAYOUT = [
    [("wq", KD * DIM), ("wk", DIM), ("wv", DIM), ("wo", KD * DIM), ("bo", DIM)],
    [("w1", KD * HID0), ("w3", KD * HID0), ("w2", HID0P // P * DIM)],
    [("wq", KD * 2048), ("wk", 1024), ("wv", 1024)],
    [("wq", KD * DIM), ("wk", KD * DIM), ("wv", KD * DIM), ("wo", KD * DIM), ("a", KD * MODK), ("a2", KD * MODK),
     ("ln1", KD), ("ln2", KD), ("unit0", UNIT), ("unit1", UNIT)],
    [("wq", KD * 2048), ("wk", 2048), ("wv", 2048), ("gq", 1), ("gk", 1)],
    [("unit0", UNIT), ("unit1", UNIT)],
    [("wq", KD * DIM), ("wk", DIM), ("wv", DIM), ("wkd", DIM), ("wvd", DIM), ("wo", KD * DIM), ("bq", DIM),
     ("bk", DIM), ("bv", DIM), ("bvd", DIM), ("bo", DIM), ("qnw", DIM), ("qnb", DIM),
     ("knw", DIM), ("knb", DIM), ("segc", 4)],
    [("router", KD * EXPERTS), ("unit0", UNIT), ("unit1", UNIT)],
]
WIDTH = [sum(c for _, c in part) for part in LAYOUT]


class Count:

    def __init__(self, sem):
        self.sem, self.base, self.per, self.turns = sem, 1, 0, 0

    def begin(self, per, turns=TURNS):
        self.base += self.per * self.turns
        self.per, self.turns = per, turns

    def at(self, i, n):
        return i * self.per + (self.base + n)


def build(nc, x_in, ctxT_in, pos_in, mrow_in, mcol_in, gates_in, weights, wo_in, modb_in, experts_in, out):
    with ExitStack() as ctx:
        def sb(name, shape, dt=F32):
            return ctx.enter_context(nc.sbuf_tensor(name, shape, dt))

        def count(name):
            return Count(ctx.enter_context(nc.semaphore(name)))

        X = sb("X", [P, BATCH, DIM])
        XNT = sb("XNT", [P, KD, BATCH * TOK])
        WREG = [sb(f"WREG{r}", [P, max(WIDTH[r::2])]) for r in range(2)]
        TG = sb("TG", [P, 8])
        SINCOS = sb("SINCOS", [P, 2, BATCH, 4])
        MCOL = sb("MCOL", [P, BATCH])
        IDENT = sb("IDENT", [P, P])
        IDENTB = sb("IDENTB", [P, P], BF16)
        CAUSAL = sb("CAUSAL", [P, 2, P], BF16)
        ONES = sb("ONES", [P, P])
        ONESB = sb("ONESB", [1, P], BF16)
        MHALF = sb("MHALF", [P, 64])
        AQ = sb("AQ", [P, BATCH])
        RW = sb("RW", [P, BATCH, 2 + EXPERTS])
        STAT = sb("STAT", [P, 128])
        PS = [ctx.enter_context(nc.psum_tensor(f"PS{b}", [P, 512], F32)) for b in range(8)]
        PSB = [b[:, :].bitcast(BF16) for b in PS]

        w_loaded = [count(f"w_loaded{s}") for s in range(len(LAYOUT))]
        inputs_loaded, x_loaded = count("inputs_loaded"), count("x_loaded")
        stored = count("stored")
        dve_step, act_step, pool_step = count("dve_step"), count("act_step"), count("pool_step")
        rstd_in, rstd_out = count("rstd_in"), count("rstd_out")
        xn_ready, xnT_ps, xnT_sb = count("xn_ready"), count("xnT_ps"), count("xnT_sb")
        copied = count("copied")
        ctx_loaded = count("ctx_loaded")
        qk_ps, v_ps, qk_pad, qkT_ps, qkT_sb, v_sb = (count(n) for n in ("qk_ps", "v_ps", "qk_pad", "qkT_ps", "qkT_sb", "v_sb"))
        s_ps, s_sub, p_exp, p_norm, pT_ps, pT_sb, av_ps = (count(n) for n in ("s_ps", "s_sub", "p_exp", "p_norm", "pT_ps", "pT_sb", "av_ps"))
        o_tok, oT_ps, oT_sb, out_ps, x_done = (count(n) for n in ("o_tok", "oT_ps", "oT_sb", "out_ps", "x_done"))
        gu_ps, silu_done, h_done, down_ps = (count(n) for n in ("gu_ps", "silu_done", "h_done", "down_ps"))
        sq_done = count("sq_done")
        p_sum, p_two, p_three, v_one = (count(n) for n in ("p_sum", "p_two", "p_three", "v_one"))
        gained, zeroed = count("gained"), count("zeroed")
        s_max, m_pad, mT_ps, mT_sb, st_ps = (count(n) for n in ("s_max", "m_pad", "mT_ps", "mT_sb", "st_ps"))
        mask_loaded = count("mask_loaded")
        quant_step = count("quant_step")
        modb_loaded = count("modb_loaded")
        wo_loaded = [count("wo_loaded0"), count("wo_loaded1")]
        x_hi, x_lo, w_hi, w_lo = (count(n) for n in ("x_hi", "x_lo", "w_hi", "w_lo"))
        raw_loaded = [count("raw_loaded0"), count("raw_loaded1")]
        q_ps, qT_sb = count("q_ps"), count("qT_sb")

        STEPS = 256
        scope = [None, 0]

        def tile(name, shape, dt=F32):
            return scope[0].enter_context(nc.sbuf_tensor(f"{name}_{scope[1]}", shape, dt))

        class Chain:

            def __init__(self, eng, cnt, i=0):
                self.eng, self.cnt, self.i, self.n = eng, cnt, i, 0

            def step(self, ins):
                self.n += 1
                ins.then_inc(self.cnt.sem, 1)

            def settle(self):
                self.eng.wait_ge(self.cnt.sem, self.cnt.at(self.i, self.n))

            def link(self, ins):
                self.step(ins)
                self.settle()

            def close(self):
                self.settle()
                self.eng.sem_inc(self.cnt.sem, STEPS - self.n)

        def w(s, name):
            at = 0
            for n, c in LAYOUT[s]:
                if n == name:
                    return WREG[s % 2][:, at:at + c]
                at += c
            raise KeyError(name)

        def wk(s, name, k):
            return w(s, name).rearrange("p (k n) -> p k n", k=k)

        def load_weights(sp, s):
            half = WIDTH[s] // 2
            for a, b in ((0, half), (half, WIDTH[s])):
                sp.dma_start(WREG[s % 2][:, a:b], weights[s][:, a:b]).then_inc(w_loaded[s].sem, 16)

        def begin(turns, **per):
            for name, n in per.items():
                named[name].begin(n, turns)

        named = dict(dve_step=dve_step, act_step=act_step, pool_step=pool_step, rstd_in=rstd_in, rstd_out=rstd_out,
                     xn_ready=xn_ready, xnT_ps=xnT_ps, xnT_sb=xnT_sb, copied=copied, qk_ps=qk_ps, v_ps=v_ps,
                     qk_pad=qk_pad, qkT_ps=qkT_ps, qkT_sb=qkT_sb, v_sb=v_sb, s_ps=s_ps, s_sub=s_sub, p_exp=p_exp,
                     p_norm=p_norm, pT_ps=pT_ps, pT_sb=pT_sb, av_ps=av_ps, o_tok=o_tok, oT_ps=oT_ps, oT_sb=oT_sb,
                     out_ps=out_ps, x_done=x_done, gu_ps=gu_ps, silu_done=silu_done, h_done=h_done,
                     down_ps=down_ps, sq_done=sq_done, gained=gained, zeroed=zeroed, p_sum=p_sum, p_two=p_two, p_three=p_three, v_one=v_one, s_max=s_max, m_pad=m_pad, mT_ps=mT_ps, mT_sb=mT_sb,
                     st_ps=st_ps, ctx_loaded=ctx_loaded, q_ps=q_ps, qT_sb=qT_sb,
                     x_hi=x_hi, x_lo=x_lo, w_hi=w_hi, w_lo=w_lo, raw_loaded0=raw_loaded[0], raw_loaded1=raw_loaded[1])

        def first_block():
            begin(1, dve_step=STEPS, act_step=STEPS, pool_step=STEPS, p_exp=1, s_sub=1)
            angles = tile("angles", [P, 2 * 128])
            gates = tile("gates", [P, 8])
            ang = angles[:, 0:128].rearrange("p (c b f) -> p c b f", c=2, b=BATCH)
            turn = angles[:, 128:256].rearrange("p (c b f) -> p c b f", c=2, b=BATCH)
            pos = tile("pos", [P, BATCH, 2])[:, :, :]
            mcol8 = tile("mcol8", [P, BATCH], U8)[:, :]
            with nc.Block() as block:
                @block.sync
                def _(sp):
                    sp.dma_start(pos, pos_in).then_inc(inputs_loaded.sem, 16)
                    sp.dma_start(mcol8, mcol_in).then_inc(inputs_loaded.sem, 16)
                    sp.dma_start(gates[:, :], gates_in).then_inc(inputs_loaded.sem, 16)
                    sp.dma_start(X[:, :, :], x_in).then_inc(x_loaded.sem, 16)
                    load_weights(sp, 0)

                @block.gpsimd
                def _(pool):
                    for c in named.values():
                        pool.sem_inc(c.sem, 1)
                    ch = Chain(pool, pool_step)
                    ch.step(pool.memset(IDENT[:, :], 0.0))
                    ch.step(pool.memset(IDENTB[:, :], 0.0))
                    ch.step(pool.memset(CAUSAL[:, :, :], 0.0))
                    ch.step(pool.memset(ONES[:, :], 1.0))
                    ch.step(pool.memset(ONESB[:, :], 1.0))
                    ch.step(pool.memset(MHALF[:, :], -0.5))
                    ch.settle()
                    for m in (IDENT, IDENTB):
                        ch.step(pool.affine_select(out=m[:, :], in_=m[:, :], compare_op=ALU.not_equal, fill=1.0,
                                                   base=0, pattern=[[-1, P]], channel_multiplier=1))
                    for a, sign in enumerate((1, -1)):
                        ch.step(pool.affine_select(out=CAUSAL[:, a, :], in_=CAUSAL[:, a, :], compare_op=ALU.is_ge, fill=-BIG,
                                                   base=0, pattern=[[-sign, P]], channel_multiplier=sign))
                    ch.close()

                @block.vector
                def _(dve):
                    ch = Chain(dve, dve_step)
                    dve.wait_ge(inputs_loaded.sem, 16 * INPUTS)
                    for f, freq in enumerate((1.0, 10000.0 ** -0.5)):
                        for c in range(2):
                            dst = ang[:, c, :, :].rearrange("p b (a f) -> p b a f", f=2)[:, :, :, f]
                            ch.step(dve.tensor_scalar(dst, pos, freq, 0.5 * PI * c, ALU.mult, ALU.add))
                    ch.settle()
                    ch.link(dve.tensor_scalar(turn, ang, 0.5 / PI, MAGIC, ALU.mult, ALU.add))
                    ch.link(dve.tensor_scalar(turn, turn, MAGIC, -2.0 * PI, ALU.subtract, ALU.mult))
                    ch.link(dve.tensor_tensor(ang, ang, turn, ALU.add))
                    ch.link(dve.tensor_scalar(ang, ang, 3.1415925, -3.1415925, ALU.min, ALU.max))
                    ch.step(dve.tensor_copy(MCOL[:, :], mcol8))
                    ch.settle()
                    ch.link(dve.memset(STAT[:, :], 0.0))
                    dve.sem_inc(s_sub.sem, 1)
                    dve.wait_ge(p_exp.sem, p_exp.at(0, 1))
                    ch.close()

                @block.scalar
                def _(act):
                    act.wait_ge(s_sub.sem, s_sub.at(0, 1))
                    nc.scalar.activation(SINCOS[:, :, :, :], ang, ACT.Sin).then_inc(act_step.sem, 1)
                    nc.scalar.activation(TG[:, :], gates[:, :], ACT.Tanh).then_inc(p_exp.sem, 1)
                    act.wait_ge(p_exp.sem, p_exp.at(0, 1))
                    act.sem_inc(act_step.sem, STEPS - 1)

        def norm_block(prefetch, kind="plain", tg=None, first=False):
            rms, quant = kind == "rms", kind == "quant"
            begin(TURNS, xn_ready=1, xnT_ps=KD, xnT_sb=KD)
            begin(1, dve_step=STEPS, rstd_in=1 + rms, rstd_out=1 + rms)
            XN = tile("xn", [P, BATCH, DIM])
            SQ = tile("sq", [P, 2, DIM]) if rms else None
            st, mv = tile("st", [P, BATCH, 6]), tile("mv", [P, BATCH, 2])
            var, rstd, aux, rinv = (tile(n, [P, BATCH]) for n in ("var", "rstd", "aux", "rinv"))
            XQT = XNT[:, 0, :].bitcast(BF16).rearrange("p (k t) -> p k t", k=KD)
            with nc.Block() as block:
                if prefetch is not None:
                    @block.sync
                    def _(sp):
                        load_weights(sp, prefetch)

                @block.vector
                def _(dve):
                    ch = Chain(dve, dve_step)
                    if first:
                        dve.wait_ge(x_loaded.sem, 16)
                    for b in range(BATCH):
                        ch.step(dve.bn_stats(st[:, b, :], X[:, b, :]))
                    for b in range(BATCH):
                        dve.wait_ge(dve_step.sem, dve_step.at(0, b + 1))
                        ch.step(dve.bn_aggr(mv[:, b, :], st[:, b, :]))
                    ch.settle()
                    dve.tensor_scalar(var[:, :], mv[:, :, 1], 1e-5, None, ALU.add).then_inc(rstd_in.sem, 1)
                    dve.wait_ge(rstd_out.sem, rstd_out.at(0, 1))
                    for b in range(BATCH):
                        ins = dve.tensor_scalar(XN[:, b, :], X[:, b, :], mv[:, b, 0:1], rstd[:, b:b + 1], ALU.subtract, ALU.mult)
                        if kind == "plain" and b % GROUP == GROUP - 1:
                            ins.then_inc(xn_ready.sem, 1)
                        elif kind != "plain":
                            ch.step(ins)
                    if rms:
                        ch.settle()
                        for b in range(BATCH):
                            if b >= 2:
                                dve.wait_ge(dve_step.sem, dve_step.at(0, 3 * BATCH + 2 * (b - 1)))
                            ch.step(dve.tensor_tensor_reduce(SQ[:, b % 2, :], XN[:, b, :], XN[:, b, :], 1.0, 0.0,
                                                             ALU.mult, ALU.add, aux[:, b:b + 1]))
                            ch.step(dve.scalar_tensor_tensor(out=X[:, b, :], in0=XN[:, b, :], scalar=TG[:, tg:tg + 1],
                                                             in1=X[:, b, :], op0=ALU.mult, op1=ALU.add))
                        ch.settle()
                        dve.tensor_scalar(var[:, :], aux[:, :], 1.0 / DIM, 1e-6, ALU.mult, ALU.add).then_inc(rstd_in.sem, 1)
                        dve.wait_ge(rstd_out.sem, rstd_out.at(0, 2))
                        for g in range(TURNS):
                            part = XN[:, g * GROUP:(g + 1) * GROUP, :]
                            scale = rstd[:, g * GROUP:(g + 1) * GROUP].unsqueeze(2).broadcast_to([P, GROUP, DIM])
                            dve.tensor_tensor(part, part, scale, ALU.mult).then_inc(xn_ready.sem, 1)
                    if quant:
                        ch.settle()
                        ch.link(dve.tensor_reduce(aux[:, :], XN[:, :, :], AX, ALU.max, apply_absolute_value=True))
                        ch.link(dve.tensor_scalar(aux[:, :], aux[:, :], 1e-5, None, ALU.max))
                        ch.step(dve.tensor_scalar(AQ[:, :], aux[:, :], 1.0 / 127.0, None, ALU.mult))
                        ch.link(dve.reciprocal(rinv[:, :], aux[:, :]))
                        ch.link(dve.tensor_scalar(rinv[:, :], rinv[:, :], 127.0, None, ALU.mult))
                        for b in range(BATCH):
                            ch.step(dve.tensor_scalar(XN[:, b, :], XN[:, b, :], rinv[:, b:b + 1], MAGIC, ALU.mult, ALU.add))
                        ch.settle()
                        for g in range(TURNS):
                            part = XN[:, g * GROUP:(g + 1) * GROUP, :]
                            ch.link(dve.tensor_scalar(part, part, MAGIC + 127.0, MAGIC - 128.0, ALU.min, ALU.max))
                            dve.tensor_scalar(part, part, MAGIC, None, ALU.subtract).then_inc(xn_ready.sem, 1)
                    ch.close()

                @block.gpsimd
                def _(pool):
                    for n in range(1 + rms):
                        pool.wait_ge(rstd_in.sem, rstd_in.at(0, n + 1))
                        pool.tensor_tensor(rstd[:, :], var[:, :], MHALF[:, 0:BATCH], ALU.pow).then_inc(rstd_out.sem, 1)

                @block.tensor
                def _(pe):
                    for g in range(TURNS):
                        pe.wait_ge(xn_ready.sem, xn_ready.at(g, 1))
                        for k in range(KD):
                            if g >= 2:
                                pe.wait_ge(xnT_sb.sem, xnT_sb.at(g - 2, k + 1))
                            for b in range(GROUP):
                                ins = pe.transpose(PS[2 * (g % 2) + k][:, b * P:(b + 1) * P],
                                                   XN[:, g * GROUP + b, k * P:(k + 1) * P], IDENT[:, :])
                            ins.then_inc(xnT_ps.sem, 1)

                @block.scalar
                def _(act):
                    dst = XQT if quant else XNT
                    for g in range(TURNS):
                        for k in range(KD):
                            act.wait_ge(xnT_ps.sem, xnT_ps.at(g, k + 1))
                            act.copy(dst[:, k, g * GT:(g + 1) * GT], PS[2 * (g % 2) + k][:, :]).then_inc(xnT_sb.sem, 1)

        def small_attention(s, tg, NH, HD, kind, MODT=None):
            seg, causal = kind == "dca", kind == "causal"
            SL = 4 * HD
            PER = P // SL
            NS = NH // 4
            MR = 3 * HD
            NM = 4 if seg else 2
            V = 2 * (HD + 1) if seg else HD + 1
            segs = ((0, MAIN), (MAIN, TOK)) if seg else ((0, TOK),)
            parts = NS == 8
            LAG = 4 if parts else 3
            OFF = dict(project=-10 if NS == 4 else -9, heads=-9 if NS == 4 else -8, turn=-4, value=-1, score=0, pad_max=NS - 1, turn_max=NS,
                       score_t=NS + 1, split=NS + 2, vsplit=-1, copy_x=-12 if NS == 4 else -16,
                       rstd=-9 if NS == 4 else -8, av=NS + LAG, attended=2 * NS + LAG, turn_out=2 * NS + LAG + 1, out=2 * NS + LAG + 2,
                       add=2 * NS + LAG + 3, mod=2 * NS + 7)
            LASTP = BATCH - 1 + OFF["mod"] // NS
            FIRSTP = OFF["project"] // NS
            LOOP0 = 3
            LOOPS = (BATCH + FIRSTP - LOOP0) // 3
            S_BANK = (0, 0) if seg else (0, 1)
            begin(BATCH, copied=1, ctx_loaded=0 if causal else 16 * len(segs), qk_ps=1, v_ps=1, qk_pad=1, qkT_ps=4,
                  qkT_sb=4, v_sb=1, s_ps=NS, s_max=NS, m_pad=1, mT_ps=2, mT_sb=2, st_ps=NS, p_exp=NS, p_two=NS * parts, p_three=NS * parts, v_one=int(parts), av_ps=NS,
                  o_tok=1, oT_ps=1, oT_sb=1, out_ps=1, x_done=1, rstd_in=2 * seg, rstd_out=2 * seg,
                  q_ps=int(causal), qT_sb=int(causal))
            begin(LASTP - FIRSTP + 1, dve_step=STEPS)
            begin(1, pool_step=1 if causal else 2, zeroed=1, gained=1)

            with nc.Block() as block:
                xs = tile("xs", [P, 3, KD, TOK])
                cs = None if causal else tile("cs", [P, 3, len(segs), TOK])
                qp, kp = tile("qp", [P, 3, NH, SL], F32R), tile("kp", [P, 3, NH, SL], F32R)
                qT, kT, qM = (tile(n, [P, 3, 8, TOK], F32R) for n in ("qT", "kT", "qM"))
                if parts:
                    v1, v2, v3 = (tile(n, [P, 3, NH, V], BF16) for n in ("v1", "v2", "v3"))
                else:
                    v1 = tile("vs", [P, 3, NH, V])
                pT = tile("pT", [P, 2, 512])
                if parts:
                    pres = tile("pres", [P, 2, 512])
                    p1, p2, p3 = (tile(n, [P, 4, 512], BF16) for n in ("p1", "p2", "p3"))
                prod = None if causal else tile("prod", [P, 4, NH * HD // 2])
                fresh = tile("fresh", [P, 2, DIM])
                nmax = tile("nmax", [P, 2, NH])
                rsum = tile("rsum", [P, 2, NH])
                otok = tile("otok", [P, len(segs), DIM])
                oT = tile("oT", [P, KD, TOK])
                sc = tile("sc", [P, 2, 4])
                hsum, hvar, hrstd = (tile(n, [P, 2, NH]) for n in ("hsum", "hvar", "hrstd"))
                aT = tile("aT", [P, KD, TOK]) if causal else None
                vres = tile("vres", [P, DIM]) if parts else None
                vbias = w(s, "bv") if seg else None
                obias = None if causal else w(s, "bo")
                wq, wo = wk(s, "wq", KD), wk(s, "wo", KD)

                def slot_ops(beta, u):
                    for stage, count_ in STAGES:
                        for n in range(count_):
                            back, at = divmod(OFF[stage] + n, NS)
                            if at == u:
                                yield stage, back, n

                STAGES = [("attended", 1), ("add", 1), ("turn_max", 2), ("score", NS), ("split", NS), ("rstd", 2),
                          ("copy_x", 1), ("score_t", NS), ("av", NS), ("pad_max", 1), ("turn", 4), ("turn_out", 1), ("out", 1), ("mod", int(causal)),
                          ("value", 1), ("vsplit", 1), ("project", 1), ("heads", 3)]

                def features(part):
                    if seg:
                        return part.rearrange("p h (a v) -> p h a v", a=2)[:, :, :, 0:HD]
                    return part[:, :, 0:HD]

                def values_in_psum():
                    if seg:
                        return PS[7][:, :].rearrange("p (a h e) -> p h a e", a=2, h=NH)
                    return PS[7][:, 0:DIM].rearrange("p (h e) -> p h e", h=NH)


                def run(eng, stages, start_of_period=None, end_of_period=None):
                    def period(beta, phase):
                        if start_of_period:
                            start_of_period(beta)
                        for u in range(NS):
                            for stage, back, n in slot_ops(beta, u):
                                if stage not in stages:
                                    continue
                                if isinstance(beta, int) and not 0 <= beta - back < BATCH:
                                    continue
                                stages[stage](beta - back, n, (phase - back) % 3)
                        if end_of_period:
                            end_of_period(beta)

                    for beta in range(FIRSTP, LOOP0):
                        period(beta, beta)
                    with eng.Fori(1, 1 + LOOPS) as i:
                        for r in range(3):
                            period(i * 3 + r, r)
                    for beta in range(LOOP0 + 3 * LOOPS, LASTP + 1):
                        period(beta, beta)

                @block.sync
                def _(sp):
                    if not causal:
                        sp.wait_ge(pool_step.sem, pool_step.at(0, 1))

                        def load(b, r, again):
                            if again:
                                if seg:
                                    sp.wait_ge(v_ps.sem, v_ps.at(b - 3, 1))
                                else:
                                    sp.wait_ge(qk_ps.sem, qk_ps.at(b - 1, 1))
                            elif b:
                                sp.wait_ge(ctx_loaded.sem, ctx_loaded.at(b - 1, 16 * len(segs)))
                            for a, (lo, hi) in enumerate(segs):
                                sp.dma_start(cs[:, r, a, lo:hi], ctxT_in[:, bass.ds(b, 1), lo:hi].rearrange("p b t -> p (b t)"))\
                                    .then_inc(ctx_loaded.sem, 16)

                        for b in range(3):
                            load(b, b, False)
                        with sp.Fori(1, 5) as i:
                            for r in range(3):
                                load(i * 3 + r, r, True)
                        load(BATCH - 1, 0, True)

                @block.gpsimd
                def _(pool):
                    if not causal:
                        pool.memset(cs[:, :, :, :], 0.0)
                    if parts:
                        pool.memset(v2[:, :, :, :], 0.0)
                        pool.memset(v3[:, :, :, :], 0.0)
                    pool.memset(v1[:, :, :, :], 1.0).then_inc(pool_step.sem, 1)
                    if not causal:
                        pool.wait_ge(w_loaded[s].sem, 32)
                        pool.tensor_scalar(obias, obias, TG[:, tg:tg + 1], None, ALU.mult).then_inc(pool_step.sem, 1)
                        pool.wait_ge(pool_step.sem, pool_step.at(0, 2))

                    def copy_x(b, n, r):
                        if not (isinstance(b, int) and b < 3):
                            pool.wait_ge(v_ps.sem, v_ps.at(b - 3, 1))
                        if not causal:
                            xb = X[:, bass.ds(b, 1), :].rearrange("p a d -> p (a d)")
                            pool.tensor_tensor(xb, xb, obias, ALU.add)
                        src = XNT[:, :, bass.ds(b * TOK, TOK)]
                        pool.tensor_copy(xs[:, r, :, :], src).then_inc(copied.sem, 1)

                    def head_rstd(b, n, r):
                        pool.wait_ge(rstd_in.sem, rstd_in.at(b, n + 1))
                        pool.tensor_tensor(hrstd[:, n, :], hvar[:, n, :], MHALF[:, 0:NH], ALU.pow).then_inc(rstd_out.sem, 1)

                    def split(b, u, r):
                        pool.wait_ge(p_two.sem, p_two.at(b, u + 1))
                        pool.tensor_tensor(p3[:, u % 4, :], pres[:, u % 2, :], p2[:, u % 4, :], ALU.subtract).then_inc(p_three.sem, 1)

                    stages = dict(copy_x=copy_x)
                    if parts:
                        stages["split"] = split
                    if seg:
                        stages["rstd"] = head_rstd
                    run(pool, stages)

                @block.tensor
                def _(pe):
                    pe.wait_ge(w_loaded[s].sem, 32)
                    if causal:
                        pe.wait_ge(gained.sem, gained.at(0, 1))

                    def context(dst, r, name, dca_name=None):
                        if causal:
                            for c in range(KD):
                                ins = pe.matmul(dst, xs[:, r, c, :], wk(s, name, KD)[:, c, :], start=(c == 0), stop=(c == KD - 1))
                            return ins
                        if not seg:
                            return pe.matmul(dst, cs[:, r, 0, :], w(s, name), start=True, stop=True)
                        for a, nm in enumerate((name, dca_name)):
                            ins = pe.matmul(dst, cs[:, r, a, :], w(s, nm), start=(a == 0), stop=(a == 1))
                        return ins

                    def project(b, n, r):
                        pe.wait_ge(copied.sem, copied.at(b, 1))
                        if not causal:
                            pe.wait_ge(ctx_loaded.sem, ctx_loaded.at(b, 16 * len(segs)))
                        if not (isinstance(b, int) and b == 0):
                            pe.wait_ge(qk_pad.sem, qk_pad.at(b - 1, 1))
                        q, k = PS[6][:, 0:DIM], PS[6][:, DIM:2 * DIM]
                        for c in range(KD):
                            pe.matmul(q, xs[:, r, c, :], wq[:, c, :], start=(c == 0), stop=(c == KD - 1))
                        context(k, r, "wk", "wkd").then_inc(qk_ps.sem, 1)

                    def value(b, n, r):
                        before = OFF["add"] // NS + 1
                        if not (isinstance(b, int) and b < before):
                            pe.wait_ge(x_done.sem, x_done.at(b - before, 1))
                            if causal:
                                pe.wait_ge(qT_sb.sem, qT_sb.at(b - before, 1))
                        if not (isinstance(b, int) and b == 0):
                            pe.wait_ge(v_sb.sem, v_sb.at(b - 1, 1))
                        if seg:
                            for a, nm in enumerate(("wv", "wvd")):
                                dst = PS[7][:, a * DIM:(a + 1) * DIM]
                                ins = pe.matmul(dst, cs[:, r, a, :], w(s, nm), start=True, stop=True)
                        else:
                            ins = context(PS[7][:, 0:DIM], r, "wv")
                        ins.then_inc(v_ps.sem, 1)

                    def turn(b, n, r):
                        if n == 0:
                            pe.wait_ge(qk_pad.sem, qk_pad.at(b, 1))
                        if NS == 4 and n < 2:
                            if not (isinstance(b, int) and b < 2):
                                pe.wait_ge(mT_sb.sem, mT_sb.at(b - 2, n + 1))
                            elif n:
                                pe.wait_ge(qkT_sb.sem, qkT_sb.at(b, n))
                        elif n == 0:
                            if not (isinstance(b, int) and b < 2):
                                pe.wait_ge(mT_sb.sem, mT_sb.at(b - 2, 2))
                        else:
                            pe.wait_ge(qkT_sb.sem, qkT_sb.at(b, n))
                        if n == 0 and isinstance(b, int) and b == 1:
                            pe.wait_ge(qkT_sb.sem, qkT_sb.at(0, 4))
                        src = (qp, kp)[n // 2][:, r, :, :].bitcast(F32).rearrange("p h e -> p (h e)")
                        for c in range(4):
                            at = (4 * (n % 2) + c) * P
                            ins = pe.transpose(PS[5][:, c * P:(c + 1) * P], src[:, at:at + P], IDENT[:, :])
                        ins.then_inc(qkT_ps.sem, 1)

                    def turn_max(b, n, r):
                        if n == 0:
                            pe.wait_ge(m_pad.sem, m_pad.at(b, 1))
                        last = isinstance(b, int) and b == BATCH - 1
                        if n == 0:
                            pe.wait_ge(qkT_sb.sem, qkT_sb.at(b if last else b + 1, 4))
                        elif NS == 4 and not (isinstance(b, int) and b + 2 >= BATCH):
                            pe.wait_ge(qkT_sb.sem, qkT_sb.at(b + 2, 1))
                        else:
                            pe.wait_ge(mT_sb.sem, mT_sb.at(b, 1))
                        src = qp[:, r, :, :].bitcast(F32).rearrange("p h e -> p (h e)")
                        for c in range(4):
                            at = (4 * n + c) * P
                            ins = pe.transpose(PS[5][:, c * P:(c + 1) * P], src[:, at:at + P], IDENT[:, :])
                        ins.then_inc(mT_ps.sem, 1)

                    def score(b, u, r):
                        j, half = u % PER, u // PER
                        if u == 0:
                            pe.wait_ge(qkT_sb.sem, qkT_sb.at(b, 4))
                        d = 1 if seg else 2
                        if u >= d:
                            pe.wait_ge(s_max.sem, s_max.at(b, u - d + 1))
                        elif not (isinstance(b, int) and b == 0):
                            pe.wait_ge(s_max.sem, s_max.at(b - 1, NS + u - d + 1))
                        bank = PS[S_BANK[u % 2]]
                        if causal:
                            pe.matmul(bank[:, :].rearrange("p (h c) -> p h c", h=4), IDENTB[:, :],
                                      CAUSAL[:, 0, :].unsqueeze(1).broadcast_to([P, 4, P]), start=True, stop=False,
                                      skip_group_check=True)
                        rows = slice(SL * j, SL * j + MR)
                        for c in range(4):
                            ins = pe.matmul(bank[:, c * P:(c + 1) * P], qT[rows, r, 4 * half + c, :],
                                            kT[rows, r, 4 * half + c, :], start=not causal, stop=True, skip_group_check=True)
                        ins.then_inc(s_ps.sem, 1)

                    def score_t(b, u, r):
                        j, half = u % PER, u // PER
                        pe.wait_ge(mT_sb.sem, mT_sb.at(b, half + 1))
                        if u >= 2:
                            pe.wait_ge(p_exp.sem, p_exp.at(b, u - 1))
                        elif not (isinstance(b, int) and b == 0):
                            pe.wait_ge(p_exp.sem, p_exp.at(b - 1, NS + u - 1))
                        bank = PS[2 + u % 2]
                        if causal:
                            pe.matmul(bank[:, :].rearrange("p (h c) -> p h c", h=4), IDENTB[:, :],
                                      CAUSAL[:, 1, :].unsqueeze(1).broadcast_to([P, 4, P]), start=True, stop=False,
                                      skip_group_check=True)
                        rows = slice(SL * j, SL * j + MR + NM)
                        for c in range(4):
                            ins = pe.matmul(bank[:, c * P:(c + 1) * P], kT[rows, r, 4 * half + c, :],
                                            qM[rows, r, 4 * half + c, :], start=not causal, stop=True, skip_group_check=True)
                        ins.then_inc(st_ps.sem, 1)

                    def av(b, u, r):
                        j, half = u % PER, u // PER
                        if parts:
                            pe.wait_ge(p_three.sem, p_three.at(b, u + 1))
                        else:
                            pe.wait_ge(p_exp.sem, p_exp.at(b, u + 1))
                        if u == 0:
                            pe.wait_ge(v_sb.sem, v_sb.at(b, 1))
                            if not (isinstance(b, int) and b == 0):
                                pe.wait_ge(o_tok.sem, o_tok.at(b - 1, 1))
                        for c in range(4):
                            h = PER * (4 * half + c) + j
                            if seg:
                                dst = PS[(4, 1)[h // 8]][:, h % 8 * V:(h % 8 + 1) * V]
                            else:
                                dst = PS[4][:, h * V:(h + 1) * V]
                            if not parts:
                                ins = pe.matmul(dst, pT[:, u % 2, c * P:(c + 1) * P], v1[:, r, h, :], start=True, stop=True)
                                continue
                            pairs = ((p1, v1), (p1, v2), (p1, v3), (p2, v1), (p2, v2), (p3, v1))
                            for m, (pp, vv) in enumerate(pairs):
                                ins = pe.matmul(dst, pp[:, u % 4, c * P:(c + 1) * P], vv[:, r, h, :], start=(m == 0),
                                                stop=(m == len(pairs) - 1))
                        ins.then_inc(av_ps.sem, 1)

                    def turn_out(b, n, r):
                        pe.wait_ge(o_tok.sem, o_tok.at(b, 1))
                        ahead = OFF["turn_out"] // NS
                        if not isinstance(b, int) or b + ahead < BATCH:
                            pe.wait_ge(v_sb.sem, v_sb.at(b + ahead, 1))
                        elif b + ahead == BATCH:
                            pe.wait_ge(v_sb.sem, v_sb.at(BATCH - 1, 1))
                        if not (isinstance(b, int) and b == 0):
                            pe.wait_ge(x_done.sem, x_done.at(b - 1, 1))
                            if causal:
                                pe.wait_ge(qT_sb.sem, qT_sb.at(b - 1, 1))
                        for c in range(KD):
                            ins = pe.transpose(PS[7][:, c * P:(c + 1) * P], otok[:, 0, c * P:(c + 1) * P], IDENT[:, :])
                        ins.then_inc(oT_ps.sem, 1)

                    def out_(b, n, r):
                        pe.wait_ge(oT_sb.sem, oT_sb.at(b, 1))
                        dst = PS[7][:, DIM:2 * DIM]
                        if causal:
                            for m in range(KD):
                                for c in range(KD):
                                    ins = pe.matmul(dst[:, m * P:(m + 1) * P], wo[:, c, m * P:(m + 1) * P], oT[:, c, :],
                                                    start=(c == 0), stop=(c == KD - 1))
                        else:
                            for c in range(KD):
                                ins = pe.matmul(dst, oT[:, c, :], wo[:, c, :], start=(c == 0), stop=(c == KD - 1))
                        ins.then_inc(out_ps.sem, 1)

                    def mod(b, n, r):
                        pe.wait_ge(x_done.sem, x_done.at(b, 1))
                        a = wk(s, "a", KD)
                        for c in range(KD):
                            ins = pe.matmul(PS[7][0:MODK, 0:TOK], a[:, c, :], aT[:, c, :], start=(c == 0), stop=(c == KD - 1))
                        ins.then_inc(q_ps.sem, 1)

                    run(pe, dict(score=score, score_t=score_t, av=av, turn=turn, turn_max=turn_max, turn_out=turn_out,
                                 out=out_, mod=mod, value=value, project=project))

                @block.vector
                def _(dve):
                    dve.memset(qp[:, :, :, MR:SL].bitcast(F32), 0.0)
                    dve.memset(kp[:, :, :, MR:SL].bitcast(F32), 0.0).then_inc(zeroed.sem, 1)
                    dve.wait_ge(zeroed.sem, zeroed.at(0, 1))
                    dve.wait_ge(pool_step.sem, pool_step.at(0, 1))
                    if seg:
                        dve.wait_ge(w_loaded[s].sem, 32)
                        for r in range(3):
                            dve.tensor_copy(kp[:, r, :, MR:MR + NM], w(s, "segc").unsqueeze(1).broadcast_to([P, NH, NM]))
                        for r in range(3):
                            for a in range(2):
                                ins = dve.tensor_copy(v1[:, r, :, a * (HD + 1) + HD],
                                                      w(s, "segc")[:, 2 * a:2 * a + 1].broadcast_to([P, NH]))
                        ins = dve.tensor_tensor(vbias, vbias, w(s, "bvd"), ALU.add)
                        ins.then_inc(gained.sem, 1)
                    else:
                        for r in range(3):
                            ins = dve.tensor_copy(kp[:, r, :, MR:MR + NM], ONES[:, 0:NM].unsqueeze(1).broadcast_to([P, NH, NM]))
                        if not causal:
                            ins.then_inc(gained.sem, 1)
                    if causal:
                        dve.wait_ge(w_loaded[s].sem, 32)
                        gained_parts = [(wk(s, n, KD), "ln1") for n in ("wq", "wk", "wv")] + [(wk(s, "a2", KD), "ln2")]
                        for u in ("unit0", "unit1"):
                            for lo in (0, KD * UH):
                                gained_parts.append((w(s, u)[:, lo:lo + KD * UH].rearrange("p (k n) -> p k n", k=KD), "ln2"))
                        for part, gain in gained_parts:
                            for c in range(KD):
                                ins = dve.tensor_scalar(part[:, c, :], part[:, c, :], w(s, gain)[:, c:c + 1], None, ALU.mult)
                        ins.then_inc(gained.sem, 1)
                    dve.wait_ge(gained.sem, gained.at(0, 1))
                    chain = [None]
                    both = PS[6][:, :].rearrange("p (a h e) -> p a h e", a=2, h=NH)

                    def split_slots(ch, part, r):
                        dst = (qp, kp)[part][:, r, :, :]
                        src = fresh[:, part, :].rearrange("p (h e) -> p h e", h=NH)
                        step = (1, 2)[part] * HD
                        for at in (0, step):
                            ch.step(dve.tensor_copy(dst[:, :, at:at + HD], src))
                        ch.settle()
                        lo = (2, 1)[part] * HD
                        ch.step(dve.tensor_tensor(dst[:, :, lo:lo + HD], src, dst[:, :, 0:HD].bitcast(F32), ALU.subtract))

                    def heads(b, n, r):
                        ch = chain[0]
                        if n == 0:
                            dve.wait_ge(qk_ps.sem, qk_ps.at(b, 1))
                        if kind == "rope":
                            if n == 0:
                                ch.link(dve.tensor_copy(sc[:, :, :], SINCOS[:, :, bass.ds(b, 1), :].rearrange("p c b f -> p c (b f)")))
                            if n < 2:
                                src = both[:, n].rearrange("p h (f e) -> p h f e", e=2)
                                sin = sc[:, 0, :].unsqueeze(1).broadcast_to([P, NH, 4])
                                cos = sc[:, 1, :].unsqueeze(1).broadcast_to([P, NH, 4])
                                m = prod[:, :, :].rearrange("p a (h f) -> p a h f", f=4)
                                ch.step(dve.tensor_tensor(m[:, 0], src[:, :, :, 0], cos, ALU.mult))
                                ch.step(dve.tensor_tensor(m[:, 1], src[:, :, :, 1], sin, ALU.mult))
                                ch.step(dve.tensor_tensor(m[:, 2], src[:, :, :, 0], sin, ALU.mult))
                                ch.step(dve.tensor_tensor(m[:, 3], src[:, :, :, 1], cos, ALU.mult))
                                ch.settle()
                                d = fresh[:, n, :].rearrange("p (h f e) -> p h f e", f=4, e=2)
                                ch.step(dve.tensor_tensor(d[:, :, :, 0], m[:, 0], m[:, 1], ALU.subtract))
                                ch.step(dve.tensor_tensor(d[:, :, :, 1], m[:, 2], m[:, 3], ALU.add))
                                ch.settle()
                        elif causal:
                            if n < 2:
                                ch.link(dve.tensor_copy(fresh[:, n, :], PS[6][:, n * DIM:(n + 1) * DIM]))
                        else:
                            if n < 2:
                                cen = fresh[:, n, :].rearrange("p (h e) -> p h e", h=NH)
                                ch.link(dve.tensor_tensor(fresh[:, n, :], PS[6][:, n * DIM:(n + 1) * DIM],
                                                          w(s, ("bq", "bk")[n]), ALU.add))
                                sq = prod[:, 2 * n:2 * n + 2, :].rearrange("p a (h e) -> p (a h) e", e=HD)
                                mean = hsum[:, n, :]
                                ch.link(dve.tensor_reduce(mean, cen, AX, ALU.add))
                                ch.link(dve.tensor_scalar(mean, mean, 1.0 / HD, None, ALU.mult))
                                ch.link(dve.tensor_tensor(cen, cen, mean.unsqueeze(2).broadcast_to([P, NH, HD]), ALU.subtract))
                                ch.link(dve.tensor_tensor(sq, cen, cen, ALU.mult))
                                ch.link(dve.tensor_reduce(mean, sq, AX, ALU.add))
                                dve.tensor_scalar(hvar[:, n, :], mean, 1.0 / HD, 1e-6, ALU.mult, ALU.add).then_inc(rstd_in.sem, 1)
                            else:
                                for p in range(2):
                                    cen = fresh[:, p, :].rearrange("p (h e) -> p h e", h=NH)
                                    dve.wait_ge(rstd_out.sem, rstd_out.at(b, p + 1))
                                    ch.step(dve.tensor_tensor(cen, cen, hrstd[:, p, :].unsqueeze(2).broadcast_to([P, NH, HD]), ALU.mult))
                                ch.settle()
                                for op, names in ((ALU.mult, ("qnw", "knw")), (ALU.add, ("qnb", "knb"))):
                                    for p in range(2):
                                        ch.step(dve.tensor_tensor(fresh[:, p, :], fresh[:, p, :], w(s, names[p]), op))
                                    ch.settle()
                        if n == 2:
                            if not (isinstance(b, int) and b < 3):
                                dve.wait_ge(mT_ps.sem, mT_ps.at(b - 3, 2))
                            split_slots(ch, 0, r)
                            split_slots(ch, 1, r)
                            ch.settle()
                            dve.sem_inc(qk_pad.sem, 1)

                    def score(b, u, r):
                        ch = chain[0]
                        j, half = u % PER, u // PER
                        dve.wait_ge(s_ps.sem, s_ps.at(b, u + 1))
                        S = PS[S_BANK[u % 2]][:, :].rearrange("p (h c) -> p h c", h=4)
                        for a, (lo, hi) in enumerate(segs):
                            first = PER * 4 * half + j
                            dst = nmax[:, a, first:first + 3 * PER + 1:PER]
                            ins = dve.tensor_reduce(dst, S[:, :, lo:hi], AX, ALU.max, negate=True)
                            if a < len(segs) - 1:
                                ch.step(ins)
                        ins.then_inc(s_max.sem, 1)

                    def split(b, u, r):
                        ch = chain[0]
                        dve.wait_ge(p_exp.sem, p_exp.at(b, u + 1))
                        if u >= 2:
                            dve.wait_ge(p_three.sem, p_three.at(b, u - 1))
                        elif not (isinstance(b, int) and b == 0):
                            dve.wait_ge(p_three.sem, p_three.at(b - 1, NS + u - 1))
                        ch.link(dve.tensor_tensor(pres[:, u % 2, :], pT[:, u % 2, :], p1[:, u % 4, :], ALU.subtract))
                        dve.tensor_copy(p2[:, u % 4, :], pres[:, u % 2, :]).then_inc(p_two.sem, 1)

                    def vsplit(b, n, r):
                        ch = chain[0]
                        dve.wait_ge(v_one.sem, v_one.at(b, 1))
                        ch.settle()
                        left = vres[:, :].rearrange("p (h e) -> p h e", e=HD)
                        ch.link(dve.tensor_tensor(left, values_in_psum(), features(v1[:, r, :, :]), ALU.subtract))
                        ch.link(dve.tensor_copy(features(v2[:, r, :, :]), left))
                        dve.tensor_tensor(features(v3[:, r, :, :]), left, features(v2[:, r, :, :]), ALU.subtract).then_inc(v_sb.sem, 1)

                    def pad_max(b, n, r):
                        ch = chain[0]
                        ch.settle()
                        dve.wait_ge(s_max.sem, s_max.at(b, NS))
                        dve.wait_ge(qkT_ps.sem, qkT_ps.at(b, 4))
                        for a in range(len(segs)):
                            ch.step(dve.tensor_copy(qp[:, r, :, MR + 2 * a], nmax[:, a, :]))
                        ch.settle()
                        for a in range(len(segs)):
                            ch.step(dve.tensor_tensor(qp[:, r, :, MR + 2 * a + 1], nmax[:, a, :],
                                                      qp[:, r, :, MR + 2 * a].bitcast(F32), ALU.subtract))
                        ch.settle()
                        dve.sem_inc(m_pad.sem, 1)

                    def attended(b, n, r):
                        ch = chain[0]
                        dve.wait_ge(av_ps.sem, av_ps.at(b, NS))
                        if not (isinstance(b, int) and b == 0):
                            dve.wait_ge(oT_ps.sem, oT_ps.at(b - 1, 1))
                        if seg:
                            for g, bank in enumerate((4, 1)):
                                O = PS[bank][:, 0:8 * V].rearrange("p (h a v) -> p h a v", h=8, a=2)
                                R = rsum[:, :, 8 * g:8 * g + 8].rearrange("p a h -> p h a")
                                ch.step(dve.reciprocal(R, O[:, :, :, HD]))
                            ch.settle()
                            for g, bank in enumerate((4, 1)):
                                O = PS[bank][:, 0:8 * V].rearrange("p (h a v) -> p h a v", h=8, a=2)
                                for a in range(2):
                                    dst = otok[:, a, 8 * HD * g:8 * HD * (g + 1)].rearrange("p (h e) -> p h e", e=HD)
                                    ch.step(dve.tensor_tensor(dst, O[:, :, a, 0:HD],
                                                              rsum[:, a, 8 * g:8 * g + 8].unsqueeze(2).broadcast_to([P, 8, HD]), ALU.mult))
                            ch.settle()
                            ch.link(dve.tensor_tensor(otok[:, 0, :], otok[:, 0, :], otok[:, 1, :], ALU.add))
                            dve.tensor_tensor(otok[:, 0, :], otok[:, 0, :], vbias, ALU.add).then_inc(o_tok.sem, 1)
                        else:
                            O = PS[4][:, 0:NH * V].rearrange("p (h v) -> p h v", v=V)
                            ch.link(dve.reciprocal(rsum[:, 0, :], O[:, :, HD]))
                            dve.tensor_tensor(otok[:, 0, :].rearrange("p (h e) -> p h e", e=HD), O[:, :, 0:HD],
                                              rsum[:, 0, :].unsqueeze(2).broadcast_to([P, NH, HD]), ALU.mult).then_inc(o_tok.sem, 1)

                    def add(b, n, r):
                        dve.wait_ge(out_ps.sem, out_ps.at(b, 1))
                        src = PS[7][:, DIM:2 * DIM]
                        if causal:
                            if not (isinstance(b, int) and b == 0):
                                dve.wait_ge(q_ps.sem, q_ps.at(b - 1, 1))
                            dve.tensor_copy(aT[:, :, :].rearrange("p c t -> p (c t)"), src).then_inc(x_done.sem, 1)
                            return
                        xb = X[:, bass.ds(b, 1), :].rearrange("p a d -> p (a d)")
                        dve.scalar_tensor_tensor(out=xb, in0=src, scalar=TG[:, tg:tg + 1], in1=xb,
                                                 op0=ALU.mult, op1=ALU.add).then_inc(x_done.sem, 1)

                    def start_of_period(beta):
                        chain[0] = Chain(dve, dve_step, beta - FIRSTP)

                    def end_of_period(beta):
                        chain[0].close()

                    splits = dict(split=split, vsplit=vsplit) if parts else {}
                    run(dve, dict(score=score, **splits, pad_max=pad_max, heads=heads, attended=attended, add=add), start_of_period, end_of_period)

                @block.scalar
                def _(act):
                    act.wait_ge(pool_step.sem, pool_step.at(0, 1))

                    def turn(b, n, r):
                        act.wait_ge(qkT_ps.sem, qkT_ps.at(b, n + 1))
                        dst = (qT, kT)[n // 2][:, r, 4 * (n % 2):4 * (n % 2) + 4, :].rearrange("p n t -> p (n t)")
                        act.copy(dst, PS[5][:, :]).then_inc(qkT_sb.sem, 1)

                    def turn_max(b, n, r):
                        act.wait_ge(mT_ps.sem, mT_ps.at(b, n + 1))
                        act.copy(qM[:, r, 4 * n:4 * n + 4, :].rearrange("p n t -> p (n t)"), PS[5][:, :]).then_inc(mT_sb.sem, 1)

                    def value(b, n, r):
                        act.wait_ge(v_ps.sem, v_ps.at(b, 1))
                        if not (isinstance(b, int) and b < 3):
                            act.wait_ge(av_ps.sem, av_ps.at(b - 3, NS))
                        act.copy(features(v1[:, r, :, :]), values_in_psum()).then_inc((v_one if parts else v_sb).sem, 1)

                    def score_t(b, u, r):
                        act.wait_ge(st_ps.sem, st_ps.at(b, u + 1))
                        if not parts:
                            if u >= 2:
                                act.wait_ge(av_ps.sem, av_ps.at(b, u - 1))
                            elif not (isinstance(b, int) and b == 0):
                                act.wait_ge(av_ps.sem, av_ps.at(b - 1, NS + u - 1))
                            act.activation(pT[:, u % 2, :], PS[2 + u % 2][:, :], ACT.Exp, scale=float(HD) ** -0.5).then_inc(p_exp.sem, 1)
                            return
                        if u >= 4:
                            act.wait_ge(av_ps.sem, av_ps.at(b, u - 3))
                        elif not (isinstance(b, int) and b == 0):
                            act.wait_ge(av_ps.sem, av_ps.at(b - 1, NS + u - 3))
                        if u >= 2:
                            act.wait_ge(p_two.sem, p_two.at(b, u - 1))
                        elif not (isinstance(b, int) and b == 0):
                            act.wait_ge(p_two.sem, p_two.at(b - 1, NS + u - 1))
                        act.activation(p1[:, u % 4, :], PS[2 + u % 2][:, :], ACT.Exp, scale=float(HD) ** -0.5)
                        act.activation(pT[:, u % 2, :], PS[2 + u % 2][:, :], ACT.Exp, scale=float(HD) ** -0.5).then_inc(p_exp.sem, 1)

                    def turn_out(b, n, r):
                        act.wait_ge(oT_ps.sem, oT_ps.at(b, 1))
                        if not (isinstance(b, int) and b == 0):
                            act.wait_ge(out_ps.sem, out_ps.at(b - 1, 1))
                        act.copy(oT[:, :, :], PS[7][:, 0:DIM].rearrange("p (c t) -> p c t", c=KD)).then_inc(oT_sb.sem, 1)

                    def mod(b, n, r):
                        act.wait_ge(q_ps.sem, q_ps.at(b, 1))
                        act.activation(MODT[:, bass.ds(b * TOK, TOK)], PS[7][0:MODK, 0:TOK], ACT.Tanh).then_inc(qT_sb.sem, 1)

                    run(act, dict(score_t=score_t, turn=turn, turn_max=turn_max, value=value, turn_out=turn_out, mod=mod))

        def big_attention(s, tg, kind):
            rms = kind == "rms"
            W = 2 if rms else GROUP
            turns = BATCH // W
            WT = W * TOK
            N = 4 * W
            NKV = N if rms else 16
            NR = 2 * N if rms else 0
            lag = 2 if rms else 1
            END = N + lag + 6
            begin(turns, dve_step=STEPS, act_step=STEPS, copied=1, ctx_loaded=16, v_ps=NKV, v_sb=NKV,
                  q_ps=NR if rms else N, sq_done=NR, rstd_in=NR, rstd_out=NR, qk_pad=NR, qkT_ps=NR,
                  qT_sb=NR if rms else N, s_ps=N, s_sub=N, p_exp=N, p_sum=N, p_norm=N, pT_ps=N, pT_sb=N, av_ps=N, oT_sb=N,
                  out_ps=N, x_done=W)
            if not rms:
                begin(1, pool_step=0, gained=1)
            wq = wk(s, "wq", KD)
            WO = tile("WO", [P, 16 * DIM])
            wo = WO[:, :].rearrange("p (k n) -> p k n", k=16)
            XS, CS = tile("XS", [P, KD, WT]), tile("CS", [P, 1, WT])
            QT, KT, VS = tile("QT", [P, 4096]), tile("KT", [P, 4096]), tile("VS", [P, 4096])
            PR, PTS = tile("PR", [P, 2, 512]), tile("PTS", [P, 2, 512])
            QN, SQ, QTS, OTS = (QT[:, n * 1024:(n + 1) * 1024].rearrange("p (a n) -> p a n", a=2) for n in range(4))
            kT = KT[:, :].rearrange("p (b h t) -> p b h t", b=W, t=TOK) if rms else KT[:, :].rearrange("p (h b t) -> p b h t", b=W, t=TOK)
            vs = VS[:, :].rearrange("p (b n) -> p b n", b=W)
            nmax = STAT[:, 0:8].rearrange("p (a h) -> p a h", a=2)
            psums = STAT[:, 16:24].rearrange("p (a h) -> p a h", a=2)
            qvar = STAT[:, 32:40].rearrange("p (a h) -> p a h", a=2)
            qrstd = STAT[:, 48:56].rearrange("p (a h) -> p a h", a=2)
            qsum = STAT[:, 64:72].rearrange("p (a h) -> p a h", a=2)
            mcol = STAT[:, 96:96 + GROUP]
            if not rms:
                mraw = tile("mraw", [1, BATCH * TOK], U8)[:, :]
                mrow = tile("mrow", [1, BATCH * TOK], BF16)[:, :]
                mgroup = tile("mgroup", [1, WT], BF16)[:, :]
            item_bank = lambda m: (6, 3)[m % 2] if m >= N else (6, 4, 3)[m % 3]
            value_bank = lambda n: n % 3 if rms else n % 4
            probs_bank = lambda t: 2 if rms else 2 + t % 2
            itemT_bank = lambda m: 7 if m >= N else (7, 5)[m % 2]

            with nc.Block() as block:
                @block.sync
                def _(sp):
                    sp.dma_start(WO[:, :], wo_in[int(rms)]).then_inc(wo_loaded[int(rms)].sem, 16)
                    if not rms:
                        sp.dma_start(mraw, mrow_in).then_inc(mask_loaded.sem, 16)
                    with sp.Fori(0, turns) as i:
                        sp.wait_ge(v_ps.sem, v_ps.at(i, 0))
                        sp.dma_start(CS[:, 0, 0:WT].rearrange("p (b t) -> p b t", t=TOK),
                                     ctxT_in[:, bass.ds(i * W, W), :]).then_inc(ctx_loaded.sem, 16)

                @block.gpsimd
                def _(pool):
                    if not rms:
                        pool.wait_ge(gained.sem, gained.at(0, 1))
                    with pool.Fori(0, turns) as i:
                        pool.wait_ge(q_ps.sem, q_ps.at(i, 0))
                        if not rms:
                            pool.wait_ge(s_ps.sem, s_ps.at(i, 0))
                            pool.tensor_copy(mgroup, mrow[:, bass.ds(i * WT, WT)])
                            pool.tensor_copy(mcol, MCOL[:, bass.ds(i * W, W)])
                        pool.tensor_copy(XS[:, :, 0:WT], XNT[:, :, bass.ds(i * WT, WT)]).then_inc(copied.sem, 1)


                        def item_rstd(m):
                            pool.wait_ge(rstd_in.sem, rstd_in.at(i, m + 1))
                            pool.tensor_tensor(qrstd[:, m % 2, :], qvar[:, m % 2, :], MHALF[:, 0:4],
                                               ALU.pow).then_inc(rstd_out.sem, 1)

                        def normalise(t):
                            pool.wait_ge(p_sum.sem, p_sum.at(i, t + 1))
                            pr = PR[:, t % 2, :].rearrange("p (h c) -> p h c", h=4)
                            pool.tensor_tensor(pr, pr, psums[:, t % 2, :].unsqueeze(2).broadcast_to([P, 4, P]),
                                               ALU.mult).then_inc(p_norm.sem, 1)

                        for m in range(NR - N if rms else 0):
                            item_rstd(m)
                        for t in range(END):
                            if rms and t < N:
                                item_rstd(N + t)
                            if 0 <= t - lag - 1 < N:
                                normalise(t - lag - 1)

                @block.tensor
                def _(pe):
                    pe.wait_ge(w_loaded[s].sem, 32)
                    pe.wait_ge(wo_loaded[int(rms)].sem, 16)

                    def keys_values(i, n):
                        if n >= 4:
                            pe.wait_ge(v_sb.sem, v_sb.at(i, n - 3))
                        if n < 8:
                            ins = pe.matmul(PS[n % 4][:, :], w(s, "wk")[:, n * P:(n + 1) * P], CS[:, 0, :], start=True, stop=True)
                        else:
                            b, half = divmod(n - 8, 2)
                            ins = pe.matmul(PS[n % 4][:, :], CS[:, 0, b * TOK:(b + 1) * TOK],
                                            w(s, "wv")[:, half * 512:(half + 1) * 512], start=True, stop=True)
                        ins.then_inc(v_ps.sem, 1)

                    def values_of(i, n):
                        b, part = divmod(n, 4)
                        if n >= 3:
                            pe.wait_ge(v_sb.sem, v_sb.at(i, n - 2))
                        pe.matmul(PS[value_bank(n)][:, :], CS[:, 0, b * TOK:(b + 1) * TOK], w(s, "wv")[:, part * 512:(part + 1) * 512],
                                  start=True, stop=True).then_inc(v_ps.sem, 1)

                    def item(i, m):
                        b, part = divmod(m % N, 4)
                        tok, cols = slice(b * TOK, (b + 1) * TOK), slice(part * 512, (part + 1) * 512)
                        back = 3 if m < N else 2
                        if m >= back:
                            pe.wait_ge(qk_pad.sem, qk_pad.at(i, m - back + 1))
                        bank = PS[item_bank(m)]
                        if m < N:
                            ins = pe.matmul(bank[:, :], CS[:, 0, tok], w(s, "wk")[:, cols], start=True, stop=True)
                        else:
                            for c in range(KD):
                                ins = pe.matmul(bank[:, :], XS[:, c, tok], wq[:, c, cols], start=(c == 0), stop=(c == KD - 1))
                        ins.then_inc(q_ps.sem, 1)

                    def turn_item(i, m):
                        pe.wait_ge(qk_pad.sem, qk_pad.at(i, m + 1))
                        back = 1 if m > N else 2
                        if m >= back:
                            pe.wait_ge(qT_sb.sem, qT_sb.at(i, m - back + 1))
                        for c in range(4):
                            ins = pe.transpose(PS[itemT_bank(m)][:, c * P:(c + 1) * P], QN[:, m % 2, c * P:(c + 1) * P], IDENT[:, :])
                        ins.then_inc(qkT_ps.sem, 1)

                    def queries(i, t):
                        b, part = divmod(t, 4)
                        if t >= 2:
                            pe.wait_ge(qT_sb.sem, qT_sb.at(i, t - 1))
                        for c in range(4):
                            h = 4 * part + c
                            for k in range(KD):
                                ins = pe.matmul(PS[6 + t % 2][:, c * P:(c + 1) * P], wq[:, k, h * P:(h + 1) * P],
                                                XS[:, k, b * TOK:(b + 1) * TOK], start=(k == 0), stop=(k == KD - 1))
                        ins.then_inc(q_ps.sem, 1)

                    def scores(i, t):
                        b, part = divmod(t, 4)
                        pe.wait_ge(qT_sb.sem, qT_sb.at(i, NR - N + t + 1 if rms else t + 1))
                        if t == 0:
                            pe.wait_ge(v_sb.sem, v_sb.at(i, NKV))
                        if t >= 2:
                            pe.wait_ge(s_sub.sem, s_sub.at(i, t - 1))
                        if not rms:
                            mask = mgroup[0:1, b * TOK:(b + 1) * TOK]
                            pe.matmul(PS[t % 2][:, :].rearrange("p (h c) -> p h c", h=4), ONESB[0:1, :],
                                      mask.unsqueeze(1).broadcast_to([1, 4, TOK]), start=True, stop=False,
                                      skip_group_check=True)
                        for c in range(4):
                            h = 4 * part + c
                            ins = pe.matmul(PS[t % 2][:, c * P:(c + 1) * P], QTS[:, t % 2, c * P:(c + 1) * P],
                                            kT[:, b, h if rms else h // 2, :], start=rms, stop=True, skip_group_check=True)
                        ins.then_inc(s_ps.sem, 1)

                    def turn_probs(i, t):
                        pe.wait_ge(p_norm.sem, p_norm.at(i, t + 1))
                        d = 1 if rms else 2
                        if t >= d:
                            pe.wait_ge(pT_sb.sem, pT_sb.at(i, t - d + 1))
                        for c in range(4):
                            ins = pe.transpose(PS[probs_bank(t)][:, c * P:(c + 1) * P], PR[:, t % 2, c * P:(c + 1) * P], IDENT[:, :])
                        ins.then_inc(pT_ps.sem, 1)

                    def values(i, t):
                        b, part = divmod(t, 4)
                        pe.wait_ge(pT_sb.sem, pT_sb.at(i, t + 1))
                        if t:
                            pe.wait_ge(oT_sb.sem, oT_sb.at(i, t))
                        n = 4 if rms else 2
                        for c in range(n):
                            cols = slice(c * 512 // n, (c + 1) * 512 // n)
                            g = n * part + c
                            ins = pe.matmul(PS[4][:, cols], vs[:, b, g * P:(g + 1) * P], PTS[:, t % 2, cols], start=True, stop=True)
                        ins.then_inc(av_ps.sem, 1)

                    def project_out(i, t):
                        b, part = divmod(t, 4)
                        pe.wait_ge(oT_sb.sem, oT_sb.at(i, t + 1))
                        if part == 0:
                            pe.wait_ge(x_done.sem, x_done.at(i, b))
                        for c in range(4):
                            ins = pe.matmul(PS[5][:, 0:DIM], OTS[:, t % 2, c * P:(c + 1) * P], wo[:, 4 * part + c, :],
                                            start=(part == 0 and c == 0), stop=(part == 3 and c == 3))
                        ins.then_inc(out_ps.sem, 1)

                    with pe.Fori(0, turns) as i:
                        pe.wait_ge(copied.sem, copied.at(i, 1))
                        pe.wait_ge(ctx_loaded.sem, ctx_loaded.at(i, 16))
                        pe.wait_ge(x_done.sem, x_done.at(i, 0))
                        if rms:
                            for m in range(N + 2):
                                if m < N:
                                    item(i, m)
                                    values_of(i, m)
                                if m == N:
                                    item(i, m)
                                if m >= 2:
                                    turn_item(i, m - 2)
                        else:
                            for n in range(NKV):
                                keys_values(i, n)
                        for t in range(END):
                            if rms:
                                if 1 <= t < N:
                                    item(i, N + t)
                            elif t < N:
                                queries(i, t)
                            if 0 <= t - lag < N:
                                scores(i, t - lag)
                            if rms and 0 <= t - 1 < N:
                                turn_item(i, N + t - 1)
                            if 0 <= t - lag - 2 < N:
                                turn_probs(i, t - lag - 2)
                            if 0 <= t - lag - 3 < N:
                                values(i, t - lag - 3)
                            if 0 <= t - lag - 4 < N:
                                project_out(i, t - lag - 4)

                @block.vector
                def _(dve):
                    if not rms:
                        dve.wait_ge(mask_loaded.sem, 16)
                        dve.tensor_scalar(mrow, mraw, 1.0, BIG, ALU.subtract, ALU.mult).then_inc(gained.sem, 1)

                    def norm_item(ch, i, m):
                        dve.wait_ge(sq_done.sem, sq_done.at(i, m + 1))
                        ch.link(dve.tensor_reduce(qsum[:, m % 2, :], SQ[:, m % 2, :].rearrange("p (h c) -> p h c", h=4), AX, ALU.add))
                        dve.tensor_scalar(qvar[:, m % 2, :], qsum[:, m % 2, :], 1.0 / P, 1e-5, ALU.mult, ALU.add).then_inc(rstd_in.sem, 1)

                    def scale_item(ch, i, m):
                        dve.wait_ge(rstd_out.sem, rstd_out.at(i, m + 1))
                        if m >= 2:
                            dve.wait_ge(qkT_ps.sem, qkT_ps.at(i, m - 1))
                        src = PS[item_bank(m)][:, :].rearrange("p (h c) -> p h c", h=4)
                        dve.tensor_tensor(QN[:, m % 2, :].rearrange("p (h c) -> p h c", h=4), src,
                                          qrstd[:, m % 2, :].unsqueeze(2).broadcast_to([P, 4, P]), ALU.mult).then_inc(qk_pad.sem, 1)

                    def subtract_max(ch, i, t):
                        S = PS[t % 2][:, :].rearrange("p (h c) -> p h c", h=4)
                        dve.wait_ge(s_ps.sem, s_ps.at(i, t + 1))
                        ch.link(dve.tensor_reduce(nmax[:, t % 2, :], S, AX, ALU.max, negate=True))
                        if t >= 2:
                            dve.wait_ge(pT_ps.sem, pT_ps.at(i, t - 1))
                        dve.tensor_tensor(PR[:, t % 2, :].rearrange("p (h c) -> p h c", h=4), S,
                                          nmax[:, t % 2, :].unsqueeze(2).broadcast_to([P, 4, P]), ALU.add).then_inc(s_sub.sem, 1)

                    def sums(ch, i, t):
                        pr = PR[:, t % 2, :].rearrange("p (h c) -> p h c", h=4)
                        psum_ = psums[:, t % 2, :]
                        dve.wait_ge(p_exp.sem, p_exp.at(i, t + 1))
                        ch.link(dve.tensor_reduce(psum_, pr, AX, ALU.add))
                        dve.reciprocal(psum_, psum_).then_inc(p_sum.sem, 1)

                    with dve.Fori(0, turns) as i:
                        ch = Chain(dve, dve_step, i)
                        if rms:
                            norm_item(ch, i, 0)
                            for m in range(N):
                                if m + 1 < N:
                                    norm_item(ch, i, m + 1)
                                scale_item(ch, i, m)
                        for t in range(END):
                            b, late = divmod(t - lag - 5 - 3, 4)
                            if late == 0 and 0 <= b < W:
                                dve.wait_ge(out_ps.sem, out_ps.at(i, 4 * b + 4))
                                xb = X[:, bass.ds(i * W + b, 1), :].rearrange("p a d -> p (a d)")
                                dve.scalar_tensor_tensor(out=xb, in0=PS[5][:, 0:DIM], scalar=TG[:, tg:tg + 1], in1=xb,
                                                         op0=ALU.mult, op1=ALU.add).then_inc(x_done.sem, 1)
                            if rms and t < N:
                                norm_item(ch, i, N + t)
                            if 0 <= t - lag < N:
                                subtract_max(ch, i, t - lag)
                            if rms and t < N:
                                scale_item(ch, i, N + t)
                            if 0 <= t - lag - 1 < N:
                                sums(ch, i, t - lag - 1)
                        ch.close()

                @block.scalar
                def _(act):
                    if rms:
                        act.wait_ge(w_loaded[s].sem, 32)

                    def square_item(i, m):
                        act.wait_ge(q_ps.sem, q_ps.at(i, m + 1))
                        if m >= 2:
                            act.wait_ge(rstd_in.sem, rstd_in.at(i, m - 1))
                        act.activation(SQ[:, m % 2, :], PS[item_bank(m)][:, :], ACT.Square).then_inc(sq_done.sem, 1)

                    def item_out(i, m):
                        act.wait_ge(qkT_ps.sem, qkT_ps.at(i, m + 1))
                        src = PS[itemT_bank(m)][:, :]
                        if m < N:
                            b, part = divmod(m, 4)
                            dst = kT[:, b, 4 * part:4 * part + 4, :]
                            src = src.rearrange("p (h t) -> p h t", h=4)
                        else:
                            if m >= N + 2:
                                act.wait_ge(s_ps.sem, s_ps.at(i, m - N - 1))
                            dst = QTS[:, m % 2, :]
                        act.activation(dst, src, ACT.Copy, scale=w(s, "gk" if m < N else "gq")).then_inc(qT_sb.sem, 1)

                    def keys_values_out(i, n):
                        act.wait_ge(v_ps.sem, v_ps.at(i, n + 1))
                        if rms:
                            b, part = divmod(n, 4)
                            act.copy(vs[:, b, part * 512:(part + 1) * 512], PS[value_bank(n)][:, :]).then_inc(v_sb.sem, 1)
                        elif n < 8:
                            act.copy(kT[:, :, n, :], PS[n % 4][:, :].rearrange("p (b t) -> p b t", b=W)).then_inc(v_sb.sem, 1)
                        else:
                            b, half = divmod(n - 8, 2)
                            act.activation(vs[:, b, half * 512:(half + 1) * 512], PS[n % 4][:, :], ACT.Copy,
                                           scale=mcol[:, b:b + 1]).then_inc(v_sb.sem, 1)

                    def queries_out(i, t):
                        act.wait_ge(q_ps.sem, q_ps.at(i, t + 1))
                        if t >= 2:
                            act.wait_ge(s_ps.sem, s_ps.at(i, t - 1))
                        act.copy(QTS[:, t % 2, :], PS[6 + t % 2][:, :]).then_inc(qT_sb.sem, 1)

                    def exponent(i, t):
                        act.wait_ge(s_sub.sem, s_sub.at(i, t + 1))
                        act.activation(PR[:, t % 2, :], PR[:, t % 2, :], ACT.Exp, scale=float(P) ** -0.5).then_inc(p_exp.sem, 1)

                    def probs_out(i, t):
                        act.wait_ge(pT_ps.sem, pT_ps.at(i, t + 1))
                        if t >= 2:
                            act.wait_ge(av_ps.sem, av_ps.at(i, t - 1))
                        act.copy(PTS[:, t % 2, :], PS[probs_bank(t)][:, :]).then_inc(pT_sb.sem, 1)

                    def attended(i, t):
                        act.wait_ge(av_ps.sem, av_ps.at(i, t + 1))
                        if t >= 2:
                            act.wait_ge(out_ps.sem, out_ps.at(i, t - 1))
                        act.copy(OTS[:, t % 2, :], PS[4][:, :]).then_inc(oT_sb.sem, 1)

                    with act.Fori(0, turns) as i:
                        if rms:
                            for m in range(N + 2):
                                if m < N:
                                    square_item(i, m)
                                    keys_values_out(i, m)
                                if m >= 2:
                                    item_out(i, m - 2)
                        else:
                            for n in range(NKV):
                                keys_values_out(i, n)
                        for t in range(END):
                            if rms and t < N:
                                square_item(i, N + t)
                            if not rms and t < N:
                                queries_out(i, t)
                            if rms and 0 <= t - 1 < N:
                                item_out(i, N + t - 1)
                            if 0 <= t - lag < N:
                                exponent(i, t - lag)
                            if 0 <= t - lag - 2 < N:
                                probs_out(i, t - lag - 2)
                            if 0 <= t - lag - 3 < N:
                                attended(i, t - lag - 3)
                        act.sem_inc(act_step.sem, STEPS)

        def ffn_block(s, kind, pairs, tg=None, MODT=None):
            mod, moe = kind == "mod", kind == "moe"
            NF = UH // P
            T = 2 * TURNS
            HALF = UNIT // 2
            begin(pairs, dve_step=STEPS, gu_ps=T * NF, silu_done=T * NF, h_done=T * NF, down_ps=T * NF, x_done=T)
            begin(1, w_hi=4 * pairs, w_lo=4 * pairs, x_hi=1 + T * pairs, x_lo=1 + T * pairs, q_ps=TURNS * mod,
                  qk_pad=mod, p_norm=7 * mod, raw_loaded0=16 * (pairs - 1), raw_loaded1=16 * (pairs - 1))
            WHI, WLO = tile("WHI", [P, 2, UNIT], F32R), tile("WLO", [P, 2, UNIT], F32R)
            XHI, XLO = tile("XHI", [P, 2, KD, GT], F32R), tile("XLO", [P, 2, KD, GT], F32R)
            H = tile("H", [P, 2, GT])
            HHI, HLO = tile("HHI", [P, 2, GT], F32R), tile("HLO", [P, 2, GT], F32R)
            scale = tile("scale", [P, 2, BATCH]) if moe else None
            BM = tile("BM", [MODK, FF], F32R) if mod else None
            modb = tile("modb", [MODK, FF]) if mod else None
            MH = tile("MH", [MODK, BATCH * TOK], F32R) if mod else None
            raw = [w(s, "unit0"), w(s, "unit1")]

            def gate_or_up(tile_, a, which, k, f):
                at = which * KD * UH + k * UH + f * P
                return tile_[:, a, at:at + P]

            def down(tile_, a, f):
                at = 2 * KD * UH + f * DIM
                return tile_[:, a, at:at + DIM]

            def all_pairs(eng, body):
                if pairs == 1:
                    body(0)
                else:
                    with eng.Fori(0, pairs) as q:
                        body(q)

            def split_ahead(eng, first, x_part, w_part, per_step=None):
                def body(q, more):
                    for t in range(T):
                        a, g = divmod(t, TURNS)
                        for f in range(NF):
                            if per_step:
                                per_step(q, NF * t + f)
                            if f == 1:
                                x_part(q, t + 1)
                            if f == 2 and g in (1, 2) and (a == 0 or more):
                                w_part(q, a, g - 1)
                first()
                if pairs > 1:
                    with eng.Fori(0, pairs - 1) as q:
                        body(q, True)
                body(pairs - 1, False)

            with nc.Block() as block:
                if mod:
                    @block.sync
                    def _(sp):
                        sp.dma_start(modb[:, :], modb_in).then_inc(modb_loaded.sem, 16)

                if moe:
                    @block.sync
                    def _(sp):
                        with sp.Fori(1, pairs) as q:
                            for a in range(2):
                                sp.wait_ge(w_lo.sem, w_lo.at(0, 4 * q + (2 * a - 2)))
                                sp.dma_start(raw[a], experts_in[:, bass.ds(2 * q + (a - 2), 1), :].rearrange("p a n -> p (a n)"))\
                                    .then_inc(raw_loaded[a].sem, 16)

                @block.tensor
                def _(pe):
                    if mod:
                        for g in range(TURNS):
                            for k in range(KD):
                                ins = pe.matmul(PS[4 + g][0:MODK, :], wk(s, "a2", KD)[:, k, :], XNT[:, k, g * GT:(g + 1) * GT],
                                                start=(k == 0), stop=(k == KD - 1))
                            ins.then_inc(q_ps.sem, 1)
                        pe.wait_ge(qk_pad.sem, qk_pad.at(0, 1))

                    def gate_up(q, n):
                        t, f = divmod(n, NF)
                        a, g = divmod(t, TURNS)
                        if n >= 2:
                            pe.wait_ge(h_done.sem, h_done.at(q, n - 1))
                        for which in range(2):
                            bank = PS[2 * which + n % 2]
                            if mod and which == 0:
                                at = a * UH + f * P
                                pe.matmul(bank[:, :], BM[:, at:at + P], MH[:, g * GT:(g + 1) * GT],
                                          start=True, stop=False)
                            for k in range(KD):
                                for m, (wt, xt) in enumerate(((WHI, XHI), (WLO, XHI), (WHI, XLO))):
                                    ins = pe.matmul(bank[:, :], gate_or_up(wt, a, which, k, f), xt[:, t % 2, k, :],
                                                    start=(k == 0 and m == 0 and not (mod and which == 0)),
                                                    stop=(k == KD - 1 and m == 2))
                        ins.then_inc(gu_ps.sem, 1)

                    def project_down(q, n):
                        t, f = divmod(n, NF)
                        a = t // TURNS
                        pe.wait_ge(h_done.sem, h_done.at(q, n + 1))
                        if f == 0:
                            pe.wait_ge(x_done.sem, x_done.at(q, max(t - 1, 0)))
                        for b in range(GROUP):
                            bank = PS[4 + 2 * (t % 2) + b // 2]
                            tok = slice(b * TOK, (b + 1) * TOK)
                            for m, (ht, wt) in enumerate(((HHI, WHI), (HLO, WHI), (HHI, WLO))):
                                ins = pe.matmul(bank[:, b % 2 * DIM:(b % 2 + 1) * DIM], ht[:, n % 2, tok], down(wt, a, f),
                                                start=(f == 0 and b % 2 == 0 and m == 0), stop=(f == NF - 1 and m == 2),
                                                skip_group_check=True)
                        ins.then_inc(down_ps.sem, 1)

                    def pair(q):
                        for n in range(T * NF):
                            if n % NF == 0:
                                pe.wait_ge(x_lo.sem, x_lo.at(0, T * q + (n // NF + 1)))
                                if n % (T * NF // 2) == 0:
                                    pe.wait_ge(w_lo.sem, w_lo.at(0, 4 * q + (2 * (n // (T * NF // 2)) + 2)))
                            gate_up(q, n)
                            if n:
                                project_down(q, n - 1)
                        project_down(q, T * NF - 1)

                    all_pairs(pe, pair)

                @block.scalar
                def _(act):
                    act.wait_ge(w_loaded[s].sem, 32)

                    def w_high(a, j):
                        cols = slice(j * HALF, (j + 1) * HALF)
                        act.copy(WHI[:, a, cols], raw[a][:, cols]).then_inc(w_hi.sem, 1)

                    def x_high(t):
                        g = t % TURNS
                        act.copy(XHI[:, t % 2, :, :], XNT[:, :, g * GT:(g + 1) * GT]).then_inc(x_hi.sem, 1)

                    def first():
                        w_high(0, 0)
                        x_high(0)
                        w_high(0, 1)

                    def x_part(q, t):
                        act.wait_ge(gu_ps.sem, gu_ps.at(q, NF * (t - 1)))
                        x_high(t)

                    def w_part(q, a, j):
                        if moe:
                            act.wait_ge(raw_loaded[1 - a].sem, raw_loaded[1 - a].at(0, 16 * (q + a)))
                        act.wait_ge(down_ps.sem, down_ps.at(q, a * T * NF // 2))
                        w_high(1 - a, j)

                    def silu(q, n):
                        act.wait_ge(gu_ps.sem, gu_ps.at(q, n + 1))
                        if n >= 2:
                            act.wait_ge(h_done.sem, h_done.at(q, n - 1))
                        act.activation(H[:, n % 2, :], PS[n % 2][:, :], ACT.Silu).then_inc(silu_done.sem, 1)

                    split_ahead(act, first, x_part, w_part, silu)

                @block.gpsimd
                def _(pool):
                    def w_low(count_, a, j):
                        pool.wait_ge(w_hi.sem, w_hi.at(0, count_))
                        cols = slice(j * HALF, (j + 1) * HALF)
                        pool.tensor_tensor(WLO[:, a, cols], raw[a][:, cols], WHI[:, a, cols].bitcast(F32),
                                           ALU.subtract).then_inc(w_lo.sem, 1)

                    def x_low(count_, t):
                        pool.wait_ge(x_hi.sem, x_hi.at(0, count_))
                        g = t % TURNS
                        pool.tensor_tensor(XLO[:, t % 2, :, :], XNT[:, :, g * GT:(g + 1) * GT],
                                           XHI[:, t % 2, :, :].bitcast(F32), ALU.subtract).then_inc(x_lo.sem, 1)

                    def first():
                        w_low(1, 0, 0)
                        x_low(1, 0)
                        w_low(2, 0, 1)

                    split_ahead(pool, first, lambda q, t: x_low(T * q + (t + 1), t),
                                lambda q, a, j: w_low(4 * q + (2 * a + 3 + j), 1 - a, j))

                @block.vector
                def _(dve):
                    if mod:
                        mch = Chain(dve, p_norm)
                        dve.wait_ge(modb_loaded.sem, 16)
                        mch.link(dve.tensor_copy(BM[:, :], modb[:, :]))
                        mid, last = slice(32, 32 + RANK), slice(64, MODK)
                        mch.step(dve.tensor_tensor(BM[mid, :], modb[mid, :], BM[mid, :].bitcast(F32), ALU.subtract))
                        for g in range(TURNS):
                            dve.wait_ge(q_ps.sem, q_ps.at(0, g + 1))
                            m = MODT[:, g * GT:(g + 1) * GT]
                            mch.step(dve.scalar_tensor_tensor(out=m, in0=PS[4 + g][0:MODK, :], scalar=0.1, in1=m,
                                                              op0=ALU.mult, op1=ALU.mult))
                        mch.settle()
                        mch.link(dve.tensor_copy(MH[:, :], MODT[:, :]))
                        dve.tensor_tensor(MH[last, :], MODT[last, :], MH[last, :].bitcast(F32),
                                          ALU.subtract).then_inc(qk_pad.sem, 1)

                    def hidden(ch, q, n):
                        dve.wait_ge(silu_done.sem, silu_done.at(q, n + 1))
                        h = H[:, n % 2, :]
                        ch.link(dve.tensor_tensor(h, h, PS[2 + n % 2][:, :], ALU.mult))
                        if n >= 2:
                            dve.wait_ge(down_ps.sem, down_ps.at(q, n - 1))
                        ch.link(dve.tensor_copy(HHI[:, n % 2, :], h))
                        dve.tensor_tensor(HLO[:, n % 2, :], h, HHI[:, n % 2, :].bitcast(F32), ALU.subtract).then_inc(h_done.sem, 1)

                    def combine(ch, q, t):
                        a, g = divmod(t, TURNS)
                        dve.wait_ge(down_ps.sem, down_ps.at(q, NF * (t + 1)))
                        dve.wait_ge(x_done.sem, x_done.at(q, t))
                        for b in range(GROUP):
                            xb = X[:, g * GROUP + b, :]
                            bank = PS[4 + 2 * (t % 2) + b // 2]
                            k = g * GROUP + b
                            ins = dve.scalar_tensor_tensor(out=xb, in0=bank[:, b % 2 * DIM:(b % 2 + 1) * DIM],
                                                           scalar=scale[:, a, k:k + 1] if moe else TG[:, tg:tg + 1],
                                                           in1=xb, op0=ALU.mult, op1=ALU.add)
                            if b < GROUP - 1:
                                ch.step(ins)
                        ins.then_inc(x_done.sem, 1)

                    def pair(q):
                        ch = Chain(dve, dve_step, q)
                        if moe:
                            dve.wait_ge(x_done.sem, x_done.at(q, 0))
                            for a in range(2):
                                ch.step(dve.tensor_copy(scale[:, a, :], RW[:, :, bass.ds(2 * q + a, 1)].rearrange("p b e -> p (b e)")))
                            ch.settle()
                        for n in range(T * NF):
                            hidden(ch, q, n)
                            if n % NF == 1 and n > NF:
                                combine(ch, q, n // NF - 1)
                        combine(ch, q, T - 1)
                        ch.close()

                    all_pairs(dve, pair)

        def quant_block(s, tg):
            begin(TURNS, dve_step=STEPS, act_step=STEPS, copied=1, gu_ps=GROUP, silu_done=GROUP, h_done=GROUP,
                  o_tok=GROUP, pT_ps=GROUP, pT_sb=GROUP, down_ps=GROUP, x_done=GROUP, rstd_in=1)
            begin(1, s_ps=1, s_sub=1, gained=1, p_exp=1)
            NCH = HID0P // P
            WB = tile("WB", [P, WIDTH[s]], BF16)
            XS = tile("XS", [P, KD, GT])
            w1 = WB[:, 0:KD * HID0].rearrange("p (k n) -> p k n", k=KD)
            w3 = WB[:, KD * HID0:2 * KD * HID0].rearrange("p (k n) -> p k n", k=KD)
            w2 = WB[:, 2 * KD * HID0:].rearrange("p (k n) -> p k n", k=NCH)
            XQT = XNT[:, 0, :].bitcast(BF16).rearrange("p (k t) -> p k t", k=KD)
            XSB = XS[:, 0, :].bitcast(BF16).rearrange("p (k t) -> p k t", k=KD)
            SG = tile("SG", [P, 2, HID0])
            H, Y = tile("H", [P, HID0])[:, :], tile("Y", [P, HID0])[:, :]
            HQ, HT = tile("HQ", [P, 2, HID0P], BF16), tile("HT", [P, 2, HID0P], BF16)
            halves = ((0, 512), (512, HID0))

            def hidden_bank(b, which, c):
                lo, hi = halves[c]
                if c == 0:
                    return PS[3 * (b % 2) + which][:, 0:512]
                return PS[3 * (b % 2) + 2][:, which * (hi - lo):(which + 1) * (hi - lo)]

            wsum, wmean, wstep = STAT[:, 0:3], STAT[:, 4:7], STAT[:, 8:11]
            cg, cu = STAT[:, 16:16 + GROUP], STAT[:, 24:24 + GROUP]
            hmax, hinv, hout = STAT[:, 32:33], STAT[:, 34:35], STAT[:, 36:38]
            parts = (("w1", 0, KD * HID0), ("w3", KD * HID0, 2 * KD * HID0), ("w2", 2 * KD * HID0, WIDTH[s]))
            with nc.Block() as block:
                @block.gpsimd
                def _(pool):
                    with pool.Fori(0, TURNS) as i:
                        pool.wait_ge(gu_ps.sem, gu_ps.at(i, 0))
                        pool.tensor_copy(XSB[:, :, :], XQT[:, :, bass.ds(i * GT, GT)]).then_inc(copied.sem, 1)

                @block.tensor
                def _(pe):
                    pe.wait_ge(s_ps.sem, s_ps.at(0, 1))
                    pe.matmul(PS[7][:, 0:3], ONES[:, :], wsum, start=True, stop=True).then_inc(s_sub.sem, 1)
                    pe.wait_ge(gained.sem, gained.at(0, 1))

                    def gate_up(i, b):
                        if b >= 2:
                            pe.wait_ge(h_done.sem, h_done.at(i, b - 1))
                        tok = slice(b * TOK, (b + 1) * TOK)
                        for n, m in enumerate((w1, w3)):
                            for c, (lo, hi) in enumerate(halves):
                                for k in range(KD):
                                    ins = pe.matmul(hidden_bank(b, n, c), XSB[:, k, tok], m[:, k, lo:hi],
                                                    start=(k == 0), stop=(k == KD - 1))
                        ins.then_inc(gu_ps.sem, 1)

                    def turn_hidden(i, b):
                        pe.wait_ge(o_tok.sem, o_tok.at(i, b + 1))
                        pe.wait_ge(pT_sb.sem, pT_sb.at(i, b))
                        for c in range(NCH):
                            ins = pe.transpose(PSB[6][:, c * P:(c + 1) * P], HQ[:, b % 2, c * P:(c + 1) * P], IDENTB[:, :])
                        ins.then_inc(pT_ps.sem, 1)

                    def project_down(i, b):
                        pe.wait_ge(pT_sb.sem, pT_sb.at(i, b + 1))
                        pe.wait_ge(x_done.sem, x_done.at(i, b))
                        for c in range(NCH):
                            ins = pe.matmul(PS[7][:, 0:DIM], HT[:, b % 2, c * P:(c + 1) * P], w2[:, c, :],
                                            start=(c == 0), stop=(c == NCH - 1))
                        ins.then_inc(down_ps.sem, 1)

                    with pe.Fori(0, TURNS) as i:
                        pe.wait_ge(copied.sem, copied.at(i, 1))
                        gate_up(i, 0)
                        for b in range(GROUP):
                            if b + 1 < GROUP:
                                gate_up(i, b + 1)
                            turn_hidden(i, b)
                            project_down(i, b)

                @block.scalar
                def _(act):
                    with act.Fori(0, TURNS) as i:
                        act.wait_ge(rstd_in.sem, rstd_in.at(i, 1))
                        ch = Chain(act, act_step, i)

                        def hidden_out(b):
                            act.wait_ge(pT_ps.sem, pT_ps.at(i, b + 1))
                            act.copy(HT[:, b % 2, :], PSB[6][:, 0:HID0P]).then_inc(pT_sb.sem, 1)

                        for b in range(GROUP):
                            act.wait_ge(gu_ps.sem, gu_ps.at(i, b + 1))
                            for c, (lo, hi) in enumerate(halves):
                                ins = act.activation(SG[:, b % 2, lo:hi], hidden_bank(b, 0, c), ACT.Silu, scale=cg[:, b:b + 1])
                                if c == 0:
                                    ch.step(ins)
                            ins.then_inc(silu_done.sem, 1)
                            if b:
                                hidden_out(b - 1)
                        hidden_out(GROUP - 1)
                        ch.close()

                @block.vector
                def _(dve):
                    dve.wait_ge(w_loaded[s].sem, 32)
                    for n, (_, lo, hi) in enumerate(parts):
                        ins = dve.tensor_reduce(wsum[:, n:n + 1], WREG[s % 2][:, lo:hi], AX, ALU.add, apply_absolute_value=True)
                    ins.then_inc(s_ps.sem, 1)
                    dve.wait_ge(s_sub.sem, s_sub.at(0, 1))
                    ch = Chain(dve, p_exp)
                    dve.tensor_scalar(wmean, PS[7][:, 0:3], 1.0 / (HID0 * DIM), 1e-5, ALU.mult, ALU.max).then_inc(quant_step.sem, 1)
                    dve.wait_ge(quant_step.sem, 1)
                    dve.reciprocal(wstep, wmean).then_inc(quant_step.sem, 1)
                    dve.wait_ge(quant_step.sem, 2)
                    for n, (_, lo, hi) in enumerate(parts):
                        m = WREG[s % 2][:, lo:hi]
                        ins = dve.tensor_scalar(m, m, wstep[:, n:n + 1], MAGIC, ALU.mult, ALU.add)
                    ins.then_inc(quant_step.sem, 1)
                    dve.wait_ge(quant_step.sem, 3)
                    m = WREG[s % 2][:, 0:WIDTH[s]]
                    dve.tensor_scalar(m, m, MAGIC + 1.0, MAGIC - 1.0, ALU.min, ALU.max).then_inc(quant_step.sem, 1)
                    dve.memset(HQ[:, :, :], 0.0)
                    dve.wait_ge(quant_step.sem, 4)
                    dve.tensor_scalar(WB[:, :], m, MAGIC, None, ALU.subtract).then_inc(gained.sem, 1)

                    def hidden(ch, i, b):
                        dve.wait_ge(silu_done.sem, silu_done.at(i, b + 1))
                        for c, (lo, hi) in enumerate(halves):
                            ins = dve.scalar_tensor_tensor(out=H[:, lo:hi], in0=hidden_bank(b, 1, c), scalar=cu[:, b:b + 1],
                                                           in1=SG[:, b % 2, lo:hi], op0=ALU.mult, op1=ALU.mult)
                            if c == 0:
                                ch.step(ins)
                        ins.then_inc(h_done.sem, 1)
                        ch.settle()
                        dve.wait_ge(h_done.sem, h_done.at(i, b + 1))
                        ch.link(dve.tensor_reduce(hmax, H, AX, ALU.max, apply_absolute_value=True))
                        ch.link(dve.tensor_scalar(hmax, hmax, 1e-5, None, ALU.max))
                        ch.step(dve.reciprocal(hinv, hmax))
                        ch.step(dve.tensor_scalar(hout[:, b % 2:b % 2 + 1], hmax, 1.0 / 127.0, wmean[:, 2:3], ALU.mult, ALU.mult))
                        ch.settle()
                        ch.step(dve.tensor_scalar(hinv, hinv, 127.0, None, ALU.mult))
                        ch.step(dve.tensor_scalar(hout[:, b % 2:b % 2 + 1], hout[:, b % 2:b % 2 + 1], TG[:, tg:tg + 1], None, ALU.mult))
                        ch.settle()
                        ch.link(dve.tensor_scalar(Y, H, hinv, MAGIC, ALU.mult, ALU.add))
                        ch.link(dve.tensor_scalar(Y, Y, MAGIC + 127.0, MAGIC - 128.0, ALU.min, ALU.max))
                        if b >= 2:
                            dve.wait_ge(pT_ps.sem, pT_ps.at(i, b - 1))
                        dve.tensor_scalar(HQ[:, b % 2, 0:HID0], Y, MAGIC, None, ALU.subtract).then_inc(o_tok.sem, 1)

                    def add_out(i, b):
                        dve.wait_ge(down_ps.sem, down_ps.at(i, b + 1))
                        xb = X[:, bass.ds(i * GROUP + b, 1), :].rearrange("p a d -> p (a d)")
                        dve.scalar_tensor_tensor(out=xb, in0=PS[7][:, 0:DIM], scalar=hout[:, b % 2:b % 2 + 1], in1=xb,
                                                 op0=ALU.mult, op1=ALU.add).then_inc(x_done.sem, 1)

                    with dve.Fori(0, TURNS) as i:
                        ch = Chain(dve, dve_step, i)
                        ch.step(dve.tensor_scalar(cu, AQ[:, bass.ds(i * GROUP, GROUP)], wmean[:, 1:2], None, ALU.mult))
                        dve.tensor_scalar(cg, AQ[:, bass.ds(i * GROUP, GROUP)], wmean[:, 0:1], None, ALU.mult).then_inc(rstd_in.sem, 1)
                        for b in range(GROUP):
                            hidden(ch, i, b)
                            if b:
                                add_out(i, b - 1)
                        add_out(i, GROUP - 1)
                        ch.close()
                    dve.sem_inc(p_exp.sem, 1)

        def router_block(s, tg):
            begin(1, dve_step=STEPS, p_exp=1, s_ps=1)
            rt = wk(s, "router", KD)
            BE = BATCH * EXPERTS
            work = tile("work", [P, 7 * BE])
            area = lambda n, c=BE: work[:, n * BE:n * BE + c]
            three = lambda n: area(n).rearrange("p (b e) -> p b e", e=EXPERTS)
            eq, run, first1, rest, first2, wide = (three(n) for n in range(6))
            m1, m2, ex, s1, s2 = (area(6)[:, n * BATCH:(n + 1) * BATCH] for n in range(5))
            L = RW[:, :, 2:2 + EXPERTS]

            def wide_of(v):
                return v.unsqueeze(2).broadcast_to([P, BATCH, EXPERTS])

            with nc.Block() as block:
                @block.tensor
                def _(pe):
                    pe.wait_ge(w_loaded[s].sem, 32)
                    for b in range(BATCH):
                        for k in range(KD):
                            ins = pe.matmul(PS[0][:, b * EXPERTS:(b + 1) * EXPERTS], XNT[:, k, b * TOK:(b + 1) * TOK],
                                            rt[:, k, :], start=(k == 0), stop=(k == KD - 1))
                    ins.then_inc(s_ps.sem, 1)

                @block.vector
                def _(dve):
                    ch = Chain(dve, dve_step)
                    dve.wait_ge(s_ps.sem, s_ps.at(0, 1))
                    ch.link(dve.tensor_copy(L, PS[0][:, 0:BE].rearrange("p (b e) -> p b e", e=EXPERTS)))

                    def first_of(logits, top, dst):
                        ch.link(dve.tensor_reduce(top, logits, AX, ALU.max))
                        ch.link(dve.tensor_tensor(eq, logits, wide_of(top), ALU.is_equal))
                        ch.link(dve.tensor_copy(run[:, :, 0:1], eq[:, :, 0:1]))
                        for e in range(1, EXPERTS):
                            ch.link(dve.tensor_tensor(run[:, :, e:e + 1], run[:, :, e - 1:e], eq[:, :, e:e + 1], ALU.add))
                        ch.link(dve.tensor_scalar(run, run, 1.0, None, ALU.is_le))
                        ch.link(dve.tensor_tensor(dst, run, eq, ALU.mult))

                    ch.step(dve.tensor_scalar(RW[:, :, 0:2], ONES[:, 0:2 * BATCH].rearrange("p (b e) -> p b e", e=2),
                                              TG[:, tg:tg + 1], None, ALU.mult))
                    first_of(L, m1, first1)
                    ch.link(dve.scalar_tensor_tensor(out=rest, in0=first1, scalar=-BIG, in1=L, op0=ALU.mult, op1=ALU.add))
                    first_of(rest, m2, first2)
                    dve.tensor_tensor(ex, m2, m1, ALU.subtract).then_inc(quant_step.sem, 1)
                    dve.wait_ge(p_exp.sem, p_exp.at(0, 1))
                    ch.link(dve.tensor_scalar(s1, ex, 1.0, None, ALU.add))
                    ch.link(dve.reciprocal(s1, s1))
                    ch.link(dve.tensor_scalar(s1, s1, TG[:, tg:tg + 1], None, ALU.mult))
                    ch.link(dve.tensor_tensor(s2, s1, ex, ALU.mult))
                    ch.step(dve.tensor_tensor(first1, first1, wide_of(s1), ALU.mult))
                    ch.step(dve.tensor_tensor(first2, first2, wide_of(s2), ALU.mult))
                    ch.settle()
                    ch.link(dve.tensor_tensor(L, first1, first2, ALU.add))
                    ch.close()

                @block.scalar
                def _(act):
                    act.wait_ge(quant_step.sem, 5)
                    act.activation(ex, ex, ACT.Exp).then_inc(p_exp.sem, 1)

        def last_block():
            with nc.Block() as block:
                @block.sync
                def _(sp):
                    sp.dma_start(out, X[:, :, :]).then_inc(stored.sem, 16)
                    sp.wait_ge(stored.sem, 16)

        with ExitStack() as area:
            scope[0] = area
            first_block()
        held = ExitStack()
        keep = []

        def modulation(first):
            if first:
                keep.append(held.enter_context(nc.sbuf_tensor("MODT", [MODK, BATCH * TOK], F32)))
            return keep[0]

        MOD_END = 8

        program = [
            lambda: norm_block(1, first=True),
            lambda: small_attention(0, 0, 32, 8, "rope"),
            lambda: norm_block(2, "quant"),
            lambda: quant_block(1, 4),
            lambda: norm_block(3),
            lambda: big_attention(2, 1, "mask"),
            lambda: norm_block(4, "rms", 5),
            lambda: small_attention(3, None, 16, 16, "causal", MODT=modulation(True)),
            lambda: ffn_block(3, "mod", 1, 5, MODT=modulation(False)),
            lambda: norm_block(5),
            lambda: big_attention(4, 2, "rms"),
            lambda: norm_block(6),
            lambda: ffn_block(5, "plain", 1, 6),
            lambda: norm_block(7),
            lambda: small_attention(6, 3, 16, 16, "dca"),
            lambda: norm_block(None),
            lambda: router_block(7, 7),
            lambda: ffn_block(7, "moe", (2 + EXPERTS) // 2),
        ]
        for n, part in enumerate(program):
            with ExitStack() as area:
                scope[0], scope[1] = area, n + 1
                part()
            if n == MOD_END:
                held.close()
        last_block()


def rows(m):
    k, n = m.shape
    return m.reshape(k // P, P, n).transpose(1, 0, 2).reshape(P, -1)


def padded(m, k):
    z = np.zeros((k,) + m.shape[1:], m.dtype)
    z[:m.shape[0]] = m
    return z


def thrice(m, axis):
    shape = list(m.shape)
    shape[axis] = MODK
    z = np.zeros(shape, m.dtype)
    for at in (0, 32, 64):
        if axis:
            z[:, at:at + RANK] = m
        else:
            z[at:at + RANK] = m
    return z


def everywhere(v):
    return np.broadcast_to(v, (P, v.size))


def units(gate, up, down):
    return [np.concatenate([rows(gate[:, u:u + UH]), rows(up[:, u:u + UH]), rows(down[u:u + UH])], 1)
            for u in range(0, gate.shape[1], UH)]


def lay_out(i):
    c = lambda n: np.asarray(i[n])
    kv = c("L0_xattn_Wkv")
    kvd = c("L3_xattn_Wkv_dca")
    kv3 = [c("L3_xattn_Wk"), c("L3_xattn_Wv")]
    cat = np.concatenate(kv3, 1).reshape(CDIM, 16, 2, 16)
    bcat = np.concatenate([c("L3_xattn_bk"), c("L3_xattn_bv")]).reshape(16, 2, 16)
    l3k, l3v = cat[:, :, 0].reshape(CDIM, DIM), cat[:, :, 1].reshape(CDIM, DIM)
    b3k, b3v = bcat[:, 0].reshape(DIM), bcat[:, 1].reshape(DIM)

    heads = lambda n: everywhere(np.tile(c(f"L3_xattn_{n}"), 16))
    rows_of = lambda a, b: np.concatenate([a[:MAIN], b[MAIN:]], 0)
    segc = np.zeros((P, 4), np.float32)
    segc[:MAIN, 0:2] = 1
    segc[MAIN:, 2:4] = 1
    col = lambda v: v.reshape(-1, P).T
    return [
        [rows(c("L0_xattn_Wq")), kv[:, :DIM], kv[:, DIM:], rows(c("L0_xattn_Wout")), everywhere(c("L0_xattn_bout"))],
        [rows(c("L0_ffn_w1").T), rows(c("L0_ffn_w3").T), rows(padded(c("L0_ffn_w2").T, HID0P))],
        [rows(c("L1_xattn_Wq")), c("L1_xattn_Wk"), c("L1_xattn_Wv")],
        [rows(c("L1_ffn_Wq").T), rows(c("L1_ffn_Wk").T), rows(c("L1_ffn_Wv").T), rows(c("L1_ffn_Wo").T),
         rows(thrice(c("L1_ffn_A"), 1)), rows(thrice(c("L1_ffn_A"), 1)), col(c("L1_ffn_ln1_w")), col(c("L1_ffn_ln2_w")),
         *units(c("L1_ffn_W_in_base").T, c("L1_ffn_W_up_base").T, c("L1_ffn_W_down").T)],
        [rows(c("L2_xattn_Wq")), c("L2_xattn_Wk"), c("L2_xattn_Wv"), col(c("L2_xattn_gq")),
         col(c("L2_xattn_gk"))],
        units(c("L2_ffn_w_gate").T, c("L2_ffn_w_up").T, c("L2_ffn_w_down").T),
        [rows(c("L3_xattn_Wq")), l3k, l3v, kvd[:, :DIM], kvd[:, DIM:], rows(c("L3_xattn_Wo")),
         everywhere(c("L3_xattn_bq")), rows_of(everywhere(b3k), everywhere(c("L3_xattn_bkv_dca")[:DIM])), everywhere(b3v),
         everywhere(c("L3_xattn_bkv_dca")[DIM:]), everywhere(c("L3_xattn_bo")), heads("qn_w"), heads("qn_b"), rows_of(heads("kn_w"), heads("kn_dca_w")),
         rows_of(heads("kn_b"), heads("kn_dca_b")), segc],
        [rows(c("L3_ffn_router_w")), *units(c("L3_ffn_w_gate"), c("L3_ffn_w_up"), c("L3_ffn_w_down"))],
    ]


def kernel(**inputs):
    import concourse.bacc as bacc
    from concourse.bass_utils import run_bass_kernel_spmd

    nc = bacc.Bacc("TRN2", target_bir_lowering=False, num_devices=1)
    mask = np.asarray(inputs["mask_BxS2_bf1"]).view(np.uint8)
    arrays = {
        "x": np.asarray(inputs["x"]).transpose(1, 0, 2),
        "ctxT": np.asarray(inputs["ctx_1024"]).transpose(2, 0, 1),
        "pos": np.asarray(inputs["fside_BxSx2_0"]).transpose(1, 0, 2),
        "mask_row": mask.reshape(1, BATCH * TOK),
        "mask_col": mask.T,
        "gates": everywhere(np.concatenate([np.asarray(inputs["g_xattn"]), np.asarray(inputs["g_ffn"])])),
    }
    for s, parts in enumerate(lay_out(inputs)):
        assert [p.shape[1] for p in parts] == [c for _, c in LAYOUT[s]], s
        arrays[f"weights{s}"] = np.concatenate(parts, 1)
    for n, layer in enumerate((1, 2)):
        arrays[f"wo{n}"] = rows(np.asarray(inputs[f"L{layer}_xattn_Wo"]))
    arrays["modb"] = thrice(np.asarray(inputs["L1_ffn_B"]), 0)
    w1, w2 = np.asarray(inputs["L3_ffn_w1"]), np.asarray(inputs["L3_ffn_w2"])
    arrays["experts"] = np.stack([units(w1[e][:, :INTER], w1[e][:, INTER:], w2[e])[0] for e in range(EXPERTS)], 1)
    arrays = {n: np.ascontiguousarray(a) for n, a in arrays.items()}
    aps = {n: nc.dram_tensor(n, a.shape, mybir.dt.from_np(a.dtype), kind="ExternalInput").ap() for n, a in arrays.items()}
    out = nc.dram_tensor("out", (TOK, BATCH, DIM), F32, kind="ExternalOutput").ap()
    build(nc, aps["x"], aps["ctxT"], aps["pos"], aps["mask_row"], aps["mask_col"], aps["gates"],
          [aps[f"weights{s}"] for s in range(len(LAYOUT))], [aps["wo0"], aps["wo1"]], aps["modb"], aps["experts"], out)
    r = run_bass_kernel_spmd(nc, [arrays], core_ids=[0])
    return np.ascontiguousarray(r.results[0]["out"].transpose(1, 0, 2))
```
